# Optimizing a Trainium2 kernel written in Bass

```python
import numpy as np
import jax
import jax.numpy as jnp

def _softmax(x, axis=-1):
    return jax.nn.softmax(x, axis=axis)

def _gelu(x):
    return jax.nn.gelu(x, approximate=True)

def _silu(x):
    return jax.nn.silu(x)

def _sigmoid(x):
    return jax.nn.sigmoid(x)

def _layernorm(x, axis=-1, eps=1e-05):
    m = jnp.mean(x, axis=axis, keepdims=True)
    v = jnp.var(x, axis=axis, keepdims=True)
    return (x - m) / jnp.sqrt(v + eps)

def _scatter_add(tgt, idx, src, axis=0):
    return tgt.at[idx].add(src)

def _segment_sum(src, seg, n):
    return jax.ops.segment_sum(src, seg, n)
kernel_name = 'mk_gnn_preln_d2_gnn_r64_e9655f'

def setup_inputs(seed: int=0):
    np.random.seed(seed)
    _w = jnp.asarray

    def _rec_inputs():
        import jax
        import jax.numpy as jnp
        _gk = jax.random.key(seed)
        x = -0.0003713 + 1 * jax.random.normal(jax.random.fold_in(_gk, 1), (100000, 256), jnp.float32)
        src = jax.random.randint(jax.random.fold_in(_gk, 2), (25000,), 0, 100000, jnp.int32)
        dst = jax.random.randint(jax.random.fold_in(_gk, 3), (25000,), 0, 100000, jnp.int32)
        _o = jnp.argsort(dst, stable=True)
        src = src[_o]
        dst = dst[_o]
        return (x, src, dst)
    x, src, dst = _rec_inputs()

    def _L0_gnn_setup():
        import jax, jax.numpy as jnp
        import numpy as np
        N, DIM, H, C, E = (50000, 256, 4, 64, 12500)
        NEG_SLOPE = 0.2
        LN_EPS = 1e-05
        key = jax.random.key(seed)
        ks = jax.random.split(key, 8)
        x = jax.random.normal(ks[0], (N, DIM), dtype=jnp.float32)
        edge_index = jax.random.randint(ks[1], (2, E), 0, N, dtype=jnp.int64)
        W = jax.random.normal(ks[2], (DIM, H * C), dtype=jnp.float32) * (1.0 / np.sqrt(DIM))
        a_src = jax.random.normal(ks[3], (H, C), dtype=jnp.float32) * (1.0 / np.sqrt(C))
        a_dst = jax.random.normal(ks[4], (H, C), dtype=jnp.float32) * (1.0 / np.sqrt(C))
        bias_gat = jnp.zeros((DIM,), dtype=jnp.float32)
        W_res = jax.random.normal(ks[5], (DIM, DIM), dtype=jnp.float32) * (1.0 / np.sqrt(DIM))
        b_res = jnp.zeros((DIM,), dtype=jnp.float32)
        gamma = jnp.ones((DIM,), dtype=jnp.float32)
        beta = jnp.zeros((DIM,), dtype=jnp.float32)
        return {'x': x, 'edge_index': edge_index, 'W': W, 'a_src': a_src, 'a_dst': a_dst, 'bias_gat': bias_gat, 'W_res': W_res, 'b_res': b_res, 'gamma': gamma, 'beta': beta}
    _L0_gnn_all = _L0_gnn_setup()
    _L0_gnn_in = {k: v for k, v in _L0_gnn_all.items() if k in ('W', 'a_src', 'a_dst', 'bias_gat', 'W_res', 'b_res', 'gamma', 'beta')}
    del _L0_gnn_all

    def _L1_gnn_setup():
        import jax, jax.numpy as jnp
        import numpy as np
        N_NODES = 50000
        N_EDGES = 25000
        F_IN = 256
        F_OUT = 256

        def _gcn_conv(x, edge_index, W, b, num_nodes):
            src, dst = (edge_index[0], edge_index[1])
            loop = jnp.arange(num_nodes, dtype=src.dtype)
            src = jnp.concatenate([src, loop])
            dst = jnp.concatenate([dst, loop])
            deg = jax.ops.segment_sum(jnp.ones_like(dst, dtype=x.dtype), dst, num_segments=num_nodes)
            dis = jnp.where(deg > 0, jax.lax.rsqrt(jnp.maximum(deg, 1.0)), 0.0)
            norm = dis[src] * dis[dst]
            h = x @ W
            msg = h[src] * norm[:, None]
            out = jax.ops.segment_sum(msg, dst, num_segments=num_nodes)
            return out + b
        key = jax.random.key(seed)
        ks = jax.random.split(key, 6)
        x = jax.random.normal(ks[0], (N_NODES, F_IN), dtype=jnp.float32)
        edge_index = jax.random.randint(ks[1], (2, N_EDGES), 0, N_NODES, dtype=jnp.int64 if jax.config.jax_enable_x64 else jnp.int32)
        s = 1.0 / np.sqrt(F_IN)
        W1 = jax.random.normal(ks[2], (F_IN, F_OUT), dtype=jnp.float32) * s
        b1 = jnp.zeros((F_OUT,), dtype=jnp.float32)
        W2 = jax.random.normal(ks[3], (F_OUT, F_OUT), dtype=jnp.float32) * (1.0 / np.sqrt(F_OUT))
        b2 = jnp.zeros((F_OUT,), dtype=jnp.float32)
        prelu_a = jnp.full((F_OUT,), 0.25, dtype=jnp.float32)
        return {'x': x, 'edge_index': edge_index, 'W1': W1, 'b1': b1, 'W2': W2, 'b2': b2, 'prelu_a': prelu_a}
    _L1_gnn_all = _L1_gnn_setup()
    _L1_gnn_in = {k: v for k, v in _L1_gnn_all.items() if k in ('W1', 'b1', 'W2', 'b2', 'prelu_a')}
    del _L1_gnn_all
    return {'x': x, 'src': src, 'dst': dst, 'L0_gnn_W': _L0_gnn_in['W'], 'L0_gnn_a_src': _L0_gnn_in['a_src'], 'L0_gnn_a_dst': _L0_gnn_in['a_dst'], 'L0_gnn_bias_gat': _L0_gnn_in['bias_gat'], 'L0_gnn_W_res': _L0_gnn_in['W_res'], 'L0_gnn_b_res': _L0_gnn_in['b_res'], 'L0_gnn_gamma': _L0_gnn_in['gamma'], 'L0_gnn_beta': _L0_gnn_in['beta'], 'L1_gnn_W1': _L1_gnn_in['W1'], 'L1_gnn_b1': _L1_gnn_in['b1'], 'L1_gnn_W2': _L1_gnn_in['W2'], 'L1_gnn_b2': _L1_gnn_in['b2'], 'L1_gnn_prelu_a': _L1_gnn_in['prelu_a']}

def reference(x, src, dst, L0_gnn_W, L0_gnn_a_src, L0_gnn_a_dst, L0_gnn_bias_gat, L0_gnn_W_res, L0_gnn_b_res, L0_gnn_gamma, L0_gnn_beta, L1_gnn_W1, L1_gnn_b1, L1_gnn_W2, L1_gnn_b2, L1_gnn_prelu_a):
    import jax
    import jax.numpy as jnp

    def _L0_gnn_ref(x, edge_index, W, a_src, a_dst, bias_gat, W_res, b_res, gamma, beta):
        import jax, jax.numpy as jnp
        import numpy as np
        N, DIM, H, C, E = (50000, 256, 4, 64, 12500)
        NEG_SLOPE = 0.2
        LN_EPS = 1e-05
        n = x.shape[0]
        loops = jnp.arange(n, dtype=edge_index.dtype)
        src = jnp.concatenate([edge_index[0], loops])
        dst = jnp.concatenate([edge_index[1], loops])
        h = (x @ W).reshape(n, H, C)
        al_src = jnp.einsum('nhc,hc->nh', h, a_src)
        al_dst = jnp.einsum('nhc,hc->nh', h, a_dst)
        e = jax.nn.leaky_relu(al_src[src] + al_dst[dst], NEG_SLOPE)
        emax = jax.ops.segment_max(e, dst, num_segments=n)
        ee = jnp.exp(e - emax[dst])
        denom = jax.ops.segment_sum(ee, dst, num_segments=n)
        alpha = ee / (denom[dst] + 1e-16)
        msg = h[src] * alpha[:, :, None]
        out = jax.ops.segment_sum(msg, dst, num_segments=n)
        out = out.reshape(n, H * C) + bias_gat
        y = out + x @ W_res + b_res
        mu = jnp.mean(y, axis=-1, keepdims=True)
        var = jnp.mean((y - mu) ** 2, axis=-1, keepdims=True)
        return gamma * (y - mu) * jax.lax.rsqrt(var + LN_EPS) + beta

    def _L1_gnn_ref(x, edge_index, W1, b1, W2, b2, prelu_a):
        import jax, jax.numpy as jnp
        import numpy as np
        N_NODES = 50000
        N_EDGES = 25000
        F_IN = 256
        F_OUT = 256

        def _gcn_conv(x, edge_index, W, b, num_nodes):
            src, dst = (edge_index[0], edge_index[1])
            loop = jnp.arange(num_nodes, dtype=src.dtype)
            src = jnp.concatenate([src, loop])
            dst = jnp.concatenate([dst, loop])
            deg = jax.ops.segment_sum(jnp.ones_like(dst, dtype=x.dtype), dst, num_segments=num_nodes)
            dis = jnp.where(deg > 0, jax.lax.rsqrt(jnp.maximum(deg, 1.0)), 0.0)
            norm = dis[src] * dis[dst]
            h = x @ W
            msg = h[src] * norm[:, None]
            out = jax.ops.segment_sum(msg, dst, num_segments=num_nodes)
            return out + b
        n = x.shape[0]
        z = _gcn_conv(x, edge_index, W1, b1, n)
        z = _gcn_conv(z, edge_index, W2, b2, n)
        z = jnp.where(z >= 0, z, prelu_a[None, :] * z)
        return z
    edge_index = jnp.stack([src, dst])
    h = jnp.maximum(_layernorm(x, axis=-1), 0.0)
    x = x + _L0_gnn_ref(h, edge_index, L0_gnn_W, L0_gnn_a_src, L0_gnn_a_dst, L0_gnn_bias_gat, L0_gnn_W_res, L0_gnn_b_res, L0_gnn_gamma, L0_gnn_beta)
    h = jnp.maximum(_layernorm(x, axis=-1), 0.0)
    x = x + _L1_gnn_ref(h, edge_index, L1_gnn_W1, L1_gnn_b1, L1_gnn_W2, L1_gnn_b2, L1_gnn_prelu_a)
    return x

_drawn_inputs = setup_inputs


def setup_inputs(seed=0):
    import zlib

    import numpy as np

    out = dict(_drawn_inputs(seed))
    spreads = {'L0_gnn_bias_gat': (0.0, 0.1),
     'L0_gnn_b_res': (0.0, 0.1),
     'L0_gnn_gamma': (1.0, 0.2),
     'L0_gnn_beta': (0.0, 0.1),
     'L1_gnn_b1': (0.0, 0.1),
     'L1_gnn_b2': (0.0, 0.1),
     'L1_gnn_prelu_a': (0.25, 0.6)}
    factors = {'L0_gnn_a_dst': 5.036}
    for name, (base, spread) in spreads.items():
        noise = np.random.default_rng([zlib.crc32(name.encode()), seed]).standard_normal(out[name].shape)
        drawn = base * np.exp(spread * noise) if base else spread * noise
        out[name] = jnp.asarray(drawn.astype(out[name].dtype))
    for name, factor in factors.items():
        out[name] = (out[name] * factor).astype(out[name].dtype)
    return out
```

```python
import math
from contextlib import ExitStack

import concourse.bass as bass
from concourse import mybir


def gat_then_gcn_kernel(
    nc, x, src, dst, w_gat, a_src, a_dst, bias_gat, w_res, b_res, gamma, beta, w1, b1, w2, b2, prelu_a, out
):
    fp32, bf16, i32 = mybir.dt.float32, mybir.dt.bfloat16, mybir.dt.int32
    ALU, ACT, AX = mybir.AluOpType, mybir.ActivationFunctionType, mybir.AxisListType

    P = 128
    N, D = x.shape
    E = src.shape[0]
    H, HC = a_src.shape
    K = D // P
    EPS, TINY, SLOPE = 1e-5, 1e-16, 0.2
    T = 4
    GROUP = T * P
    G = math.ceil(N / GROUP)
    U = 4
    C = U * math.ceil(E / (U * P))
    EP = C * P
    FAR = float(1 << 23)
    LOW = -1e37
    NH = H * (HC + 1)
    assert D == H * HC and G % U == 0 and G >= 3 * U and C >= 3 * U

    rows = nc.dram_tensor("rows", [N + 2 * EP, D], fp32, kind="Internal").ap()
    x1_slots = nc.dram_tensor("x1_slots", [EP, D], fp32, kind="Internal").ap()
    keys = nc.dram_tensor("keys", [EP + 2], fp32, kind="Internal").ap()
    srcs = nc.dram_tensor("srcs", [EP], fp32, kind="Internal").ap()
    place = nc.dram_tensor("place", [N, 2], fp32, kind="Internal").ap()

    top = ExitStack()

    def sb(stack, name, shape, dt=fp32):
        return stack.enter_context(nc.sbuf_tensor(name, shape, dt))

    def pb(stack, name, shape=(P, 512), dt=fp32):
        return stack.enter_context(nc.psum_tensor(name, list(shape), dt))

    in_use = []

    def sem(name):
        in_use.append(nc.alloc_semaphore(name=name))
        return in_use[-1]

    def end_phase():
        nc.clear_and_free_semaphores(list(in_use))
        in_use.clear()
        nc.all_engine_barrier()

    with top:
        ident = sb(top, "ident", [P, P])
        tri = sb(top, "tri", [P, P])
        last_row = sb(top, "last_row", [P, 1])
        low = sb(top, "low", [H, 1])
        neg_half = sb(top, "neg_half", [P, 2 * T])
        eps = sb(top, "eps", [P, T])
        eps_d = sb(top, "eps_d", [P, T])
        gamma_d = sb(top, "gamma_d", [P, D])
        ones3 = sb(top, "ones3", [3, P], bf16)
        w_all = sb(top, "w_all", [P, K, 2 * D])
        w_sum = sb(top, "w_sum", [P, K, D])
        w_12 = sb(top, "w_12", [P, K, D])
        w_att = sb(top, "w_att", [P, K, 3, H])
        gamma_b = sb(top, "gamma_b", [P, D])
        beta_b = sb(top, "beta_b", [P, D])
        am1_b = sb(top, "am1_b", [P, D])
        b1w2_b = sb(top, "b1w2_b", [P, D])
        bias_y = sb(top, "bias_y", [3, D], bf16)
        bias_yc = sb(top, "bias_yc", [3, D], bf16)
        bias_z = sb(top, "bias_z", [3, D], bf16)
        bias_2 = sb(top, "bias_2", [3, D], bf16)
        key_col = sb(top, "key_col", [P, C])
        index = sb(top, "index", [P, C, 4], i32)
        slot_row = sb(top, "slot_row", [P, C])
        dis_own = sb(top, "dis_own", [P, C])
        dis2_own = sb(top, "dis2_own", [P, C])
        dis_src = sb(top, "dis_src", [P, C])
        place_src = sb(top, "place_src", [P, C])

        with ExitStack() as st, nc.Block() as block:
            w1_in = sb(st, "w1_in", [P, K, D])
            w2_in = sb(st, "w2_in", [P, K, D])
            w1_t = sb(st, "w1_t", [P, K, D])
            as_b = sb(st, "as_b", [P, D])
            ad_b = sb(st, "ad_b", [P, D])
            bg_b = sb(st, "bg_b", [P, D])
            br_b = sb(st, "br_b", [P, D])
            a_b = sb(st, "a_b", [P, D])
            b2_b = sb(st, "b2_b", [P, D])
            b1_col = sb(st, "b1_col", [P, K])
            b1_rep = sb(st, "b1_rep", [P, K, P])
            mean_w = sb(st, "mean_w", [P, K + 1])
            prod = sb(st, "prod", [P, D])
            full = sb(st, "full", [P, D])
            part = sb(st, "part", [P, 3, D], bf16)
            rest = sb(st, "rest", [P, D])
            pick = sb(st, "pick", [P, D])
            cz_b = sb(st, "cz_b", [P, D])
            by_b = sb(st, "by_b", [P, D])
            byc_b = sb(st, "byc_b", [P, D])
            EPART = max(q for q in range(1, P + 1) if E % q == 0)
            NPART = max(q for q in range(1, P + 1) if N % q == 0)
            key_i = sb(st, "key_i", [EPART, E // EPART], i32)
            src_i = sb(st, "src_i", [EPART, E // EPART], i32)
            key_f = sb(st, "key_f", [EPART, E // EPART])
            src_f = sb(st, "src_f", [EPART, E // EPART])
            edge_val = sb(st, "edge_val", [1, 2 + EP - E + 1])
            far_zero = sb(st, "far_zero", [1, max(1, EP - E)])
            place_i = sb(st, "place_i", [NPART, N // NPART], i32)
            place_f = sb(st, "place_f", [NPART, N // NPART, 2])
            slot_i = sb(st, "slot_i", [P, C], i32)
            CR = math.ceil(C / P)
            by_chunk = sb(st, "by_chunk", [P, 3, CR, P])
            next_col = sb(st, "next_col", [P, C])
            src_col = sb(st, "src_col", [P, C])
            far = sb(st, "far", [P, C])
            ps_w = pb(st, "ps_w")
            ps_b = pb(st, "ps_b")
            ps_t = pb(st, "ps_t", (P, 512))

            weights_in = sem("weights_in")
            vectors_in = sem("vectors_in")
            edges_in = sem("edges_in")
            edges_f = sem("edges_f")
            edge_consts = sem("edge_consts")
            keys_out = sem("keys_out")
            chunks_in = sem("chunks_in")
            place_ready = sem("place_ready")
            place_out = sem("place_out")
            consts_ready = sem("consts_ready")
            pool_step = sem("pool_step")
            dve_step = sem("dve_step")
            w1t_ready = sem("w1t_ready")
            w1t_copied = sem("w1t_copied")
            w12_ready = sem("w12_ready")
            b1rep_ready = sem("b1rep_ready")
            b1w2_ready = sem("b1w2_ready")
            trans_ready = sem("trans_ready")
            trans_copied = sem("trans_copied")

            def row_of(v):
                return v.partition_broadcast(P)

            @block.sync
            def _(sp):
                sp.dma_start(src_i[:], src.rearrange("(p n) -> p n", p=EPART)).then_inc(edges_in, 16)
                sp.dma_start(key_i[:], dst.rearrange("(p n) -> p n", p=EPART)).then_inc(edges_in, 16)
                for to, of in ((w_all[:, :, 0:D], w_gat), (w_all[:, :, D:2 * D], w_res), (w1_in[:], w1), (w2_in[:], w2)):
                    sp.dma_start(to, of.rearrange("(k p) d -> p k d", p=P)).then_inc(weights_in, 16)
                for to, of in ((as_b, a_src.rearrange("h c -> (h c)")), (ad_b, a_dst.rearrange("h c -> (h c)")),
                               (bg_b, bias_gat), (br_b, b_res), (gamma_b, gamma), (beta_b, beta), (a_b, prelu_a),
                               (b2_b, b2)):
                    sp.dma_start(to[:], row_of(of)).then_inc(vectors_in, 16)
                for k in range(K):
                    sp.dma_start(b1_col[:, k:k + 1], b1[k * P:(k + 1) * P].rearrange("(p o) -> p o", o=1)).then_inc(vectors_in, 16)
                sp.wait_ge(edge_consts, 1)
                sp.wait_ge(edges_f, 2)
                sp.dma_start(keys[0:1].rearrange("(o n) -> o n", o=1), edge_val[:, 0:1]).then_inc(keys_out, 16)
                sp.dma_start(keys[1 + E:EP + 2].rearrange("(o n) -> o n", o=1), edge_val[:, 2:3 + EP - E]).then_inc(keys_out, 16)
                sp.dma_start(keys[1:1 + E].rearrange("(p n) -> p n", p=EPART), key_f[:]).then_inc(keys_out, 16)
                sp.dma_start(srcs[0:E].rearrange("(p n) -> p n", p=EPART), src_f[:]).then_inc(keys_out, 16)
                sp.dma_start(srcs[E:EP].rearrange("(o n) -> o n", o=1), far_zero[:, 0:EP - E]).then_inc(keys_out, 16)
                sp.wait_ge(keys_out, 5 * 16)
                for n, row in enumerate((keys[1:1 + EP], keys[2:2 + EP], srcs)):
                    for r in range(CR):
                        m = min(P, C - r * P)
                        sp.dma_start(by_chunk[0:m, n, r, :],
                                     row[r * P * P:(r * P + m) * P].rearrange("(c p) -> c p", p=P)).then_inc(chunks_in, 16)
                sp.wait_ge(place_ready, 2)
                sp.dma_start(place.rearrange("(p n) o -> p n o", p=NPART), place_f[:]).then_inc(place_out, 16)
                sp.wait_ge(place_out, 16)

            @block.gpsimd
            def _(pool):
                steps = [0]

                def done(ins):
                    steps[0] += 1
                    ins.then_inc(pool_step, 1)
                    pool.wait_ge(pool_step, steps[0])

                nc.gpsimd.memset(edge_val[:], FAR)
                done(nc.gpsimd.memset(far_zero[:], 0.0))
                nc.gpsimd.memset(edge_val[:, 0:1], -1.0).then_inc(edge_consts, 1)
                nc.gpsimd.memset(ident[:], 0.0)
                nc.gpsimd.memset(tri[:], 1.0)
                nc.gpsimd.memset(low[:], LOW)
                nc.gpsimd.memset(neg_half[:], -0.5)
                nc.gpsimd.memset(eps[:], EPS)
                nc.gpsimd.memset(eps_d[:], EPS * D)
                nc.gpsimd.memset(ones3[:], 1.0)
                nc.gpsimd.memset(index[:, :, 3], 0)
                done(nc.gpsimd.memset(last_row[:], 1.0))
                nc.gpsimd.affine_select(out=ident[:], in_=ident[:], compare_op=ALU.not_equal, fill=1.0,
                                        base=0, pattern=[[-1, P]], channel_multiplier=1)
                nc.gpsimd.affine_select(out=tri[:], in_=tri[:], compare_op=ALU.is_ge, fill=0.0,
                                        base=0, pattern=[[1, P]], channel_multiplier=-1)
                nc.gpsimd.affine_select(out=last_row[:], in_=last_row[:], compare_op=ALU.is_ge, fill=0.0,
                                        base=1 - P, pattern=[[1, 1]], channel_multiplier=1).then_inc(consts_ready, 1)
                done(nc.gpsimd.iota(place_i[:], pattern=[[1, N // NPART]], base=0, channel_multiplier=N // NPART))
                nc.gpsimd.tensor_copy(place_f[:, :, 0], place_i[:]).then_inc(place_ready, 1)
                nc.gpsimd.memset(place_f[:, :, 1], 1.0).then_inc(place_ready, 1)
                done(nc.gpsimd.iota(slot_i[:], pattern=[[P, C]], base=N, channel_multiplier=1))
                done(nc.gpsimd.tensor_copy(slot_row[:], slot_i[:]))

            @block.vector
            def _(dve):
                steps = [0]

                def done(ins):
                    steps[0] += 1
                    ins.then_inc(dve_step, 1)
                    dve.wait_ge(dve_step, steps[0])

                dve.wait_ge(edges_in, 32)
                nc.vector.tensor_copy(key_f[:], key_i[:]).then_inc(edges_f, 1)
                nc.vector.tensor_copy(src_f[:], src_i[:]).then_inc(edges_f, 1)
                dve.wait_ge(weights_in, 4 * 16)
                dve.wait_ge(vectors_in, (8 + K) * 16)
                dve.wait_ge(consts_ready, 1)
                for k in range(K):
                    done(nc.vector.tensor_tensor(w_sum[:, k, :], w_all[:, k, 0:D], w_all[:, k, D:2 * D], ALU.add))
                    done(nc.vector.reduce_sum(mean_w[:, k:k + 1], w_sum[:, k, :], axis=AX.X))
                    done(nc.vector.tensor_scalar(mean_w[:, k:k + 1], mean_w[:, k:k + 1], 1.0 / D, None, ALU.mult))
                    done(nc.vector.tensor_scalar(w_sum[:, k, :], w_sum[:, k, :], mean_w[:, k:k + 1], None, ALU.subtract))
                for k in range(K):
                    for n, a in enumerate((as_b, ad_b)):
                        done(nc.vector.tensor_tensor(prod[:], w_all[:, k, 0:D], a[:], ALU.mult))
                        done(nc.vector.reduce_sum(w_att[:, k, n, :], prod[:].rearrange("p (h c) -> p h c", h=H), axis=AX.X))
                    done(nc.vector.tensor_tensor(w_att[:, k, 2, :], w_att[:, k, 0, :], w_att[:, k, 1, :], ALU.add))
                nc.vector.tensor_scalar(gamma_d[:], gamma_b[:], math.sqrt(D), None, ALU.mult)
                nc.vector.tensor_scalar(am1_b[:], a_b[:], -1.0, None, ALU.add)
                for k in range(K):
                    last = nc.vector.tensor_scalar(b1_rep[:, k, :], tri[:], 0.0, b1_col[:, k:k + 1], ALU.mult, ALU.add)
                last.then_inc(b1rep_ready, 1)
                dve.wait_ge(w1t_ready, 1)
                nc.vector.tensor_copy(w1_t[:].rearrange("p k d -> p (k d)"), ps_w[:]).then_inc(w1t_copied, 1)
                dve.wait_ge(w12_ready, 1)
                nc.vector.tensor_copy(w_12[:].rearrange("p k d -> p (k d)"), ps_w[:])
                dve.wait_ge(b1w2_ready, 1)
                done(nc.vector.tensor_copy(b1w2_b[:], ps_b[:, 0:D]))
                done(nc.vector.tensor_tensor(cz_b[:], b1w2_b[:], b2_b[:], ALU.add))
                done(nc.vector.tensor_tensor(by_b[:], bg_b[:], br_b[:], ALU.add))
                done(nc.vector.reduce_sum(mean_w[:, K:K + 1], by_b[:], axis=AX.X))
                done(nc.vector.tensor_scalar(mean_w[:, K:K + 1], mean_w[:, K:K + 1], 1.0 / D, None, ALU.mult))
                done(nc.vector.tensor_scalar(byc_b[:], by_b[:], mean_w[:, K:K + 1], None, ALU.subtract))
                for to, of in ((bias_y, by_b), (bias_yc, byc_b), (bias_z, cz_b), (bias_2, b2_b)):
                    done(nc.vector.tensor_copy(part[:, 0, :], of[:]))
                    done(nc.vector.tensor_tensor(rest[:], of[:], part[:, 0, :], ALU.subtract))
                    done(nc.vector.tensor_copy(part[:, 1, :], rest[:]))
                    done(nc.vector.tensor_tensor(rest[:], rest[:], part[:, 1, :], ALU.subtract))
                    done(nc.vector.tensor_copy(part[:, 2, :], rest[:]))
                    done(nc.vector.tensor_scalar(pick[:], part[:, 0, :], ident[:, 0:1], None, ALU.mult))
                    done(nc.vector.scalar_tensor_tensor(pick[:], part[:, 1, :], ident[:, 1:2], pick[:], ALU.mult, ALU.add))
                    done(nc.vector.scalar_tensor_tensor(to[:], part[0:3, 2, :], ident[0:3, 2:3], pick[0:3, :], ALU.mult, ALU.add))
                n = 0
                for cols in (key_col, next_col, src_col):
                    for r in range(CR):
                        m = min(P, C - r * P)
                        n += 1
                        dve.wait_ge(trans_ready, n)
                        nc.vector.tensor_copy(cols[:, r * P:r * P + m], ps_t[:, 0:m]).then_inc(trans_copied, 1)
                dve.wait_ge(trans_copied, n)
                nc.vector.tensor_copy(index[:, :, 0], src_col[:])
                nc.vector.tensor_scalar(index[:, :, 1], key_col[:], float(N - 1), None, ALU.min)
                done(nc.vector.tensor_tensor(far[:], key_col[:], next_col[:], ALU.is_equal))
                done(nc.vector.scalar_tensor_tensor(index[:, :, 2], far[:], FAR, key_col[:], ALU.mult, ALU.add))

            @block.tensor
            def _(pe):
                pe.wait_ge(weights_in, 4 * 16)
                pe.wait_ge(consts_ready, 1)
                for k in range(K):
                    for i in range(K):
                        last = nc.tensor.transpose(ps_w[:, k * D + i * P:k * D + (i + 1) * P],
                                                   w1_in[:, i, k * P:(k + 1) * P], ident[:])
                last.then_inc(w1t_ready, 1)
                pe.wait_ge(b1rep_ready, 1)
                for k in range(K):
                    last = nc.tensor.matmul(ps_b[:, 0:D], b1_rep[:, k, :], w2_in[:, k, :], start=k == 0, stop=k == K - 1)
                last.then_inc(b1w2_ready, 1)
                pe.wait_ge(w1t_copied, 1)
                for i in range(K):
                    for k in range(K):
                        last = nc.tensor.matmul(ps_w[:, i * D:(i + 1) * D], w1_t[:, k, i * P:(i + 1) * P], w2_in[:, k, :],
                                                start=k == 0, stop=k == K - 1)
                last.then_inc(w12_ready, 1)
                pe.wait_ge(chunks_in, 3 * CR * 16)
                n = 0
                for v in range(3):
                    for r in range(CR):
                        m = min(P, C - r * P)
                        if n:
                            pe.wait_ge(trans_copied, n)
                        n += 1
                        nc.tensor.transpose(ps_t[:, 0:m], by_chunk[0:m, v, r, :], ident[0:m, 0:m]).then_inc(trans_ready, 1)


        end_phase()

        turn = [None]

        def stages(eng, count, lag, body, tail=0):
            for i in range(2 * U):
                body(i, i % U)
            with eng.Fori(2, count // U - tail) as j:
                turn[0] = j
                for b in range(U):
                    body(j * U + b, b)
            for i in range(count - tail * U, count + lag):
                body(i, i % U)

        def b_count(i, b, lag):
            if isinstance(i, int):
                return (i - lag) // U
            return turn[0] + (b - lag) // U

        def half_count(i, b, lag):
            if isinstance(i, int):
                return (i - lag) // 2
            return turn[0] * (U // 2) + (b - lag) // 2

        pool_passed = nc.alloc_semaphore(name="pool_passed")

        def passed(pool):
            pool.sem_inc(pool_passed, 1)

        def slot_rows(table, c, first):
            return table[bass.ds(c * P + first, P), :] if not isinstance(c, int) else \
                table[first + c * P:first + (c + 1) * P, :]

        def col(table, c):
            return table[:, c:c + 1] if isinstance(c, int) else table[:, bass.ds(c, 1)]

        def cols(table, c):
            flat = table[:].rearrange("p c n -> p (c n)")
            return flat[:, 4 * c:4 * c + 4] if isinstance(c, int) else flat[:, bass.ds(c * 4, 4)]

        def runs(i, lag, count):
            return not isinstance(i, int) or 0 <= i - lag < count

        def after(eng, semaphore, value):
            if not isinstance(value, int) or value > 0:
                eng.wait_ge(semaphore, value)

        with ExitStack() as st, nc.Block() as block:
            xg = [sb(st, f"xg{b}", [P, T, D]) for b in range(U)]
            xb = [sb(st, f"xb{b}", [P, T, D]) for b in range(U)]
            x1 = [sb(st, f"x1{b}", [P, T, D]) for b in range(U)]
            n1 = [sb(st, f"n1{b}", [P, T, D]) for b in range(U)]
            n0 = [sb(st, f"n0{b}", [P, T, D]) for b in range(2)]
            h0t = [sb(st, f"h0t{b}", [P, T, K, P]) for b in range(2)]
            h1t = [sb(st, f"h1t{b}", [P, T, K, P]) for b in range(2)]
            yn = [sb(st, f"yn{b}", [P, T, D]) for b in range(2)]
            zg = [sb(st, f"zg{b}", [P, T, D]) for b in range(2)]
            zx = [sb(st, f"zx{b}", [P, T, D]) for b in range(2)]
            zm = [sb(st, f"zm{b}", [P, T, D]) for b in range(2)]
            og = [sb(st, f"og{b}", [P, T, D]) for b in range(2)]
            junk = sb(st, "junk", [P, T, D])
            bs = sb(st, "bs", [P, T, 6])
            mv0 = [sb(st, f"mv0{b}", [P, T, 2]) for b in range(2)]
            mv1 = [sb(st, f"mv1{b}", [P, T, 2]) for b in range(2)]
            ssq = [sb(st, f"ssq{b}", [P, T]) for b in range(2)]
            ve = sb(st, "ve", [P, 3, T])
            held = sb(st, "held", [P, 1])
            r0 = [sb(st, f"r0{b}", [P, T]) for b in range(2)]
            ry = [sb(st, f"ry{b}", [P, T]) for b in range(2)]
            r1 = [sb(st, f"r1{b}", [P, T]) for b in range(2)]
            ps_t0 = [pb(st, f"ps_t0{h}") for h in range(2)]
            ps_y = [pb(st, f"ps_y{h}") for h in range(2)]
            ps_t1 = [pb(st, f"ps_t1{h}") for h in range(2)]
            ps_z = [pb(st, f"ps_z{h}") for h in range(2)]

            x_loaded = [sem(f"x_loaded{b}") for b in range(U)]
            rows_stored = [sem(f"rows_stored{b}") for b in range(U)]
            out_stored = [sem(f"out_stored{b}") for b in range(2)]
            x_stats, x1_stats = sem("x_stats"), sem("x1_stats")
            x_moments, x1_moments = sem("x_moments"), sem("x1_moments")
            dve_t, dve_x1 = sem("dve_t"), sem("dve_x1")
            ve_ready = sem("ve_ready")
            r0_ready, ry_ready, r1_ready = sem("r0_ready"), sem("ry_ready"), sem("r1_ready")
            xb_ready, n0_ready, n1_ready = sem("xb_ready"), sem("n0_ready"), sem("n1_ready")
            t0_ready, t1_ready = sem("t0_ready"), sem("t1_ready")
            h0t_ready, h1t_ready = sem("h0t_ready"), sem("h1t_ready")
            y_ready, z_ready = sem("y_ready"), sem("z_ready")
            ssq_ready, zg_ready = sem("ssq_ready"), sem("zg_ready")
            zm_ready, zx_ready, og_ready = sem("zm_ready"), sem("zx_ready"), sem("og_ready")
            LAG = 7

            def group_rows(table, g):
                if isinstance(g, int):
                    at = min(g * GROUP, N - GROUP)
                    part = table[at:at + GROUP, :]
                else:
                    part = table[bass.ds(g * GROUP, GROUP), :]
                return part.rearrange("(p t) d -> p t d", t=T)

            @block.sync
            def _(sp):
                def step(i, b):
                    if runs(i, 0, G):
                        after(sp, n0_ready, i - U + 1)
                        after(sp, xb_ready, i - U + 1)
                        sp.dma_start(xg[b][:], group_rows(x, i)).then_inc(x_loaded[b], 16)
                    if runs(i, 4, G):
                        g = i - 4
                        if isinstance(g, int) and g == G - 1:
                            sp.wait_ge(rows_stored[(g - 1) % U], 16 * ((g - 1) // U + 1))
                        sp.wait_ge(n1_ready, g + 1)
                        sp.dma_start(group_rows(rows[0:N, :], g), n1[(b - 4) % U][:]).then_inc(rows_stored[(b - 4) % U], 16)
                    if runs(i, 6, G):
                        g = i - 6
                        if isinstance(g, int) and g == G - 1:
                            sp.wait_ge(out_stored[(g - 1) % 2], 16 * ((g - 1) // 2 + 1))
                        sp.wait_ge(og_ready, g + 1)
                        sp.dma_start(group_rows(out, g), og[b % 2][:]).then_inc(out_stored[b % 2], 16)

                stages(sp, G, LAG, step, tail=1)
                for b in range(U):
                    sp.wait_ge(rows_stored[b], 16 * (G // U))
                for b in range(2):
                    sp.wait_ge(out_stored[b], 16 * (G // 2))

            @block.vector
            def _(dve):
                def step(i, b):
                    if runs(i, 1, G):
                        g, c = i - 1, (b - 1) % U
                        dve.wait_ge(r0_ready, g + 1)
                        after(dve, t0_ready, 2 * (g - 1))
                        for t in range(T):
                            last = nc.vector.tensor_scalar(n0[c % 2][:, t, :], xg[c][:, t, :], mv0[c % 2][:, t, 0:1],
                                                           r0[c % 2][:, t:t + 1], ALU.subtract, ALU.mult)
                        last.then_inc(n0_ready, 1)
                    if runs(i, 3, G):
                        g, c = i - 3, (b - 3) % U
                        dve.wait_ge(r1_ready, g + 1)
                        if not isinstance(g, int) or g >= U:
                            dve.wait_ge(rows_stored[c], (b_count(i, b, 3)) * 16)
                        after(dve, t1_ready, 2 * (g - U + 1))
                        for t in range(T):
                            last = nc.vector.tensor_scalar(n1[c][:, t, :], x1[c][:, t, :], mv1[c % 2][:, t, 0:1],
                                                           r1[c % 2][:, t:t + 1], ALU.subtract, ALU.mult)
                        last.then_inc(n1_ready, 1)
                    if runs(i, 0, G):
                        dve.wait_ge(x_loaded[b], (b_count(i, b, 0) + 1) * 16)
                        for t in range(T):
                            nc.vector.bn_stats(bs[:, t, :], xg[b][:, t, :]).then_inc(x_stats, 1)
                        dve.wait_ge(x_stats, (i + 1) * T)
                        nc.vector.memset(held[:], 0.0)
                        for t in range(T):
                            last = nc.vector.bn_aggr(mv0[b % 2][:, t, :], bs[:, t, :])
                        last.then_inc(x_moments, 1)
                    if runs(i, 2, G):
                        g, c = i - 2, (b - 2) % U
                        dve.wait_ge(ry_ready, g + 1)
                        dve.wait_ge(y_ready, 2 * g + 2)
                        for t in range(T):
                            last = nc.vector.scalar_tensor_tensor(
                                yn[c % 2][:, t, :], ps_y[t // 2][:, (t % 2) * D:(t % 2 + 1) * D], ry[c % 2][:, t:t + 1],
                                gamma_d[:], ALU.mult, ALU.mult)
                        last.then_inc(dve_t, 1)
                        dve.wait_ge(dve_t, g + 1)
                        dve.wait_ge(xb_ready, g + 1)
                        after(dve, zx_ready, g - U + 1)
                        nc.vector.tensor_tensor(x1[c][:], yn[c % 2][:], xb[c][:], ALU.add).then_inc(dve_x1, 1)
                        dve.wait_ge(dve_x1, g + 1)
                        for t in range(T):
                            nc.vector.bn_stats(bs[:, t, :], x1[c][:, t, :]).then_inc(x1_stats, 1)
                        dve.wait_ge(x1_stats, (g + 1) * T)
                        nc.vector.memset(held[:], 0.0)
                        for t in range(T):
                            last = nc.vector.bn_aggr(mv1[c % 2][:, t, :], bs[:, t, :])
                        last.then_inc(x1_moments, 1)
                    if runs(i, 4, G):
                        g, c = i - 4, (b - 4) % U
                        dve.wait_ge(zg_ready, 2 * g + 2)
                        after(dve, og_ready, g - 1)
                        nc.vector.scalar_tensor_tensor(zm[c % 2][:], zg[c % 2][:], 0.0,
                                                       am1_b[:].unsqueeze(1).broadcast_to([P, T, D]),
                                                       ALU.min, ALU.mult).then_inc(zm_ready, 1)

                stages(dve, G, LAG, step)

            @block.gpsimd
            def _(pool):
                def inv_sd(to, var, g, b, s, kind, add):
                    nc.gpsimd.tensor_tensor(ve[:, kind, :], var, add[:, 0:T], ALU.add).then_inc(ve_ready, 1)
                    pool.wait_ge(ve_ready, ve_count(g, kind))
                    nc.gpsimd.tensor_tensor(to, ve[:, kind, :], neg_half[:, 0:T], ALU.pow).then_inc(s, 1)

                def ve_count(i, kind):
                    if isinstance(i, int):
                        before = sum(min(max(i - lag, 0), G) for lag in (0, 1, 2))
                        return before + sum(0 <= i - lag < G for lag in order[:order.index(kind) + 1])
                    return i * 3 - 3 + order.index(kind) + 1

                order = (0, 2, 1)

                def step(i, b):
                    if runs(i, 0, G):
                        pool.wait_ge(x_loaded[b], (b_count(i, b, 0) + 1) * 16)
                        after(pool, dve_x1, i - U + 1)
                        nc.gpsimd.tensor_tensor(xb[b][:], xg[b][:], beta_b[:].unsqueeze(1).broadcast_to([P, T, D]),
                                                ALU.add).then_inc(xb_ready, 1)
                    if runs(i, 4, G):
                        g, c = i - 4, (b - 4) % U
                        pool.wait_ge(zg_ready, 2 * g + 2)
                        after(pool, og_ready, g - 1)
                        nc.gpsimd.tensor_tensor(zx[c % 2][:], zg[c % 2][:], x1[c][:], ALU.add).then_inc(zx_ready, 1)
                    if runs(i, 5, G):
                        g, c = i - 5, (b - 5) % U
                        pool.wait_ge(zm_ready, g + 1)
                        if not isinstance(g, int) or g >= 2:
                            pool.wait_ge(out_stored[c % 2], half_count(i, b, 5) * 16)
                        pool.wait_ge(zx_ready, g + 1)
                        nc.gpsimd.tensor_tensor(og[c % 2][:], zx[c % 2][:], zm[c % 2][:], ALU.add).then_inc(og_ready, 1)
                    if runs(i, 0, G):
                        pool.wait_ge(x_moments, i + 1)
                        inv_sd(r0[b % 2][:], mv0[b % 2][:, :, 1], i, b, r0_ready, 0, eps)
                    if runs(i, 2, G):
                        g, c = i - 2, (b - 2) % U
                        pool.wait_ge(x1_moments, g + 1)
                        inv_sd(r1[c % 2][:], mv1[c % 2][:, :, 1], i, b, r1_ready, 2, eps)
                    if runs(i, 1, G):
                        g, c = i - 1, (b - 1) % U
                        pool.wait_ge(ssq_ready, 2 * g + 2)
                        inv_sd(ry[c % 2][:], ssq[c % 2][:], i, b, ry_ready, 1, eps_d)

                stages(pool, G, LAG, step)

            @block.scalar
            def _(act):
                def step(i, b):
                    for lag, ps, ready, to, done, used in ((1, ps_t0, t0_ready, h0t, h0t_ready, y_ready),
                                                           (3, ps_t1, t1_ready, h1t, h1t_ready, z_ready)):
                        if runs(i, lag, G):
                            g, c = i - lag, (b - lag) % U
                            for h in range(2):
                                act.wait_ge(ready, 2 * g + h + 1)
                                after(act, used, 2 * (g - 2) + h + 1)
                                nc.scalar.activation(to[c % 2][:, 2 * h:2 * h + 2, :, :].rearrange("p t k n -> p (t k n)"),
                                                     ps[h][:], ACT.Relu).then_inc(done, 1)
                    if runs(i, 1, G):
                        g, c = i - 1, (b - 1) % U
                        for h in range(2):
                            act.wait_ge(y_ready, 2 * g + h + 1)
                            after(act, ry_ready, g - 1)
                            after(act, ssq_ready, 2 * g)
                            for t in range(2):
                                last = nc.scalar.activation(junk[:, 2 * h + t, :], ps_y[h][:, t * D:(t + 1) * D], ACT.Square,
                                                            accum_out=ssq[c % 2][:, 2 * h + t:2 * h + t + 1])
                            last.then_inc(ssq_ready, 1)
                    if runs(i, 3, G):
                        g, c = i - 3, (b - 3) % U
                        for h in range(2):
                            act.wait_ge(z_ready, 2 * g + h + 1)
                            after(act, zm_ready, g - 1)
                            after(act, zx_ready, g - 1)
                            nc.scalar.activation(zg[c % 2][:, 2 * h:2 * h + 2, :].rearrange("p t d -> p (t d)"),
                                                 ps_z[h][:], ACT.Copy).then_inc(zg_ready, 1)

                stages(act, G, LAG, step)

            @block.tensor
            def _(pe):
                def step(i, b):
                    for lag, of, ready, to, copied, done in ((1, n0, n0_ready, ps_t0, h0t_ready, t0_ready),
                                                             (3, n1, n1_ready, ps_t1, h1t_ready, t1_ready)):
                        if runs(i, lag, G):
                            g, c = i - lag, (b - lag) % U
                            pe.wait_ge(ready, g + 1)
                            for h in range(2):
                                after(pe, copied, 2 * (g - 1) + h + 1)
                                for t in range(2):
                                    for k in range(K):
                                        last = nc.tensor.transpose(
                                            to[h][:, (t * K + k) * P:(t * K + k + 1) * P],
                                            of[c % len(of)][:, 2 * h + t, k * P:(k + 1) * P], ident[:])
                                last.then_inc(done, 1)
                    for lag, of, ready, to, used, w, bias, done in (
                            (1, h0t, h0t_ready, ps_y, dve_t, w_sum, bias_yc, y_ready),
                            (3, h1t, h1t_ready, ps_z, zg_ready, w_12, bias_z, z_ready)):
                        if runs(i, lag, G):
                            g, c = i - lag, (b - lag) % U
                            for h in range(2):
                                pe.wait_ge(ready, 2 * g + h + 1)
                                after(pe, used, g if used is dve_t else 2 * (g - 1) + h + 1)
                                for t in range(2):
                                    o = to[h][:, t * D:(t + 1) * D]
                                    for k in range(K):
                                        nc.tensor.matmul(o, of[c % 2][:, 2 * h + t, k, :], w[:, k, :],
                                                         start=k == 0, stop=False)
                                    last = nc.tensor.matmul(o, ones3[:], bias[:], start=False, stop=True)
                                last.then_inc(done, 1)

                stages(pe, G, LAG, step)


        end_phase()

        with ExitStack() as st, nc.Block() as block:
            kr = [sb(st, f"kr{b}", [P, P + 2]) for b in range(U)]
            stage = [sb(st, f"stage{b}", [P, 4], i32) for b in range(U)]
            xe = [sb(st, f"xe{b}", [P, 2, D]) for b in range(U)]
            xdb = [sb(st, f"xdb{b}", [P, D]) for b in range(U)]
            bse = sb(st, "bse", [P, 2, 6])
            mve = [sb(st, f"mve{b}", [P, 2, 2]) for b in range(2)]
            re = [sb(st, f"re{b}", [P, 2]) for b in range(2)]
            vee = sb(st, "vee", [P, 2])
            ne = [sb(st, f"ne{b}", [P, 2, D]) for b in range(2)]
            het = [sb(st, f"het{b}", [P, 2 * K, P]) for b in range(2)]
            edge = [sb(st, f"edge{b}", [H, P + 1]) for b in range(U)]
            same = [sb(st, f"same{b}", [P, P]) for b in range(U)]
            cont = [sb(st, f"cont{b}", [P, P]) for b in range(U)]
            lg = [sb(st, f"lg{b}", [H, 2 * P]) for b in range(2)]
            lk = sb(st, "lk", [H, 2 * P])
            mx = sb(st, "mx", [H, P])
            fw = sb(st, "fw", [H, P])
            mm = [sb(st, f"mm{b}", [H, P]) for b in range(2)]
            dm = sb(st, "dm", [H, 3, P])
            ex = [sb(st, f"ex{b}", [H, 3, P]) for b in range(2)]
            xw = [sb(st, f"xw{b}", [P, 3 * H]) for b in range(2)]
            msg = [sb(st, f"msg{b}", [P, NH + 1]) for b in range(2)]
            car = sb(st, "car", [P, NH + 1])
            acc = [sb(st, f"acc{b}", [P, NH + 1]) for b in range(2)]
            own = sb(st, "own", [P, D])
            own2 = sb(st, "own2", [P, D])
            den = sb(st, "den", [P, H])
            den2 = sb(st, "den2", [P, H])
            rden = sb(st, "rden", [P, H])
            nrm = sb(st, "nrm", [P, D])
            ye = [sb(st, f"ye{b}", [P, D]) for b in range(2)]
            bsy = sb(st, "bsy", [P, 6])
            mvy = [sb(st, f"mvy{b}", [P, 2]) for b in range(2)]
            vy = sb(st, "vy", [P, 1])
            rye = [sb(st, f"rye{b}", [P, 1]) for b in range(2)]
            te = [sb(st, f"te{b}", [P, D]) for b in range(2)]
            tg = sb(st, "tg", [P, D])
            x1e = [sb(st, f"x1e{b}", [P, D]) for b in range(U)]
            bs1 = sb(st, "bs1", [P, 6])
            mv1e = [sb(st, f"mv1e{b}", [P, 2]) for b in range(2)]
            v1 = sb(st, "v1", [P, 1])
            r1e = [sb(st, f"r1e{b}", [P, 1]) for b in range(2)]
            n1e = [sb(st, f"n1e{b}", [P, D]) for b in range(2)]
            dg = [sb(st, f"dg{b}", [P, 1]) for b in range(2)]
            pidx = [sb(st, f"pidx{b}", [P, 4], i32) for b in range(U)]
            prow = [sb(st, f"prow{b}", [P, 2]) for b in range(U)]
            hold = sb(st, "hold", [P, 1])
            ps_t = pb(st, "ps_te")
            ps_l = pb(st, "ps_le")
            ps_x = pb(st, "ps_xe")
            ps_hs = pb(st, "ps_hs")
            ps_hd = [pb(st, f"ps_hd{b}") for b in range(2)]
            ps_a = pb(st, "ps_ae")
            ps_c = pb(st, "ps_ce")

            kr_loaded = [sem(f"kr_loaded{b}") for b in range(U)]
            src_gathered = [sem(f"src_gathered{b}") for b in range(U)]
            dst_gathered = [sem(f"dst_gathered{b}") for b in range(U)]
            place_sent = [sem(f"place_sent{b}") for b in range(U)]
            x1_sent = [sem(f"x1_sent{b}") for b in range(U)]
            n1_sent = [sem(f"n1_sent{b}") for b in range(2)]
            (staged, xdb_made, e_var, e_r, e_stats, e_moments, e_norm, e_trans, e_relu, e_logits, e_lg, e_edge, e_neq,
             e_same, e_leaky, e_pair, e_fwd, e_max, e_diff, e_diff2, e_exp, e_exp_t, e_xw, e_msg, e_msgw, e_hs, e_hd,
             e_sums, e_car, e_acc, e_own, e_own2, e_den, e_den2, e_rden, e_nrm, e_y, y_stats, y_moments, y_var, y_r,
             y_norm, e_tg, e_x1, e1_stats, e1_moments, e1_var, e1_r, e1_norm, e_deg, e_dis, e_prow, e_dis_own,
             init_done) = [
                sem("e_" + n) for n in (
                    "staged xdb var r stats moments norm trans relu logits lg edge neq same leaky pair fwd max diff "
                    "diff2 exp exp_t xw msg msgw hs hd sums car acc own own2 den den2 rden nrm y ystats ymoments "
                    "yvar yr ynorm tg x1 stats1 moments1 var1 r1 norm1 deg dis prow disown init").split()]
            LAGE = 9

            @block.sync
            def _(sp):
                def step(i, b):
                    if runs(i, 0, C):
                        after(sp, e_same, 2 * (i - U + 1))
                        after(sp, e_neq, i - U + 1)
                        at = keys[i * P:i * P + P + 2] if isinstance(i, int) else keys[bass.ds(i * P, P + 2)]
                        sp.dma_start(kr[b][:], at.partition_broadcast(P)).then_inc(kr_loaded[b], 16)
                    if runs(i, 6, C):
                        c, o = i - 6, (b - 6) % U
                        sp.wait_ge(e_x1, c + 1)
                        sp.dma_start(slot_rows(x1_slots, c, 0), x1e[o][:]).then_inc(x1_sent[o], 16)
                    if runs(i, 8, C):
                        c, o = i - 8, (b - 8) % 2
                        sp.wait_ge(e1_norm, c + 1)
                        sp.dma_start(slot_rows(rows, c, N), n1e[o][:]).then_inc(n1_sent[o], 16)

                stages(sp, C, LAGE, step)
                for b in range(U):
                    sp.wait_ge(x1_sent[b], 16 * (C // U))
                for b in range(2):
                    sp.wait_ge(n1_sent[b], 16 * (C // 2))

            @block.gpsimd
            def _(pool):
                def step(i, b):
                    if runs(i, 5, C):
                        c, o = i - 5, (b - 5) % U
                        pool.wait_ge(y_norm, c + 1)
                        after(pool, e_x1, c)
                        nc.gpsimd.tensor_tensor(tg[:], te[o % 2][:], gamma_b[:], ALU.mult).then_inc(e_tg, 1)
                        pool.wait_ge(e_tg, c + 1)
                        if not isinstance(c, int) or c >= U:
                            pool.wait_ge(x1_sent[o], 16 * b_count(i, b, 5))
                        after(pool, e1_norm, c - U + 1)
                        nc.gpsimd.tensor_tensor(x1e[o][:], tg[:], xdb[o][:], ALU.add).then_inc(e_x1, 1)
                    if runs(i, 0, C):
                        after(pool, e_moments, i - U + 1)
                        passed(pool)
                        nc.gpsimd.tensor_copy(stage[b][:], cols(index, i)).then_inc(staged, 1)
                        after(pool, e_norm, i - U + 1)
                        after(pool, xdb_made, i - U + 1)
                        pool.wait_ge(staged, i + 1)
                        passed(pool)
                        pool.indirect_dma_start(xe[b][:, 0, :], None, x, bass.IndirectOffsetOnAxis(stage[b][:, 0:1], 0)
                                                ).then_inc(src_gathered[b], 16)
                        pool.indirect_dma_start(xe[b][:, 1, :], None, x, bass.IndirectOffsetOnAxis(stage[b][:, 1:2], 0)
                                                ).then_inc(dst_gathered[b], 16)
                    if runs(i, 1, C):
                        c, o = i - 1, (b - 1) % U
                        pool.wait_ge(dst_gathered[o], 16 * (b_count(i, b, 1) + 1))
                        after(pool, e_x1, c - U + 1)
                        nc.gpsimd.tensor_tensor(xdb[o][:], xe[o][:, 1, :], beta_b[:], ALU.add).then_inc(xdb_made, 1)
                    if runs(i, 4, C):
                        c, o = i - 4, (b - 4) % U
                        pool.wait_ge(e_deg, c + 1)
                        if not isinstance(c, int) or c >= U:
                            pool.wait_ge(place_sent[o], 16 * b_count(i, b, 4))
                            passed(pool)
                        nc.gpsimd.tensor_tensor(prow[o][:, 1:2], dg[o % 2][:], neg_half[:, 0:1], ALU.pow).then_inc(e_dis, 1)
                        nc.gpsimd.tensor_copy(prow[o][:, 0:1], col(slot_row, c)).then_inc(e_prow, 1)
                        nc.gpsimd.tensor_copy(pidx[o][:], cols(index, c)).then_inc(e_prow, 1)
                        pool.wait_ge(e_dis, c + 1)
                        passed(pool)
                        nc.gpsimd.tensor_copy(col(dis_own, c), prow[o][:, 1:2]).then_inc(e_dis_own, 1)
                        pool.wait_ge(e_prow, 2 * (c + 1))
                        passed(pool)
                        pool.indirect_dma_start(place, bass.IndirectOffsetOnAxis(pidx[o][:, 2:3], 0), prow[o][:], None,
                                                bounds_check=N - 1, oob_is_err=False).then_inc(place_sent[o], 16)
                    for lag, var, made, vt, vs, to, rs, n in ((1, mve, e_moments, vee, e_var, re, e_r, 2),
                                                              (4, mvy, y_moments, vy, y_var, rye, y_r, 1),
                                                              (6, mv1e, e1_moments, v1, e1_var, r1e, e1_r, 1)):
                        if runs(i, lag, C):
                            c, o = i - lag, (b - lag) % 2
                            pool.wait_ge(made, c + 1)
                            after(pool, rs, c)
                            v = var[o][:, :, 1] if n == 2 else var[o][:, 1:2]
                            nc.gpsimd.tensor_tensor(vt[:], v, eps[:, 0:n], ALU.add).then_inc(vs, 1)
                            pool.wait_ge(vs, c + 1)
                            nc.gpsimd.tensor_tensor(to[o][:], vt[:], neg_half[:, 0:n], ALU.pow).then_inc(rs, 1)

                stages(pool, C, LAGE, step)
                for b in range(U):
                    pool.wait_ge(place_sent[b], 16 * (C // U))

            @block.vector
            def _(dve):
                def by_head(ap):
                    return ap.rearrange("p (h c) -> p h c", h=H)

                def heads(ap, n):
                    return ap.unsqueeze(2).broadcast_to([P, H, n])

                def aggregate(stats, value, to_of):
                    dve.wait_ge(stats, value)
                    nc.vector.memset(hold[:], 0.0)
                    for to, of in to_of:
                        last = nc.vector.bn_aggr(to, of)
                    return last

                nc.vector.memset(acc[1][:], 0.0).then_inc(init_done, 1)
                for b in range(2):
                    nc.vector.memset(msg[b][:, NH:NH + 1], 1.0).then_inc(init_done, 1)
                nc.vector.memset(car[:, NH:NH + 1], 0.0).then_inc(init_done, 1)
                dve.wait_ge(init_done, 4)

                def step(i, b):
                    if runs(i, 2, C):
                        c, o = i - 2, (b - 2) % U
                        dve.wait_ge(e_r, c + 1)
                        after(dve, e_trans, c - 1)
                        for n in range(2):
                            last = nc.vector.tensor_scalar(ne[o % 2][:, n, :], xe[o][:, n, :], mve[o % 2][:, n, 0:1],
                                                           re[o % 2][:, n:n + 1], ALU.subtract, ALU.mult)
                        last.then_inc(e_norm, 1)
                    if runs(i, 3, C):
                        c, o = i - 3, (b - 3) % U
                        q = o % 2
                        dve.wait_ge(e_lg, c + 1)
                        nc.vector.scalar_tensor_tensor(lk[:], lg[q][:], SLOPE, lg[q][:], ALU.mult, ALU.max
                                                       ).then_inc(e_leaky, 1)
                        dve.wait_ge(e_leaky, c + 1)
                        nc.vector.tensor_tensor(mx[:], lk[:, 0:P], lk[:, P:2 * P], ALU.max).then_inc(e_pair, 1)
                        dve.wait_ge(e_pair, c + 1)
                        before = low[:] if isinstance(c, int) and c == 0 else mm[1 - q][:, P - 1:P]
                        nc.vector.tensor_tensor_scan(fw[:], edge[o][:, 0:P], mx[:], before, ALU.add, ALU.max
                                                     ).then_inc(e_fwd, 1)
                        dve.wait_ge(e_fwd, c + 1)
                        nc.vector.tensor_tensor_scan(mm[q][:, ::-1], edge[o][:, P:0:-1], fw[:, ::-1], low[:],
                                                     ALU.add, ALU.max).then_inc(e_max, 1)
                        dve.wait_ge(e_max, c + 1)
                        after(dve, e_exp, c)
                        nc.vector.tensor_tensor(dm[:, 0:2, :], mm[q][:].unsqueeze(1).broadcast_to([H, 2, P]),
                                                lk[:].rearrange("h (n p) -> h n p", n=2), ALU.subtract).then_inc(e_diff, 1)
                        nc.vector.tensor_scalar(dm[:, 2, :], mm[q][:], before, 0.0, ALU.subtract, ALU.max
                                                ).then_inc(e_diff2, 1)
                    if runs(i, 1, C):
                        c, o = i - 1, (b - 1) % U
                        dve.wait_ge(src_gathered[o], 16 * (b_count(i, b, 1) + 1))
                        nc.vector.bn_stats(bse[:, 0, :], xe[o][:, 0, :]).then_inc(e_stats, 1)
                        dve.wait_ge(dst_gathered[o], 16 * (b_count(i, b, 1) + 1))
                        nc.vector.bn_stats(bse[:, 1, :], xe[o][:, 1, :]).then_inc(e_stats, 1)
                        aggregate(e_stats, 2 * (c + 1), [(mve[o % 2][:, n, :], bse[:, n, :]) for n in range(2)]
                                  ).then_inc(e_moments, 1)
                        dve.wait_ge(kr_loaded[o], 16 * (b_count(i, b, 1) + 1))
                        nc.vector.tensor_tensor(edge[o][:], kr[o][0:H, 0:P + 1], kr[o][0:H, 1:P + 2], ALU.not_equal
                                                ).then_inc(e_neq, 1)
                        after(dve, e_sums, c - U + 1)
                        nc.vector.scalar_tensor_tensor(same[o][:], kr[o][:, 1:P + 1], col(key_col, c), tri[:],
                                                       ALU.is_equal, ALU.mult).then_inc(e_same, 1)
                        nc.vector.tensor_scalar(cont[o][:], kr[o][:, 1:P + 1], kr[o][:, 0:1], last_row[:], ALU.is_equal,
                                                ALU.mult).then_inc(e_same, 1)
                        dve.wait_ge(e_neq, c + 1)
                        nc.vector.tensor_scalar(edge[o][:], edge[o][:], LOW, None, ALU.mult).then_inc(e_edge, 1)
                    if runs(i, 7, C):
                        c, o = i - 7, (b - 7) % U
                        dve.wait_ge(e1_r, c + 1)
                        if not isinstance(c, int) or c >= 2:
                            dve.wait_ge(n1_sent[o % 2], 16 * half_count(i, b, 7))
                        nc.vector.tensor_scalar(n1e[o % 2][:], x1e[o][:], mv1e[o % 2][:, 0:1], r1e[o % 2][:], ALU.subtract,
                                                ALU.mult).then_inc(e1_norm, 1)
                    if runs(i, 3, C):
                        c, q = i - 3, (b - 3) % 2
                        dve.wait_ge(e_exp_t, c + 1)
                        after(dve, e_y, c - 1)
                        nc.vector.tensor_copy(xw[q][:], ps_x[:, 0:3 * H]).then_inc(e_xw, 1)
                        dve.wait_ge(e_xw, c + 1)
                        dve.wait_ge(e_hs, c + 1)
                        after(dve, e_sums, c - 1)
                        m = by_head(msg[q][:, 0:NH])
                        nc.vector.tensor_tensor(m[:, :, 0:HC], by_head(ps_hs[:, 0:D]), heads(xw[q][:, 0:H], HC), ALU.mult
                                                ).then_inc(e_msg, 1)
                        nc.vector.tensor_copy(m[:, :, HC], xw[q][:, 0:H]).then_inc(e_msgw, 1)
                    if runs(i, 4, C):
                        c, q = i - 4, (b - 4) % 2
                        dve.wait_ge(e_y, c + 1)
                        nc.vector.bn_stats(bsy[:], ye[q][:]).then_inc(y_stats, 1)
                        aggregate(y_stats, c + 1, [(mvy[q][:], bsy[:])]).then_inc(y_moments, 1)
                    if runs(i, 5, C):
                        c, q = i - 5, (b - 5) % 2
                        dve.wait_ge(y_r, c + 1)
                        after(dve, e_x1, c - 1)
                        nc.vector.tensor_scalar(te[q][:], ye[q][:], mvy[q][:, 0:1], rye[q][:], ALU.subtract, ALU.mult
                                                ).then_inc(y_norm, 1)
                    if runs(i, 6, C):
                        c, o = i - 6, (b - 6) % U
                        dve.wait_ge(e_x1, c + 1)
                        nc.vector.bn_stats(bs1[:], x1e[o][:]).then_inc(e1_stats, 1)
                        aggregate(e1_stats, c + 1, [(mv1e[o % 2][:], bs1[:])]).then_inc(e1_moments, 1)
                    if runs(i, 3, C):
                        c, q = i - 3, (b - 3) % 2
                        dve.wait_ge(e_sums, c + 1)
                        nc.vector.tensor_tensor(by_head(car[:, 0:NH]), by_head(ps_c[:, 0:NH]),
                                                heads(xw[q][:, 2 * H:3 * H], HC + 1), ALU.mult).then_inc(e_car, 1)
                        nc.vector.tensor_tensor(by_head(own[:]), by_head(ps_hd[q][:, 0:D]), heads(xw[q][:, H:2 * H], HC),
                                                ALU.mult).then_inc(e_own, 1)
                        dve.wait_ge(e_car, c + 1)
                        nc.vector.tensor_tensor(acc[q][:], car[:], ps_a[:, 0:NH + 1], ALU.add).then_inc(e_acc, 1)
                        dve.wait_ge(e_acc, c + 1)
                        a = by_head(acc[q][:, 0:NH])
                        after(dve, e_dis, c - 1)
                        nc.vector.tensor_scalar(dg[q][:], acc[q][:, NH:NH + 1], 1.0, 1.0, ALU.add, ALU.max
                                                ).then_inc(e_deg, 1)
                        nc.vector.tensor_tensor(den[:], a[:, :, HC], xw[q][:, H:2 * H], ALU.add).then_inc(e_den, 1)
                        nc.vector.tensor_tensor(by_head(own2[:]), by_head(own[:]), a[:, :, 0:HC], ALU.add).then_inc(e_own2, 1)
                        dve.wait_ge(e_den, c + 1)
                        nc.vector.tensor_scalar(den2[:], den[:], TINY, None, ALU.add).then_inc(e_den2, 1)
                        dve.wait_ge(e_den2, c + 1)
                        nc.vector.reciprocal(rden[:], den2[:]).then_inc(e_rden, 1)
                        dve.wait_ge(e_rden, c + 1)
                        nc.vector.tensor_tensor(by_head(nrm[:]), by_head(own2[:]), heads(rden[:], HC), ALU.mult
                                                ).then_inc(e_nrm, 1)
                        dve.wait_ge(e_nrm, c + 1)
                        nc.vector.tensor_tensor(ye[q][:], nrm[:], ps_hd[q][:, D:2 * D], ALU.add).then_inc(e_y, 1)

                stages(dve, C, LAGE, step)

            @block.scalar
            def _(act):
                def step(i, b):
                    if runs(i, 2, C):
                        c, q = i - 2, (b - 2) % 2
                        act.wait_ge(e_trans, c + 1)
                        after(act, e_hs, c - 1)
                        nc.scalar.activation(het[q][:].rearrange("p k n -> p (k n)"), ps_t[:], ACT.Relu).then_inc(e_relu, 1)
                    if runs(i, 3, C):
                        c, q = i - 3, (b - 3) % 2
                        act.wait_ge(e_diff2, c + 1)
                        act.wait_ge(e_diff, c + 1)
                        after(act, e_exp_t, c - 1)
                        nc.scalar.activation(ex[q][:], dm[:], ACT.Exp, scale=-1.0).then_inc(e_exp, 1)
                    if runs(i, 2, C):
                        c, q = i - 2, (b - 2) % 2
                        act.wait_ge(e_logits, c + 1)
                        after(act, e_leaky, c - 1)
                        nc.scalar.activation(lg[q][:], ps_l[0:H, 0:2 * P], ACT.Copy).then_inc(e_lg, 1)

                stages(act, C, LAGE, step)

            @block.tensor
            def _(pe):
                pe.wait_ge(init_done, 4)

                def step(i, b):
                    if runs(i, 2, C):
                        c, q = i - 2, (b - 2) % 2
                        pe.wait_ge(e_norm, c + 1)
                        after(pe, e_relu, c)
                        for n in range(2):
                            for k in range(K):
                                last = nc.tensor.transpose(ps_t[:, (n * K + k) * P:(n * K + k + 1) * P],
                                                           ne[q][:, n, k * P:(k + 1) * P], ident[:])
                        last.then_inc(e_trans, 1)
                    if runs(i, 3, C):
                        c, q = i - 3, (b - 3) % 2
                        pe.wait_ge(e_exp, c + 1)
                        after(pe, e_xw, c)
                        for n in range(3):
                            last = nc.tensor.matmul(ps_x[:, n * H:(n + 1) * H], ex[q][:, n, :], ident[0:H, 0:H],
                                                    start=True, stop=True)
                        last.then_inc(e_exp_t, 1)
                    if runs(i, 2, C):
                        c, q = i - 2, (b - 2) % 2
                        pe.wait_ge(e_relu, c + 1)
                        after(pe, e_lg, c)
                        for n in range(2):
                            for k in range(K):
                                nc.tensor.matmul(ps_l[0:H, 0:P], w_att[:, k, n, :], het[q][:, n * K + k, :],
                                                 start=n + k == 0, stop=n * K + k == 2 * K - 1)
                        for k in range(K):
                            last = nc.tensor.matmul(ps_l[0:H, P:2 * P], w_att[:, k, 2, :], het[q][:, K + k, :],
                                                    start=k == 0, stop=k == K - 1)
                        last.then_inc(e_logits, 1)
                        after(pe, e_y, c - 1)
                        for k in range(K):
                            nc.tensor.matmul(ps_hd[q][:], het[q][:, K + k, :], w_all[:, k, :], start=k == 0, stop=False)
                        nc.tensor.matmul(ps_hd[q][:, D:2 * D], ones3[:], bias_y[:], start=False, stop=True
                                         ).then_inc(e_hd, 1)
                    if runs(i, 3, C):
                        c, q, o = i - 3, (b - 3) % 2, (b - 3) % U
                        after(pe, e_acc, c)
                        nc.tensor.matmul(ps_c[:, 0:NH], cont[o][:], acc[1 - q][:, 0:NH], start=True, stop=True)
                        pe.wait_ge(e_msg, c + 1)
                        pe.wait_ge(e_msgw, c + 1)
                        nc.tensor.matmul(ps_a[:, 0:NH + 1], same[o][:], msg[q][:], start=True, stop=False)
                        nc.tensor.matmul(ps_a[:, NH:NH + 1], cont[o][:], acc[1 - q][:, NH:NH + 1], start=False, stop=True
                                         ).then_inc(e_sums, 1)
                    if runs(i, 2, C):
                        c, q = i - 2, (b - 2) % 2
                        after(pe, e_msg, c)
                        for k in range(K):
                            last = nc.tensor.matmul(ps_hs[:, 0:D], het[q][:, k, :], w_all[:, k, 0:D],
                                                    start=k == 0, stop=k == K - 1)
                        last.then_inc(e_hs, 1)

                stages(pe, C, LAGE, step)


        end_phase()

        with ExitStack() as st, nc.Block() as block:
            sidx = [sb(st, f"sidx{b}", [P, 4], i32) for b in range(U)]
            got = [sb(st, f"got{b}", [P, 2]) for b in range(U)]
            is_slot = sb(st, "is_slot", [P, C])
            l_staged, l_copied, l_flag, l_index = sem("l_staged"), sem("l_copied"), sem("l_flag"), sem("l_index")
            l_got = [sem(f"l_got{b}") for b in range(U)]

            @block.gpsimd
            def _(pool):
                def step(i, b):
                    if runs(i, 3, C):
                        c, o = i - 3, (b - 3) % U
                        pool.wait_ge(l_got[o], 16 * (b_count(i, b, 3) + 1))
                        passed(pool)
                        nc.gpsimd.tensor_copy(col(place_src, c), got[o][:, 0:1]).then_inc(l_copied, 1)
                        nc.gpsimd.tensor_copy(col(dis_src, c), got[o][:, 1:2]).then_inc(l_copied, 1)
                    if runs(i, 0, C):
                        after(pool, l_copied, 2 * (i - U + 1))
                        passed(pool)
                        nc.gpsimd.tensor_copy(sidx[b][:], cols(index, i)).then_inc(l_staged, 1)
                        pool.wait_ge(l_staged, i + 1)
                        passed(pool)
                        pool.indirect_dma_start(got[b][:], None, place, bass.IndirectOffsetOnAxis(sidx[b][:, 0:1], 0)
                                                ).then_inc(l_got[b], 16)

                stages(pool, C, 3, step)

            @block.vector
            def _(dve):
                dve.wait_ge(l_copied, 2 * C)
                nc.vector.tensor_copy(index[:, :, 0], place_src[:])
                nc.vector.tensor_scalar(is_slot[:], place_src[:], float(N), float(EP), ALU.is_ge, ALU.mult
                                        ).then_inc(l_flag, 1)
                dve.wait_ge(l_flag, 1)
                nc.vector.tensor_tensor(index[:, :, 1], place_src[:], is_slot[:], ALU.add)
                nc.vector.tensor_tensor(dis2_own[:], dis_own[:], dis_own[:], ALU.mult)

        end_phase()

        for hop in (1, 2):
            if hop == 2:
                end_phase()
            with ExitStack() as st, nc.Block() as block:
                kr = [sb(st, f"hkr{hop}{b}", [P, P + 2]) for b in range(U)]
                sidx = [sb(st, f"hidx{hop}{b}", [P, 4], i32) for b in range(U)]
                far_row = [sb(st, f"far_row{hop}{b}", [P, D]) for b in range(U)]
                own_row = [sb(st, f"own_row{hop}{b}", [P, D]) for b in range(U)]
                same = [sb(st, f"hsame{hop}{b}", [P, P]) for b in range(2)]
                cont = [sb(st, f"hcont{hop}{b}", [P, P]) for b in range(2)]
                msg = [sb(st, f"hmsg{hop}{b}", [P, D + 1]) for b in range(2)]
                own = [sb(st, f"hown{hop}{b}", [P, D]) for b in range(2)]
                acc = [sb(st, f"hacc{hop}{b}", [P, D + 1]) for b in range(2)]
                uu = [sb(st, f"uu{hop}{b}", [P, D]) for b in range(U)]
                ps_a = [pb(st, f"hps_a{hop}{b}") for b in range(2)]
                kr_loaded = [sem(f"h{hop}_kr_loaded{b}") for b in range(U)]
                own_loaded = [sem(f"h{hop}_own_loaded{b}") for b in range(U)]
                far_gathered = [sem(f"h{hop}_far_gathered{b}") for b in range(U)]
                sent = [sem(f"h{hop}_sent{b}") for b in range(U)]
                (h_staged, h_sel, h_msg, h_own, h_sums, h_acc, h_u, h_init) = [
                    sem(f"h{hop}_{n}") for n in "staged sel msg own sums acc u init".split()]
                if hop == 2:
                    x1o = [sb(st, f"x1o{b}", [P, D]) for b in range(U)]
                    ut = [sb(st, f"ut{b}", [P, K, P]) for b in range(2)]
                    a1 = [sb(st, f"a1{b}", [P, 2]) for b in range(U)]
                    z = [sb(st, f"z{b}", [P, D]) for b in range(2)]
                    zn = [sb(st, f"zn{b}", [P, D]) for b in range(2)]
                    zx = [sb(st, f"hzx{b}", [P, D]) for b in range(2)]
                    oidx = [sb(st, f"oidx{b}", [P, 4], i32) for b in range(U)]
                    h_oidx = sem("h2_oidx")
                    oe = [sb(st, f"oe{b}", [P, D]) for b in range(U)]
                    ps_t = pb(st, "hps_t")
                    ps_z = pb(st, "hps_z")
                    x1_loaded = [sem(f"h2_x1_loaded{b}") for b in range(U)]
                    (h_a0, h_a1, h_trans, h_ut, h_prod, h_z, h_zn, h_zx, h_o) = [
                        sem(f"h2_{n}") for n in "a0 a1 trans ut prod z zn zx o".split()]
                first_own = N + (hop - 1) * EP
                LAGH = 8

                @block.sync
                def _(sp):
                    def step(i, b):
                        if runs(i, 0, C):
                            after(sp, h_sel, 2 * (i - U + 1))
                            at = keys[i * P:i * P + P + 2] if isinstance(i, int) else keys[bass.ds(i * P, P + 2)]
                            sp.dma_start(kr[b][:], at.partition_broadcast(P)).then_inc(kr_loaded[b], 16)
                            after(sp, h_own, i - U + 1)
                            sp.dma_start(own_row[b][:], slot_rows(rows, i, first_own)).then_inc(own_loaded[b], 16)
                        if hop == 1 and runs(i, 4, C):
                            c, o = i - 4, (b - 4) % U
                            sp.wait_ge(h_u, c + 1)
                            sp.dma_start(slot_rows(rows, c, N + EP), uu[o][:]).then_inc(sent[o], 16)
                        if hop == 2 and runs(i, 2, C):
                            c, o = i - 2, (b - 2) % U
                            after(sp, h_zx, c - U + 1)
                            sp.dma_start(x1o[o][:], slot_rows(x1_slots, c, 0)).then_inc(x1_loaded[o], 16)

                    stages(sp, C, LAGH, step)
                    for b in range(U):
                        sp.wait_ge(sent[b], 16 * (C // U))

                @block.gpsimd
                def _(pool):
                    def step(i, b):
                        if runs(i, 0, C):
                            after(pool, h_msg, i - U + 1)
                            passed(pool)
                            nc.gpsimd.tensor_copy(sidx[b][:], cols(index, i)).then_inc(h_staged, 1)
                            pool.wait_ge(h_staged, i + 1)
                            passed(pool)
                            pool.indirect_dma_start(far_row[b][:], None, rows[0:N + hop * EP, :],
                                                    bass.IndirectOffsetOnAxis(sidx[b][:, hop - 1:hop], 0)
                                                    ).then_inc(far_gathered[b], 16)
                        if hop == 2 and runs(i, 5, C):
                            c, o = i - 5, (b - 5) % U
                            pool.wait_ge(h_z, c + 1)
                            pool.wait_ge(x1_loaded[o], 16 * (b_count(i, b, 5) + 1))
                            after(pool, h_o, c - 1)
                            nc.gpsimd.tensor_tensor(zx[o % 2][:], z[o % 2][:], x1o[o][:], ALU.add).then_inc(h_zx, 1)
                            pool.wait_ge(h_zn, c + 1)
                            if not isinstance(c, int) or c >= U:
                                pool.wait_ge(sent[o], 16 * b_count(i, b, 5))
                            pool.wait_ge(h_zx, c + 1)
                            nc.gpsimd.tensor_tensor(oe[o][:], zx[o % 2][:], zn[o % 2][:], ALU.add).then_inc(h_o, 1)
                            nc.gpsimd.tensor_copy(oidx[o][:], cols(index, c)).then_inc(h_oidx, 1)
                            pool.wait_ge(h_o, c + 1)
                            pool.wait_ge(h_oidx, c + 1)
                            passed(pool)
                            pool.indirect_dma_start(out, bass.IndirectOffsetOnAxis(oidx[o][:, 2:3], 0), oe[o][:], None,
                                                    bounds_check=N - 1, oob_is_err=False).then_inc(sent[o], 16)

                    stages(pool, C, LAGH, step)

                @block.vector
                def _(dve):
                    nc.vector.memset(acc[1][:], 0.0).then_inc(h_init, 1)

                    def step(i, b):
                        if runs(i, 1, C):
                            c, o = i - 1, (b - 1) % U
                            q = o % 2
                            dve.wait_ge(kr_loaded[o], 16 * (b_count(i, b, 1) + 1))
                            after(dve, h_sums, c - 1)
                            nc.vector.scalar_tensor_tensor(same[q][:], kr[o][:, 1:P + 1], col(key_col, c), tri[:],
                                                           ALU.is_equal, ALU.mult).then_inc(h_sel, 1)
                            nc.vector.tensor_scalar(cont[q][:], kr[o][:, 1:P + 1], kr[o][:, 0:1], last_row[:],
                                                    ALU.is_equal, ALU.mult).then_inc(h_sel, 1)
                            dve.wait_ge(far_gathered[o], 16 * (b_count(i, b, 1) + 1))
                            nc.vector.tensor_scalar(msg[q][:, 0:D], far_row[o][:], 0.0, col(dis_src, c), ALU.max, ALU.mult)
                            nc.vector.tensor_copy(msg[q][:, D:D + 1], col(dis_src, c)).then_inc(h_msg, 1)
                            dve.wait_ge(own_loaded[o], 16 * (b_count(i, b, 1) + 1))
                            after(dve, h_u, c - 1)
                            nc.vector.tensor_scalar(own[q][:], own_row[o][:], 0.0, col(dis2_own, c), ALU.max, ALU.mult
                                                    ).then_inc(h_own, 1)
                        if runs(i, 2, C):
                            c, o = i - 2, (b - 2) % U
                            q = o % 2
                            dve.wait_ge(h_acc, c + 1)
                            dve.wait_ge(h_own, c + 1)
                            if hop == 1:
                                if not isinstance(c, int) or c >= U:
                                    dve.wait_ge(sent[o], 16 * b_count(i, b, 2))
                            else:
                                after(dve, h_trans, c - U + 1)
                            nc.vector.scalar_tensor_tensor(uu[o][:], acc[q][:, 0:D], col(dis_own, c), own[q][:],
                                                           ALU.mult, ALU.add).then_inc(h_u, 1)
                            if hop == 2:
                                after(dve, h_z, c - U + 1)
                                nc.vector.tensor_tensor(a1[o][:, 0:1], acc[q][:, D:D + 1], col(dis_own, c), ALU.add
                                                        ).then_inc(h_a0, 1)
                                dve.wait_ge(h_a0, c + 1)
                                nc.vector.tensor_tensor(a1[o][:, 1:2], a1[o][:, 0:1], col(dis_own, c), ALU.mult
                                                        ).then_inc(h_a1, 1)
                        if hop == 2 and runs(i, 4, C):
                            c, q, o = i - 4, (b - 4) % 2, (b - 4) % U
                            dve.wait_ge(h_prod, c + 1)
                            dve.wait_ge(h_a1, c + 1)
                            after(dve, h_zx, c - 1)
                            nc.vector.scalar_tensor_tensor(z[q][:], b1w2_b[:], a1[o][:, 1:2], ps_z[:, 0:D], ALU.mult,
                                                           ALU.add).then_inc(h_z, 1)
                            dve.wait_ge(h_z, c + 1)
                            after(dve, h_o, c - 1)
                            nc.vector.scalar_tensor_tensor(zn[q][:], z[q][:], 0.0, am1_b[:], ALU.min, ALU.mult
                                                           ).then_inc(h_zn, 1)

                    stages(dve, C, LAGH, step)

                @block.scalar
                def _(act):
                    def step(i, b):
                        if runs(i, 1, C):
                            c, q = i - 1, (b - 1) % 2
                            act.wait_ge(h_sums, c + 1)
                            after(act, h_u, c - 1)
                            if hop == 2:
                                after(act, h_a1, c - 1)
                            nc.scalar.activation(acc[q][:], ps_a[q][:, 0:D + 1], ACT.Copy).then_inc(h_acc, 1)
                        if hop == 2 and runs(i, 3, C):
                            c, q = i - 3, (b - 3) % 2
                            act.wait_ge(h_trans, c + 1)
                            after(act, h_prod, c - 1)
                            nc.scalar.activation(ut[q][:].rearrange("p k n -> p (k n)"), ps_t[:, 0:D], ACT.Copy
                                                 ).then_inc(h_ut, 1)

                    stages(act, C, LAGH, step)

                @block.tensor
                def _(pe):
                    pe.wait_ge(h_init, 1)

                    def step(i, b):
                        if runs(i, 1, C):
                            c, q = i - 1, (b - 1) % 2
                            pe.wait_ge(h_msg, c + 1)
                            after(pe, h_acc, c - 1)
                            nc.tensor.matmul(ps_a[q][:, 0:D + 1], same[q][:], msg[q][:], start=True, stop=False)
                            after(pe, h_acc, c)
                            nc.tensor.matmul(ps_a[q][:, 0:D + 1], cont[q][:], acc[1 - q][:], start=False, stop=True
                                             ).then_inc(h_sums, 1)
                        if hop == 2 and runs(i, 3, C):
                            c, o = i - 3, (b - 3) % U
                            pe.wait_ge(h_u, c + 1)
                            after(pe, h_ut, c)
                            for k in range(K):
                                last = nc.tensor.transpose(ps_t[:, k * P:(k + 1) * P], uu[o][:, k * P:(k + 1) * P],
                                                           ident[:])
                            last.then_inc(h_trans, 1)
                            pe.wait_ge(h_ut, c + 1)
                            after(pe, h_z, c)
                            for k in range(K):
                                nc.tensor.matmul(ps_z[:, 0:D], ut[o % 2][:, k, :], w_12[:, k, :], start=k == 0, stop=False)
                            nc.tensor.matmul(ps_z[:, 0:D], ones3[:], bias_2[:], start=False, stop=True
                                             ).then_inc(h_prod, 1)

                    stages(pe, C, LAGH, step)


_INS = ["x", "src", "dst", "L0_gnn_W", "L0_gnn_a_src", "L0_gnn_a_dst", "L0_gnn_bias_gat", "L0_gnn_W_res", "L0_gnn_b_res",
        "L0_gnn_gamma", "L0_gnn_beta", "L1_gnn_W1", "L1_gnn_b1", "L1_gnn_W2", "L1_gnn_b2", "L1_gnn_prelu_a"]


def kernel(**inputs):
    import numpy as np
    import concourse.bacc as bacc
    from concourse import mybir as _mybir
    from concourse.bass_utils import run_bass_kernel_spmd

    nc = bacc.Bacc("TRN2", target_bir_lowering=False, num_devices=1)
    arrays, args = {}, []
    for name in _INS:
        a = np.ascontiguousarray(inputs[name])
        arrays[f"in_{name}"] = a
        args.append(nc.dram_tensor(f"in_{name}", a.shape, _mybir.dt.from_np(a.dtype), kind="ExternalInput").ap())
    args.append(nc.dram_tensor("out_x", inputs["x"].shape, _mybir.dt.float32, kind="ExternalOutput").ap())
    gat_then_gcn_kernel(nc, *args)
    r = run_bass_kernel_spmd(nc, [arrays], core_ids=[0])
    return r.results[0]["out_x"]
```

```python
import math
from contextlib import ExitStack

import concourse.bass as bass
from concourse import mybir


def gat_then_gcn_kernel(
    nc, x, src, dst, w_gat, a_src, a_dst, bias_gat, w_res, b_res, gamma, beta, w1, b1, w2, b2, prelu_a, out
):
    fp32, bf16, i32 = mybir.dt.float32, mybir.dt.bfloat16, mybir.dt.int32
    ALU, ACT, AX = mybir.AluOpType, mybir.ActivationFunctionType, mybir.AxisListType

    P = 128
    N, D = x.shape
    E = src.shape[0]
    H, HC = a_src.shape
    K = D // P
    EPS, TINY, SLOPE = 1e-5, 1e-16, 0.2
    T = 4
    GROUP = T * P
    G = math.ceil(N / GROUP)
    U = 4
    C = U * math.ceil(E / (U * P))
    EP = C * P
    FAR = float(1 << 23)
    LOW = -1e37
    NH = H * (HC + 1)
    assert D == H * HC and G % U == 0 and G >= 3 * U and C > 3 * U

    rows = nc.dram_tensor("rows", [N + 2 * EP, D], fp32, kind="Internal").ap()
    x1_slots = nc.dram_tensor("x1_slots", [EP, D], fp32, kind="Internal").ap()
    keys = nc.dram_tensor("keys", [EP + 2], fp32, kind="Internal").ap()
    srcs = nc.dram_tensor("srcs", [EP], fp32, kind="Internal").ap()
    place = nc.dram_tensor("place", [N, 2], fp32, kind="Internal").ap()

    top = ExitStack()

    def sb(stack, name, shape, dt=fp32):
        return stack.enter_context(nc.sbuf_tensor(name, shape, dt))

    def pb(stack, name, shape=(P, 512), dt=fp32):
        return stack.enter_context(nc.psum_tensor(name, list(shape), dt))

    in_use = []

    def sem(name):
        in_use.append(nc.alloc_semaphore(name=name))
        return in_use[-1]

    def end_phase():
        nc.clear_and_free_semaphores(list(in_use))
        in_use.clear()
        nc.all_engine_barrier()

    with top:
        ident = sb(top, "ident", [P, P])
        tri = sb(top, "tri", [P, P])
        last_row = sb(top, "last_row", [P, 1])
        low = sb(top, "low", [H, 1])
        neg_half = sb(top, "neg_half", [P, 2 * T])
        eps = sb(top, "eps", [P, T])
        eps_d = sb(top, "eps_d", [P, T])
        gamma_d = sb(top, "gamma_d", [P, D])
        ones3 = sb(top, "ones3", [3, P], bf16)
        w_all = sb(top, "w_all", [P, K, 2 * D])
        w_sum = sb(top, "w_sum", [P, K, D])
        w_12 = sb(top, "w_12", [P, K, D])
        w_src = sb(top, "w_src", [P, K, D + 2 * H])
        w_att = sb(top, "w_att", [P, K, 2, H])
        gamma_b = sb(top, "gamma_b", [P, D])
        beta_b = sb(top, "beta_b", [P, D])
        am1_b = sb(top, "am1_b", [P, D])
        b1w2_b = sb(top, "b1w2_b", [P, D])
        bias_y = sb(top, "bias_y", [3, D], bf16)
        bias_yc = sb(top, "bias_yc", [3, D], bf16)
        bias_z = sb(top, "bias_z", [3, D], bf16)
        bias_2 = sb(top, "bias_2", [3, D], bf16)
        key_col = sb(top, "key_col", [P, C])
        index = sb(top, "index", [P, C, 4], i32)
        slot_row = sb(top, "slot_row", [P, C])
        dis_own = sb(top, "dis_own", [P, C])
        dis2_own = sb(top, "dis2_own", [P, C])
        dis_src = sb(top, "dis_src", [P, C])
        place_src = sb(top, "place_src", [P, C])

        with ExitStack() as st, nc.Block() as block:
            w1_in = sb(st, "w1_in", [P, K, D])
            w2_in = sb(st, "w2_in", [P, K, D])
            w1_t = sb(st, "w1_t", [P, K, D])
            as_b = sb(st, "as_b", [P, D])
            ad_b = sb(st, "ad_b", [P, D])
            bg_b = sb(st, "bg_b", [P, D])
            br_b = sb(st, "br_b", [P, D])
            a_b = sb(st, "a_b", [P, D])
            b2_b = sb(st, "b2_b", [P, D])
            b1_col = sb(st, "b1_col", [P, K])
            b1_rep = sb(st, "b1_rep", [P, K, P])
            mean_w = sb(st, "mean_w", [P, K + 1])
            prod = sb(st, "prod", [P, D])
            full = sb(st, "full", [P, D])
            part = sb(st, "part", [P, 3, D], bf16)
            rest = sb(st, "rest", [P, D])
            pick = sb(st, "pick", [P, D])
            cz_b = sb(st, "cz_b", [P, D])
            by_b = sb(st, "by_b", [P, D])
            byc_b = sb(st, "byc_b", [P, D])
            EPART = max(q for q in range(1, P + 1) if E % q == 0)
            NPART = max(q for q in range(1, P + 1) if N % q == 0)
            key_i = sb(st, "key_i", [EPART, E // EPART], i32)
            src_i = sb(st, "src_i", [EPART, E // EPART], i32)
            key_f = sb(st, "key_f", [EPART, E // EPART])
            src_f = sb(st, "src_f", [EPART, E // EPART])
            edge_val = sb(st, "edge_val", [1, 2 + EP - E + 1])
            far_zero = sb(st, "far_zero", [1, max(1, EP - E)])
            place_i = sb(st, "place_i", [NPART, N // NPART], i32)
            place_f = sb(st, "place_f", [NPART, N // NPART, 2])
            slot_i = sb(st, "slot_i", [P, C], i32)
            CR = math.ceil(C / P)
            by_chunk = sb(st, "by_chunk", [P, 3, CR, P])
            next_col = sb(st, "next_col", [P, C])
            src_col = sb(st, "src_col", [P, C])
            far = sb(st, "far", [P, C])
            ps_w = pb(st, "ps_w")
            ps_b = pb(st, "ps_b")
            ps_t = pb(st, "ps_t", (P, 512))

            weights_in = sem("weights_in")
            vectors_in = sem("vectors_in")
            edges_in = sem("edges_in")
            edges_f = sem("edges_f")
            edge_consts = sem("edge_consts")
            keys_out = sem("keys_out")
            chunks_in = sem("chunks_in")
            place_ready = sem("place_ready")
            place_out = sem("place_out")
            consts_ready = sem("consts_ready")
            pool_step = sem("pool_step")
            dve_step = sem("dve_step")
            w1t_ready = sem("w1t_ready")
            w1t_copied = sem("w1t_copied")
            w12_ready = sem("w12_ready")
            b1rep_ready = sem("b1rep_ready")
            b1w2_ready = sem("b1w2_ready")
            trans_ready = sem("trans_ready")
            trans_copied = sem("trans_copied")

            def row_of(v):
                return v.partition_broadcast(P)

            @block.sync
            def _(sp):
                sp.dma_start(src_i[:], src.rearrange("(p n) -> p n", p=EPART)).then_inc(edges_in, 16)
                sp.dma_start(key_i[:], dst.rearrange("(p n) -> p n", p=EPART)).then_inc(edges_in, 16)
                for to, of in ((w_all[:, :, 0:D], w_gat), (w_all[:, :, D:2 * D], w_res), (w1_in[:], w1), (w2_in[:], w2)):
                    sp.dma_start(to, of.rearrange("(k p) d -> p k d", p=P)).then_inc(weights_in, 16)
                for to, of in ((as_b, a_src.rearrange("h c -> (h c)")), (ad_b, a_dst.rearrange("h c -> (h c)")),
                               (bg_b, bias_gat), (br_b, b_res), (gamma_b, gamma), (beta_b, beta), (a_b, prelu_a),
                               (b2_b, b2)):
                    sp.dma_start(to[:], row_of(of)).then_inc(vectors_in, 16)
                for k in range(K):
                    sp.dma_start(b1_col[:, k:k + 1], b1[k * P:(k + 1) * P].rearrange("(p o) -> p o", o=1)).then_inc(vectors_in, 16)
                sp.wait_ge(edge_consts, 1)
                sp.wait_ge(edges_f, 2)
                sp.dma_start(keys[0:1].rearrange("(o n) -> o n", o=1), edge_val[:, 0:1]).then_inc(keys_out, 16)
                sp.dma_start(keys[1 + E:EP + 2].rearrange("(o n) -> o n", o=1), edge_val[:, 2:3 + EP - E]).then_inc(keys_out, 16)
                sp.dma_start(keys[1:1 + E].rearrange("(p n) -> p n", p=EPART), key_f[:]).then_inc(keys_out, 16)
                sp.dma_start(srcs[0:E].rearrange("(p n) -> p n", p=EPART), src_f[:]).then_inc(keys_out, 16)
                sp.dma_start(srcs[E:EP].rearrange("(o n) -> o n", o=1), far_zero[:, 0:EP - E]).then_inc(keys_out, 16)
                sp.wait_ge(keys_out, 5 * 16)
                for n, row in enumerate((keys[1:1 + EP], keys[2:2 + EP], srcs)):
                    for r in range(CR):
                        m = min(P, C - r * P)
                        sp.dma_start(by_chunk[0:m, n, r, :],
                                     row[r * P * P:(r * P + m) * P].rearrange("(c p) -> c p", p=P)).then_inc(chunks_in, 16)
                sp.wait_ge(place_ready, 2)
                sp.dma_start(place.rearrange("(p n) o -> p n o", p=NPART), place_f[:]).then_inc(place_out, 16)
                sp.wait_ge(place_out, 16)

            @block.gpsimd
            def _(pool):
                steps = [0]

                def done(ins):
                    steps[0] += 1
                    ins.then_inc(pool_step, 1)
                    pool.wait_ge(pool_step, steps[0])

                nc.gpsimd.memset(edge_val[:], FAR)
                done(nc.gpsimd.memset(far_zero[:], 0.0))
                nc.gpsimd.memset(edge_val[:, 0:1], -1.0).then_inc(edge_consts, 1)
                nc.gpsimd.memset(ident[:], 0.0)
                nc.gpsimd.memset(tri[:], 1.0)
                nc.gpsimd.memset(low[:], LOW)
                nc.gpsimd.memset(neg_half[:], -0.5)
                nc.gpsimd.memset(eps[:], EPS)
                nc.gpsimd.memset(eps_d[:], EPS * D)
                nc.gpsimd.memset(ones3[:], 1.0)
                nc.gpsimd.memset(index[:, :, 3], 0)
                done(nc.gpsimd.memset(last_row[:], 1.0))
                nc.gpsimd.affine_select(out=ident[:], in_=ident[:], compare_op=ALU.not_equal, fill=1.0,
                                        base=0, pattern=[[-1, P]], channel_multiplier=1)
                nc.gpsimd.affine_select(out=tri[:], in_=tri[:], compare_op=ALU.is_ge, fill=0.0,
                                        base=0, pattern=[[1, P]], channel_multiplier=-1)
                nc.gpsimd.affine_select(out=last_row[:], in_=last_row[:], compare_op=ALU.is_ge, fill=0.0,
                                        base=1 - P, pattern=[[1, 1]], channel_multiplier=1).then_inc(consts_ready, 1)
                done(nc.gpsimd.iota(place_i[:], pattern=[[1, N // NPART]], base=0, channel_multiplier=N // NPART))
                nc.gpsimd.tensor_copy(place_f[:, :, 0], place_i[:]).then_inc(place_ready, 1)
                nc.gpsimd.memset(place_f[:, :, 1], 1.0).then_inc(place_ready, 1)
                done(nc.gpsimd.iota(slot_i[:], pattern=[[P, C]], base=N, channel_multiplier=1))
                done(nc.gpsimd.tensor_copy(slot_row[:], slot_i[:]))

            @block.vector
            def _(dve):
                steps = [0]

                def done(ins):
                    steps[0] += 1
                    ins.then_inc(dve_step, 1)
                    dve.wait_ge(dve_step, steps[0])

                dve.wait_ge(edges_in, 32)
                nc.vector.tensor_copy(key_f[:], key_i[:]).then_inc(edges_f, 1)
                nc.vector.tensor_copy(src_f[:], src_i[:]).then_inc(edges_f, 1)
                dve.wait_ge(weights_in, 4 * 16)
                dve.wait_ge(vectors_in, (8 + K) * 16)
                dve.wait_ge(consts_ready, 1)
                for k in range(K):
                    done(nc.vector.tensor_tensor(w_sum[:, k, :], w_all[:, k, 0:D], w_all[:, k, D:2 * D], ALU.add))
                    done(nc.vector.reduce_sum(mean_w[:, k:k + 1], w_sum[:, k, :], axis=AX.X))
                    done(nc.vector.tensor_scalar(mean_w[:, k:k + 1], mean_w[:, k:k + 1], 1.0 / D, None, ALU.mult))
                    done(nc.vector.tensor_scalar(w_sum[:, k, :], w_sum[:, k, :], mean_w[:, k:k + 1], None, ALU.subtract))
                for k in range(K):
                    nc.vector.tensor_copy(w_src[:, k, 0:D], w_all[:, k, 0:D])
                    nc.vector.memset(w_src[:, k, D + H:], 0.0)
                    for a, to in ((as_b, w_src[:, k, D:D + H]), (ad_b, w_att[:, k, 0, :])):
                        done(nc.vector.tensor_tensor(prod[:], w_all[:, k, 0:D], a[:], ALU.mult))
                        done(nc.vector.reduce_sum(to, prod[:].rearrange("p (h c) -> p h c", h=H), axis=AX.X))
                    done(nc.vector.tensor_tensor(w_att[:, k, 1, :], w_src[:, k, D:D + H], w_att[:, k, 0, :], ALU.add))
                nc.vector.tensor_scalar(gamma_d[:], gamma_b[:], math.sqrt(D), None, ALU.mult)
                nc.vector.tensor_scalar(am1_b[:], a_b[:], -1.0, None, ALU.add)
                for k in range(K):
                    last = nc.vector.tensor_scalar(b1_rep[:, k, :], tri[:], 0.0, b1_col[:, k:k + 1], ALU.mult, ALU.add)
                last.then_inc(b1rep_ready, 1)
                dve.wait_ge(w1t_ready, 1)
                nc.vector.tensor_copy(w1_t[:].rearrange("p k d -> p (k d)"), ps_w[:]).then_inc(w1t_copied, 1)
                dve.wait_ge(w12_ready, 1)
                nc.vector.tensor_copy(w_12[:].rearrange("p k d -> p (k d)"), ps_w[:])
                dve.wait_ge(b1w2_ready, 1)
                done(nc.vector.tensor_copy(b1w2_b[:], ps_b[:, 0:D]))
                done(nc.vector.tensor_tensor(cz_b[:], b1w2_b[:], b2_b[:], ALU.add))
                done(nc.vector.tensor_tensor(by_b[:], bg_b[:], br_b[:], ALU.add))
                done(nc.vector.reduce_sum(mean_w[:, K:K + 1], by_b[:], axis=AX.X))
                done(nc.vector.tensor_scalar(mean_w[:, K:K + 1], mean_w[:, K:K + 1], 1.0 / D, None, ALU.mult))
                done(nc.vector.tensor_scalar(byc_b[:], by_b[:], mean_w[:, K:K + 1], None, ALU.subtract))
                for to, of in ((bias_y, by_b), (bias_yc, byc_b), (bias_z, cz_b), (bias_2, b2_b)):
                    done(nc.vector.tensor_copy(part[:, 0, :], of[:]))
                    done(nc.vector.tensor_tensor(rest[:], of[:], part[:, 0, :], ALU.subtract))
                    done(nc.vector.tensor_copy(part[:, 1, :], rest[:]))
                    done(nc.vector.tensor_tensor(rest[:], rest[:], part[:, 1, :], ALU.subtract))
                    done(nc.vector.tensor_copy(part[:, 2, :], rest[:]))
                    done(nc.vector.tensor_scalar(pick[:], part[:, 0, :], ident[:, 0:1], None, ALU.mult))
                    done(nc.vector.scalar_tensor_tensor(pick[:], part[:, 1, :], ident[:, 1:2], pick[:], ALU.mult, ALU.add))
                    done(nc.vector.scalar_tensor_tensor(to[:], part[0:3, 2, :], ident[0:3, 2:3], pick[0:3, :], ALU.mult, ALU.add))
                n = 0
                for cols in (key_col, next_col, src_col):
                    for r in range(CR):
                        m = min(P, C - r * P)
                        n += 1
                        dve.wait_ge(trans_ready, n)
                        nc.vector.tensor_copy(cols[:, r * P:r * P + m], ps_t[:, 0:m]).then_inc(trans_copied, 1)
                dve.wait_ge(trans_copied, n)
                nc.vector.tensor_copy(index[:, :, 0], src_col[:])
                nc.vector.tensor_scalar(index[:, :, 1], key_col[:], float(N - 1), None, ALU.min)
                done(nc.vector.tensor_tensor(far[:], key_col[:], next_col[:], ALU.is_equal))
                done(nc.vector.scalar_tensor_tensor(index[:, :, 2], far[:], FAR, key_col[:], ALU.mult, ALU.add))

            @block.tensor
            def _(pe):
                pe.wait_ge(weights_in, 4 * 16)
                pe.wait_ge(consts_ready, 1)
                for k in range(K):
                    for i in range(K):
                        last = nc.tensor.transpose(ps_w[:, k * D + i * P:k * D + (i + 1) * P],
                                                   w1_in[:, i, k * P:(k + 1) * P], ident[:])
                last.then_inc(w1t_ready, 1)
                pe.wait_ge(b1rep_ready, 1)
                for k in range(K):
                    last = nc.tensor.matmul(ps_b[:, 0:D], b1_rep[:, k, :], w2_in[:, k, :], start=k == 0, stop=k == K - 1)
                last.then_inc(b1w2_ready, 1)
                pe.wait_ge(w1t_copied, 1)
                for i in range(K):
                    for k in range(K):
                        last = nc.tensor.matmul(ps_w[:, i * D:(i + 1) * D], w1_t[:, k, i * P:(i + 1) * P], w2_in[:, k, :],
                                                start=k == 0, stop=k == K - 1)
                last.then_inc(w12_ready, 1)
                pe.wait_ge(chunks_in, 3 * CR * 16)
                n = 0
                for v in range(3):
                    for r in range(CR):
                        m = min(P, C - r * P)
                        if n:
                            pe.wait_ge(trans_copied, n)
                        n += 1
                        nc.tensor.transpose(ps_t[:, 0:m], by_chunk[0:m, v, r, :], ident[0:m, 0:m]).then_inc(trans_ready, 1)


        end_phase()

        turn = [None]

        def stages(eng, count, lag, body, tail=0, first=2):
            for i in range(first * U):
                body(i, i % U)
            with eng.Fori(first, count // U - tail) as j:
                turn[0] = j
                for b in range(U):
                    body(j * U + b, b)
            for i in range(count - tail * U, count + lag):
                body(i, i % U)

        def b_count(i, b, lag):
            if isinstance(i, int):
                return (i - lag) // U
            return turn[0] + (b - lag) // U

        def half_count(i, b, lag):
            if isinstance(i, int):
                return (i - lag) // 2
            return turn[0] * (U // 2) + (b - lag) // 2

        pool_passed = nc.alloc_semaphore(name="pool_passed")

        def passed(pool):
            pool.sem_inc(pool_passed, 1)

        def slot_rows(table, c, first):
            return table[bass.ds(c * P + first, P), :] if not isinstance(c, int) else \
                table[first + c * P:first + (c + 1) * P, :]

        def col(table, c):
            return table[:, c:c + 1] if isinstance(c, int) else table[:, bass.ds(c, 1)]

        def cols(table, c):
            flat = table[:].rearrange("p c n -> p (c n)")
            return flat[:, 4 * c:4 * c + 4] if isinstance(c, int) else flat[:, bass.ds(c * 4, 4)]

        def runs(i, lag, count):
            return not isinstance(i, int) or 0 <= i - lag < count

        def after(eng, semaphore, value):
            if not isinstance(value, int) or value > 0:
                eng.wait_ge(semaphore, value)

        with ExitStack() as st, nc.Block() as block:
            xg = [sb(st, f"xg{b}", [P, T, D]) for b in range(U)]
            xb = [sb(st, f"xb{b}", [P, T, D]) for b in range(U)]
            x1 = [sb(st, f"x1{b}", [P, T, D]) for b in range(U)]
            n1 = [sb(st, f"n1{b}", [P, T, D]) for b in range(U)]
            n0 = [sb(st, f"n0{b}", [P, T, D]) for b in range(2)]
            h0t = [sb(st, f"h0t{b}", [P, T, K, P]) for b in range(2)]
            h1t = [sb(st, f"h1t{b}", [P, T, K, P]) for b in range(2)]
            yn = [sb(st, f"yn{b}", [P, T, D]) for b in range(2)]
            zg = [sb(st, f"zg{b}", [P, T, D]) for b in range(2)]
            zx = [sb(st, f"zx{b}", [P, T, D]) for b in range(2)]
            zm = [sb(st, f"zm{b}", [P, T, D]) for b in range(2)]
            og = [sb(st, f"og{b}", [P, T, D]) for b in range(2)]
            junk = sb(st, "junk", [P, T, D])
            bs = sb(st, "bs", [P, T, 6])
            mv0 = [sb(st, f"mv0{b}", [P, T, 2]) for b in range(2)]
            mv1 = [sb(st, f"mv1{b}", [P, T, 2]) for b in range(2)]
            ssq = [sb(st, f"ssq{b}", [P, T]) for b in range(2)]
            ve = sb(st, "ve", [P, 3, T])
            held = sb(st, "held", [P, 1])
            r0 = [sb(st, f"r0{b}", [P, T]) for b in range(2)]
            ry = [sb(st, f"ry{b}", [P, T]) for b in range(2)]
            r1 = [sb(st, f"r1{b}", [P, T]) for b in range(2)]
            ps_t0 = [pb(st, f"ps_t0{h}") for h in range(2)]
            ps_y = [pb(st, f"ps_y{h}") for h in range(2)]
            ps_t1 = [pb(st, f"ps_t1{h}") for h in range(2)]
            ps_z = [pb(st, f"ps_z{h}") for h in range(2)]

            x_loaded = [sem(f"x_loaded{b}") for b in range(U)]
            rows_stored = [sem(f"rows_stored{b}") for b in range(U)]
            out_stored = [sem(f"out_stored{b}") for b in range(2)]
            x_stats, x1_stats = sem("x_stats"), sem("x1_stats")
            x_moments, x1_moments = sem("x_moments"), sem("x1_moments")
            dve_t, dve_x1 = sem("dve_t"), sem("dve_x1")
            ve_ready = sem("ve_ready")
            r0_ready, ry_ready, r1_ready = sem("r0_ready"), sem("ry_ready"), sem("r1_ready")
            xb_ready, n0_ready, n1_ready = sem("xb_ready"), sem("n0_ready"), sem("n1_ready")
            t0_ready, t1_ready = sem("t0_ready"), sem("t1_ready")
            h0t_ready, h1t_ready = sem("h0t_ready"), sem("h1t_ready")
            y_ready, z_ready = sem("y_ready"), sem("z_ready")
            ssq_ready, zg_ready = sem("ssq_ready"), sem("zg_ready")
            zm_ready, zx_ready, og_ready = sem("zm_ready"), sem("zx_ready"), sem("og_ready")
            LAG = 7

            def group_rows(table, g):
                if isinstance(g, int):
                    at = min(g * GROUP, N - GROUP)
                    part = table[at:at + GROUP, :]
                else:
                    part = table[bass.ds(g * GROUP, GROUP), :]
                return part.rearrange("(p t) d -> p t d", t=T)

            @block.sync
            def _(sp):
                def step(i, b):
                    if runs(i, 0, G):
                        after(sp, n0_ready, i - U + 1)
                        after(sp, xb_ready, i - U + 1)
                        sp.dma_start(xg[b][:], group_rows(x, i)).then_inc(x_loaded[b], 16)
                    if runs(i, 4, G):
                        g = i - 4
                        if isinstance(g, int) and g == G - 1:
                            sp.wait_ge(rows_stored[(g - 1) % U], 16 * ((g - 1) // U + 1))
                        sp.wait_ge(n1_ready, g + 1)
                        sp.dma_start(group_rows(rows[0:N, :], g), n1[(b - 4) % U][:]).then_inc(rows_stored[(b - 4) % U], 16)
                    if runs(i, 6, G):
                        g = i - 6
                        if isinstance(g, int) and g == G - 1:
                            sp.wait_ge(out_stored[(g - 1) % 2], 16 * ((g - 1) // 2 + 1))
                        sp.wait_ge(og_ready, g + 1)
                        sp.dma_start(group_rows(out, g), og[b % 2][:]).then_inc(out_stored[b % 2], 16)

                stages(sp, G, LAG, step, tail=1)
                for b in range(U):
                    sp.wait_ge(rows_stored[b], 16 * (G // U))
                for b in range(2):
                    sp.wait_ge(out_stored[b], 16 * (G // 2))

            @block.vector
            def _(dve):
                def step(i, b):
                    if runs(i, 1, G):
                        g, c = i - 1, (b - 1) % U
                        dve.wait_ge(r0_ready, g + 1)
                        after(dve, t0_ready, 2 * (g - 1))
                        for t in range(T):
                            last = nc.vector.tensor_scalar(n0[c % 2][:, t, :], xg[c][:, t, :], mv0[c % 2][:, t, 0:1],
                                                           r0[c % 2][:, t:t + 1], ALU.subtract, ALU.mult)
                        last.then_inc(n0_ready, 1)
                    if runs(i, 3, G):
                        g, c = i - 3, (b - 3) % U
                        dve.wait_ge(r1_ready, g + 1)
                        if not isinstance(g, int) or g >= U:
                            dve.wait_ge(rows_stored[c], (b_count(i, b, 3)) * 16)
                        after(dve, t1_ready, 2 * (g - U + 1))
                        for t in range(T):
                            last = nc.vector.tensor_scalar(n1[c][:, t, :], x1[c][:, t, :], mv1[c % 2][:, t, 0:1],
                                                           r1[c % 2][:, t:t + 1], ALU.subtract, ALU.mult)
                        last.then_inc(n1_ready, 1)
                    if runs(i, 0, G):
                        dve.wait_ge(x_loaded[b], (b_count(i, b, 0) + 1) * 16)
                        for t in range(T):
                            nc.vector.bn_stats(bs[:, t, :], xg[b][:, t, :]).then_inc(x_stats, 1)
                        dve.wait_ge(x_stats, (i + 1) * T)
                        nc.vector.memset(held[:], 0.0)
                        for t in range(T):
                            last = nc.vector.bn_aggr(mv0[b % 2][:, t, :], bs[:, t, :])
                        last.then_inc(x_moments, 1)
                    if runs(i, 2, G):
                        g, c = i - 2, (b - 2) % U
                        dve.wait_ge(ry_ready, g + 1)
                        dve.wait_ge(y_ready, 2 * g + 2)
                        for t in range(T):
                            last = nc.vector.scalar_tensor_tensor(
                                yn[c % 2][:, t, :], ps_y[t // 2][:, (t % 2) * D:(t % 2 + 1) * D], ry[c % 2][:, t:t + 1],
                                gamma_d[:], ALU.mult, ALU.mult)
                        last.then_inc(dve_t, 1)
                        dve.wait_ge(dve_t, g + 1)
                        dve.wait_ge(xb_ready, g + 1)
                        after(dve, zx_ready, g - U + 1)
                        nc.vector.tensor_tensor(x1[c][:], yn[c % 2][:], xb[c][:], ALU.add).then_inc(dve_x1, 1)
                        dve.wait_ge(dve_x1, g + 1)
                        for t in range(T):
                            nc.vector.bn_stats(bs[:, t, :], x1[c][:, t, :]).then_inc(x1_stats, 1)
                        dve.wait_ge(x1_stats, (g + 1) * T)
                        nc.vector.memset(held[:], 0.0)
                        for t in range(T):
                            last = nc.vector.bn_aggr(mv1[c % 2][:, t, :], bs[:, t, :])
                        last.then_inc(x1_moments, 1)
                    if runs(i, 4, G):
                        g, c = i - 4, (b - 4) % U
                        dve.wait_ge(zg_ready, 2 * g + 2)
                        after(dve, og_ready, g - 1)
                        nc.vector.scalar_tensor_tensor(zm[c % 2][:], zg[c % 2][:], 0.0,
                                                       am1_b[:].unsqueeze(1).broadcast_to([P, T, D]),
                                                       ALU.min, ALU.mult).then_inc(zm_ready, 1)

                stages(dve, G, LAG, step)

            @block.gpsimd
            def _(pool):
                def inv_sd(to, var, g, b, s, kind, add):
                    nc.gpsimd.tensor_tensor(ve[:, kind, :], var, add[:, 0:T], ALU.add).then_inc(ve_ready, 1)
                    pool.wait_ge(ve_ready, ve_count(g, kind))
                    nc.gpsimd.tensor_tensor(to, ve[:, kind, :], neg_half[:, 0:T], ALU.pow).then_inc(s, 1)

                def ve_count(i, kind):
                    if isinstance(i, int):
                        before = sum(min(max(i - lag, 0), G) for lag in (0, 1, 2))
                        return before + sum(0 <= i - lag < G for lag in order[:order.index(kind) + 1])
                    return i * 3 - 3 + order.index(kind) + 1

                order = (0, 2, 1)

                def step(i, b):
                    if runs(i, 0, G):
                        pool.wait_ge(x_loaded[b], (b_count(i, b, 0) + 1) * 16)
                        after(pool, dve_x1, i - U + 1)
                        nc.gpsimd.tensor_tensor(xb[b][:], xg[b][:], beta_b[:].unsqueeze(1).broadcast_to([P, T, D]),
                                                ALU.add).then_inc(xb_ready, 1)
                    if runs(i, 4, G):
                        g, c = i - 4, (b - 4) % U
                        pool.wait_ge(zg_ready, 2 * g + 2)
                        after(pool, og_ready, g - 1)
                        nc.gpsimd.tensor_tensor(zx[c % 2][:], zg[c % 2][:], x1[c][:], ALU.add).then_inc(zx_ready, 1)
                    if runs(i, 5, G):
                        g, c = i - 5, (b - 5) % U
                        pool.wait_ge(zm_ready, g + 1)
                        if not isinstance(g, int) or g >= 2:
                            pool.wait_ge(out_stored[c % 2], half_count(i, b, 5) * 16)
                        pool.wait_ge(zx_ready, g + 1)
                        nc.gpsimd.tensor_tensor(og[c % 2][:], zx[c % 2][:], zm[c % 2][:], ALU.add).then_inc(og_ready, 1)
                    if runs(i, 0, G):
                        pool.wait_ge(x_moments, i + 1)
                        inv_sd(r0[b % 2][:], mv0[b % 2][:, :, 1], i, b, r0_ready, 0, eps)
                    if runs(i, 2, G):
                        g, c = i - 2, (b - 2) % U
                        pool.wait_ge(x1_moments, g + 1)
                        inv_sd(r1[c % 2][:], mv1[c % 2][:, :, 1], i, b, r1_ready, 2, eps)
                    if runs(i, 1, G):
                        g, c = i - 1, (b - 1) % U
                        pool.wait_ge(ssq_ready, 2 * g + 2)
                        inv_sd(ry[c % 2][:], ssq[c % 2][:], i, b, ry_ready, 1, eps_d)

                stages(pool, G, LAG, step)

            @block.scalar
            def _(act):
                def step(i, b):
                    for lag, ps, ready, to, done, used in ((1, ps_t0, t0_ready, h0t, h0t_ready, y_ready),
                                                           (3, ps_t1, t1_ready, h1t, h1t_ready, z_ready)):
                        if runs(i, lag, G):
                            g, c = i - lag, (b - lag) % U
                            for h in range(2):
                                act.wait_ge(ready, 2 * g + h + 1)
                                after(act, used, 2 * (g - 2) + h + 1)
                                nc.scalar.activation(to[c % 2][:, 2 * h:2 * h + 2, :, :].rearrange("p t k n -> p (t k n)"),
                                                     ps[h][:], ACT.Relu).then_inc(done, 1)
                    if runs(i, 1, G):
                        g, c = i - 1, (b - 1) % U
                        for h in range(2):
                            act.wait_ge(y_ready, 2 * g + h + 1)
                            after(act, ry_ready, g - 1)
                            after(act, ssq_ready, 2 * g)
                            for t in range(2):
                                last = nc.scalar.activation(junk[:, 2 * h + t, :], ps_y[h][:, t * D:(t + 1) * D], ACT.Square,
                                                            accum_out=ssq[c % 2][:, 2 * h + t:2 * h + t + 1])
                            last.then_inc(ssq_ready, 1)
                    if runs(i, 3, G):
                        g, c = i - 3, (b - 3) % U
                        for h in range(2):
                            act.wait_ge(z_ready, 2 * g + h + 1)
                            after(act, zm_ready, g - 1)
                            after(act, zx_ready, g - 1)
                            nc.scalar.activation(zg[c % 2][:, 2 * h:2 * h + 2, :].rearrange("p t d -> p (t d)"),
                                                 ps_z[h][:], ACT.Copy).then_inc(zg_ready, 1)

                stages(act, G, LAG, step)

            @block.tensor
            def _(pe):
                def step(i, b):
                    for lag, of, ready, to, copied, done in ((1, n0, n0_ready, ps_t0, h0t_ready, t0_ready),
                                                             (3, n1, n1_ready, ps_t1, h1t_ready, t1_ready)):
                        if runs(i, lag, G):
                            g, c = i - lag, (b - lag) % U
                            pe.wait_ge(ready, g + 1)
                            for h in range(2):
                                after(pe, copied, 2 * (g - 1) + h + 1)
                                for t in range(2):
                                    for k in range(K):
                                        last = nc.tensor.transpose(
                                            to[h][:, (t * K + k) * P:(t * K + k + 1) * P],
                                            of[c % len(of)][:, 2 * h + t, k * P:(k + 1) * P], ident[:])
                                last.then_inc(done, 1)
                    for lag, of, ready, to, used, w, bias, done in (
                            (1, h0t, h0t_ready, ps_y, dve_t, w_sum, bias_yc, y_ready),
                            (3, h1t, h1t_ready, ps_z, zg_ready, w_12, bias_z, z_ready)):
                        if runs(i, lag, G):
                            g, c = i - lag, (b - lag) % U
                            for h in range(2):
                                pe.wait_ge(ready, 2 * g + h + 1)
                                after(pe, used, g if used is dve_t else 2 * (g - 1) + h + 1)
                                for t in range(2):
                                    o = to[h][:, t * D:(t + 1) * D]
                                    for k in range(K):
                                        nc.tensor.matmul(o, of[c % 2][:, 2 * h + t, k, :], w[:, k, :],
                                                         start=k == 0, stop=False)
                                    last = nc.tensor.matmul(o, ones3[:], bias[:], start=False, stop=True)
                                last.then_inc(done, 1)

                stages(pe, G, LAG, step)


        end_phase()

        with ExitStack() as st, nc.Block() as block:
            kr = [sb(st, f"kr{b}", [P, P + 2]) for b in range(U)]
            stage = [sb(st, f"stage{b}", [P, 4], i32) for b in range(U)]
            xe = [sb(st, f"xe{b}", [P, 2, D]) for b in range(U)]
            xdb = [sb(st, f"xdb{b}", [P, D]) for b in range(U)]
            bse = sb(st, "bse", [P, 4, 6])
            mve = [sb(st, f"mve{b}", [P, 4, 2]) for b in range(2)]
            vv = [sb(st, f"vv{b}", [P, 5]) for b in range(2)]
            rr = [sb(st, f"rr{b}", [P, 5]) for b in range(2)]
            nbe = [sb(st, f"nbe{b}", [P, 4]) for b in range(2)]
            he = [sb(st, f"he{b}", [P, 2, D]) for b in range(2)]
            het = [sb(st, f"het{b}", [P, 2 * K, P]) for b in range(2)]
            hs = [sb(st, f"hs{b}", [P, D + 2 * H]) for b in range(U)]
            hd = [sb(st, f"hd{b}", [P, 2 * D]) for b in range(U)]
            edge = [sb(st, f"edge{b}", [H, P + 1]) for b in range(U)]
            neq = sb(st, "neq", [H, P + 1])
            same = [sb(st, f"same{b}", [P, P]) for b in range(U)]
            cont = [sb(st, f"cont{b}", [P, P]) for b in range(U)]
            lkt = [sb(st, f"lkt{b}", [P, 2 * H]) for b in range(2)]
            lk = [sb(st, f"lk{b}", [H, 2 * P]) for b in range(2)]
            mx = sb(st, "mx", [H, P])
            fw = sb(st, "fw", [H, P])
            mm = [sb(st, f"mm{b}", [H, P]) for b in range(2)]
            dm = sb(st, "dm", [H, 3, P])
            ex = [sb(st, f"ex{b}", [H, 3, P]) for b in range(2)]
            xw = [sb(st, f"xw{b}", [P, 3 * H]) for b in range(2)]
            msg = [sb(st, f"msg{b}", [P, NH + 1]) for b in range(2)]
            car = sb(st, "car", [P, NH + 1])
            acc = [sb(st, f"acc{b}", [P, NH + 1]) for b in range(2)]
            own = [sb(st, f"own{b}", [P, D]) for b in range(2)]
            own2 = sb(st, "own2", [P, D])
            den = sb(st, "den", [P, H])
            rden = sb(st, "rden", [P, H])
            nrm = sb(st, "nrm", [P, D])
            ye = [sb(st, f"ye{b}", [P, D]) for b in range(U)]
            yg = sb(st, "yg", [P, D])
            x1e = [sb(st, f"x1e{b}", [P, D]) for b in range(U)]
            n1e = [sb(st, f"n1e{b}", [P, D]) for b in range(2)]
            prow = [sb(st, f"prow{b}", [P, 2]) for b in range(U)]
            pidx = [sb(st, f"pidx{b}", [P, 4], i32) for b in range(U)]
            hold = sb(st, "hold", [P, U])
            ps_t = pb(st, "ps_te")
            ps_hs = pb(st, "ps_hs")
            ps_hd = [pb(st, f"ps_hd{b}") for b in range(2)]
            ps_l = pb(st, "ps_le")
            ps_x = pb(st, "ps_xe")
            ps_a = pb(st, "ps_ae")
            ps_c = pb(st, "ps_ce")

            kr_loaded = [sem(f"kr_loaded{b}") for b in range(U)]
            src_gathered = [sem(f"src_gathered{b}") for b in range(U)]
            dst_gathered = [sem(f"dst_gathered{b}") for b in range(U)]
            place_sent = [sem(f"place_sent{b}") for b in range(U)]
            x1_sent = [sem(f"x1_sent{b}") for b in range(U)]
            n1_sent = [sem(f"n1_sent{b}") for b in range(2)]
            (e_staged, e_xdb, e_stats, e_moments, e_var, e_nb, e_h, e_trans, e_het, e_hs, e_hd, e_hs_sb, e_hd_sb,
             e_neq, e_sel, e_edge, e_leaky, e_logits, e_lk, e_pair, e_fwd, e_max, e_diff, e_exp, e_exp_t, e_xw, e_msg,
             e_sums, e_car, e_acc, e_deg, e_own, e_own2, e_den, e_rden, e_nrm, e_y, y_stats,
             e_yg, e_x1, x1_stats, e_n1, e_prow, e_dis_own, rr_ready, init_done) = [
                sem("e_" + n) for n in (
                    "staged xdb stats moments var nb h trans het hs hd hs_sb hd_sb neq sel edge leaky logits lk pair "
                    "fwd max diff exp exp_t xw msg sums car acc deg own own2 den rden nrm y ystats "
                    "yg x1 x1stats n1 prow disown rr init").split()]
            LAGE = 9

            def until(eng, semaphore, c, per=1):
                if isinstance(c, int):
                    c = min(c, C - 1)
                after(eng, semaphore, (c + 1) * per)

            def normed(i):
                return not isinstance(i, int) or 1 <= i < C + 6

            @block.sync
            def _(sp):
                def step(i, b):
                    if runs(i, 0, C):
                        until(sp, e_sel, i - U, 2)
                        until(sp, e_neq, i - U)
                        at = keys[i * P:i * P + P + 2] if isinstance(i, int) else keys[bass.ds(i * P, P + 2)]
                        sp.dma_start(kr[b][:], at.partition_broadcast(P)).then_inc(kr_loaded[b], 16)
                    if runs(i, 6, C):
                        c, o = i - 6, (b - 6) % U
                        sp.wait_ge(e_x1, c + 1)
                        sp.dma_start(slot_rows(x1_slots, c, 0), x1e[o][:]).then_inc(x1_sent[o], 16)
                    if runs(i, 8, C):
                        c, o = i - 8, (b - 8) % 2
                        sp.wait_ge(e_n1, c + 1)
                        sp.dma_start(slot_rows(rows, c, N), n1e[o][:]).then_inc(n1_sent[o], 16)

                stages(sp, C, LAGE, step, first=3)
                for b in range(U):
                    sp.wait_ge(x1_sent[b], 16 * (C // U))
                for b in range(2):
                    sp.wait_ge(n1_sent[b], 16 * (C // 2))

            @block.gpsimd
            def _(pool):
                for b in range(2):
                    nc.gpsimd.memset(vv[b][:], 1.0).then_inc(init_done, 1)

                def step(i, b):
                    if runs(i, 2, C):
                        c, o = i - 2, (b - 2) % U
                        until(pool, e_x1, c - U)
                        pool.wait_ge(dst_gathered[o], 16 * (b_count(i, b, 2) + 1))
                        nc.gpsimd.tensor_tensor(xdb[o][:], xe[o][:, 1, :], beta_b[:], ALU.add).then_inc(e_xdb, 1)
                    if runs(i, 0, C):
                        until(pool, e_h, i - U)
                        until(pool, e_xdb, i - U)
                        passed(pool)
                        nc.gpsimd.tensor_copy(stage[b][:], cols(index, i)).then_inc(e_staged, 1)
                        pool.wait_ge(e_staged, i + 1)
                        passed(pool)
                        pool.indirect_dma_start(xe[b][:, 0, :], None, x, bass.IndirectOffsetOnAxis(stage[b][:, 0:1], 0)
                                                ).then_inc(src_gathered[b], 16)
                        pool.indirect_dma_start(xe[b][:, 1, :], None, x, bass.IndirectOffsetOnAxis(stage[b][:, 1:2], 0)
                                                ).then_inc(dst_gathered[b], 16)
                    if isinstance(i, int) and i == 0:
                        pool.wait_ge(init_done, 2)
                    for s, lag in ((e_var, 1), (e_deg, 5)):
                        if normed(i) if s is e_var else runs(i, lag, C):
                            pool.wait_ge(s, i - lag + 1)
                    for s, lag in ((e_h, 3), (e_x1, 7), (e_n1, 8), (e_dis_own, 7)):
                        until(pool, s, i - lag)
                    after(pool, rr_ready, i - 1)
                    nc.gpsimd.tensor_tensor(rr[b % 2][:], vv[b % 2][:], neg_half[:, 0:5], ALU.pow).then_inc(rr_ready, 1)
                    if runs(i, 3, C):
                        c, o = i - 3, (b - 3) % U
                        pool.wait_ge(e_xw, c + 1)
                        pool.wait_ge(e_hd_sb, c + 1)
                        until(pool, e_own2, c - 2)
                        nc.gpsimd.tensor_tensor(own[o % 2][:].rearrange("p (h c) -> p h c", h=H),
                                                hd[o][:, 0:D].rearrange("p (h c) -> p h c", h=H),
                                                xw[o % 2][:, H:2 * H].unsqueeze(2).broadcast_to([P, H, HC]),
                                                ALU.mult).then_inc(e_own, 1)
                    if runs(i, 4, C):
                        c, q = i - 4, (b - 4) % 2
                        pool.wait_ge(e_acc, c + 1)
                        pool.wait_ge(e_own, c + 1)
                        until(pool, e_nrm, c - 1)
                        nc.gpsimd.tensor_tensor(own2[:].rearrange("p (h c) -> p h c", h=H),
                                                own[q][:].rearrange("p (h c) -> p h c", h=H),
                                                acc[q][:, 0:NH].rearrange("p (h c) -> p h c", h=H)[:, :, 0:HC],
                                                ALU.add).then_inc(e_own2, 1)
                    if runs(i, 5, C):
                        c, o = i - 5, (b - 5) % U
                        pool.wait_ge(rr_ready, i + 1)
                        if not isinstance(c, int) or c >= U:
                            pool.wait_ge(place_sent[o], 16 * b_count(i, b, 5))
                        passed(pool)
                        nc.gpsimd.tensor_copy(col(dis_own, c), rr[b % 2][:, 4:5]).then_inc(e_dis_own, 1)
                        nc.gpsimd.tensor_copy(prow[o][:, 1:2], rr[b % 2][:, 4:5]).then_inc(e_prow, 1)
                        nc.gpsimd.tensor_copy(prow[o][:, 0:1], col(slot_row, c)).then_inc(e_prow, 1)
                        nc.gpsimd.tensor_copy(pidx[o][:], cols(index, c)).then_inc(e_prow, 1)
                        pool.wait_ge(e_prow, 3 * (c + 1))
                        passed(pool)
                        pool.indirect_dma_start(place, bass.IndirectOffsetOnAxis(pidx[o][:, 2:3], 0), prow[o][:], None,
                                                bounds_check=N - 1, oob_is_err=False).then_inc(place_sent[o], 16)

                stages(pool, C, LAGE, step, first=3)
                for b in range(U):
                    pool.wait_ge(place_sent[b], 16 * (C // U))

            @block.vector
            def _(dve):
                def by_head(ap):
                    return ap.rearrange("p (h c) -> p h c", h=H)

                def heads(ap, n):
                    return ap.unsqueeze(2).broadcast_to([P, H, n])

                nc.vector.memset(acc[1][:], 0.0).then_inc(init_done, 1)
                for b in range(2):
                    nc.vector.memset(msg[b][:, NH:NH + 1], 1.0).then_inc(init_done, 1)
                    nc.vector.memset(mve[b][:], 1.0).then_inc(init_done, 1)
                nc.vector.memset(car[:, NH:NH + 1], 0.0).then_inc(init_done, 1)
                dve.wait_ge(init_done, 8)

                def step(i, b):
                    if runs(i, 3, C):
                        c, q, o = i - 3, (b - 3) % 2, (b - 3) % U
                        dve.wait_ge(e_lk, c + 1)
                        nc.vector.tensor_tensor(mx[:], lk[q][:, 0:P], lk[q][:, P:2 * P], ALU.max).then_inc(e_pair, 1)
                    if runs(i, 1, C):
                        c, o = i - 1, (b - 1) % U
                        dve.wait_ge(src_gathered[o], 16 * (b_count(i, b, 1) + 1))
                        nc.vector.bn_stats(bse[:, 0, :], xe[o][:, 0, :]).then_inc(e_stats, 1)
                        dve.wait_ge(dst_gathered[o], 16 * (b_count(i, b, 1) + 1))
                        nc.vector.bn_stats(bse[:, 1, :], xe[o][:, 1, :]).then_inc(e_stats, 1)
                    if runs(i, 3, C):
                        c, q, o = i - 3, (b - 3) % 2, (b - 3) % U
                        dve.wait_ge(e_pair, c + 1)
                        before = low[:] if isinstance(c, int) and c == 0 else mm[1 - q][:, P - 1:P]
                        nc.vector.tensor_tensor_scan(fw[:], edge[o][:, 0:P], mx[:], before, ALU.add, ALU.max
                                                     ).then_inc(e_fwd, 1)
                    if runs(i, 5, C):
                        c, o = i - 5, (b - 5) % U
                        dve.wait_ge(e_y, c + 1)
                        nc.vector.bn_stats(bse[:, 2, :], ye[o][:]).then_inc(y_stats, 1)
                    if runs(i, 3, C):
                        c, q, o = i - 3, (b - 3) % 2, (b - 3) % U
                        dve.wait_ge(e_fwd, c + 1)
                        nc.vector.tensor_tensor_scan(mm[q][:, ::-1], edge[o][:, P:0:-1], fw[:, ::-1], low[:],
                                                     ALU.add, ALU.max).then_inc(e_max, 1)
                    if runs(i, 6, C):
                        c, o = i - 6, (b - 6) % U
                        dve.wait_ge(e_x1, c + 1)
                        nc.vector.bn_stats(bse[:, 3, :], x1e[o][:]).then_inc(x1_stats, 1)
                    if runs(i, 3, C):
                        c, q, o = i - 3, (b - 3) % 2, (b - 3) % U
                        dve.wait_ge(e_max, c + 1)
                        until(dve, e_exp, c - 1)
                        nc.vector.tensor_tensor(dm[:, 0:2, :], mm[q][:].unsqueeze(1).broadcast_to([H, 2, P]),
                                                lk[q][:].rearrange("h (n p) -> h n p", n=2), ALU.subtract
                                                ).then_inc(e_diff, 1)
                        nc.vector.tensor_scalar(dm[:, 2, :], mm[q][:], before, 0.0, ALU.subtract, ALU.max
                                                ).then_inc(e_diff, 1)
                    for s, lag, per in ((e_stats, 1, 2), (y_stats, 5, 1), (x1_stats, 6, 1)):
                        if runs(i, lag, C):
                            dve.wait_ge(s, (i - lag + 1) * per)
                    nc.vector.memset(hold[:, b:b + 1], 0.0)
                    for n, lag in ((0, 1), (1, 1), (2, 5), (3, 6)):
                        if runs(i, lag, C):
                            last = nc.vector.bn_aggr(mve[b % 2][:, n, :], bse[:, n, :])
                    if normed(i):
                        last.then_inc(e_moments, 1)
                    if not isinstance(i, int) or i >= 2:
                        dve.wait_ge(rr_ready, i - 1)
                    if normed(i):
                        dve.wait_ge(e_moments, i)
                        nc.vector.tensor_scalar(vv[b % 2][:, 0:4], mve[b % 2][:, :, 1], EPS, None, ALU.add
                                                ).then_inc(e_var, 1)
                    if runs(i, 5, C):
                        q = (b - 5) % 2
                        nc.vector.tensor_scalar(vv[b % 2][:, 4:5], acc[q][:, NH:NH + 1], 1.0, 1.0, ALU.add, ALU.max
                                                ).then_inc(e_deg, 1)
                    if runs(i, 1, C):
                        c, o = i - 1, (b - 1) % U
                        dve.wait_ge(kr_loaded[o], 16 * (b_count(i, b, 1) + 1))
                        until(dve, e_edge, c - 1)
                        nc.vector.tensor_tensor(neq[:], kr[o][0:H, 0:P + 1], kr[o][0:H, 1:P + 2], ALU.not_equal
                                                ).then_inc(e_neq, 1)
                        until(dve, e_sums, c - U)
                        nc.vector.scalar_tensor_tensor(same[o][:], kr[o][:, 1:P + 1], col(key_col, c), tri[:],
                                                       ALU.is_equal, ALU.mult).then_inc(e_sel, 1)
                        nc.vector.tensor_scalar(cont[o][:], kr[o][:, 1:P + 1], kr[o][:, 0:1], last_row[:], ALU.is_equal,
                                                ALU.mult).then_inc(e_sel, 1)
                        dve.wait_ge(e_neq, c + 1)
                        until(dve, e_max, c - U)
                        nc.vector.tensor_scalar(edge[o][:], neq[:], LOW, None, ALU.mult).then_inc(e_edge, 1)
                    r = rr[b % 2]
                    if runs(i, 4, C):
                        c, q = i - 4, (b - 4) % 2
                        dve.wait_ge(e_sums, c + 1)
                        nc.vector.tensor_tensor(by_head(car[:, 0:NH]), by_head(ps_c[:, 0:NH]),
                                                heads(xw[q][:, 2 * H:3 * H], HC + 1), ALU.mult).then_inc(e_car, 1)
                    if runs(i, 3, C):
                        c, q = i - 3, (b - 3) % 2
                        dve.wait_ge(e_exp_t, c + 1)
                        until(dve, e_den, c - 2)
                        until(dve, e_own, c - 2)
                        nc.vector.tensor_copy(xw[q][:], ps_x[:, 0:3 * H]).then_inc(e_xw, 1)
                    if runs(i, 4, C):
                        c, q = i - 4, (b - 4) % 2
                        dve.wait_ge(e_car, c + 1)
                        nc.vector.tensor_tensor(acc[q][:], car[:], ps_a[:, 0:NH + 1], ALU.add).then_inc(e_acc, 1)
                    if runs(i, 3, C):
                        c, q, o = i - 3, (b - 3) % 2, (b - 3) % U
                        dve.wait_ge(e_xw, c + 1)
                        m = by_head(msg[q][:, 0:NH])
                        nc.vector.tensor_copy(m[:, :, HC], xw[q][:, 0:H]).then_inc(e_msg, 1)
                        nc.vector.tensor_tensor(m[:, :, 0:HC], by_head(hs[o][:, 0:D]), heads(xw[q][:, 0:H], HC), ALU.mult
                                                ).then_inc(e_msg, 1)
                    if runs(i, 4, C):
                        c, q = i - 4, (b - 4) % 2
                        a = by_head(acc[q][:, 0:NH])
                        dve.wait_ge(e_acc, c + 1)
                        nc.vector.scalar_tensor_tensor(den[:], a[:, :, HC], TINY, xw[q][:, H:2 * H], ALU.add, ALU.add
                                                       ).then_inc(e_den, 1)
                    if normed(i):
                        dve.wait_ge(rr_ready, i + 1)
                        until(dve, e_h, i - 3)
                        until(dve, e_n1, i - 8)
                        nc.vector.scalar_tensor_tensor(nbe[b % 2][:], mve[b % 2][:, :, 0], -1.0, r[:, 0:4], ALU.mult, ALU.mult
                                                       ).then_inc(e_nb, 1)
                    if runs(i, 2, C):
                        c, q, o = i - 2, (b - 2) % 2, (b - 2) % U
                        dve.wait_ge(e_hs_sb, c + 1)
                        until(dve, e_logits, c - 2)
                        nc.vector.scalar_tensor_tensor(lkt[q][:], hs[o][:, D:D + 2 * H], SLOPE, hs[o][:, D:D + 2 * H],
                                                       ALU.mult, ALU.max).then_inc(e_leaky, 1)
                    if runs(i, 4, C):
                        c, q = i - 4, (b - 4) % 2
                    if runs(i, 5, C):
                        c, o = i - 5, (b - 5) % U
                        until(dve, e_x1, c - 1)
                        nc.vector.scalar_tensor_tensor(yg[:], ye[o][:], mve[b % 2][:, 2, 0:1], gamma_b[:], ALU.subtract,
                                                       ALU.mult).then_inc(e_yg, 1)
                    if runs(i, 4, C):
                        c, q = i - 4, (b - 4) % 2
                        dve.wait_ge(e_den, c + 1)
                        nc.vector.reciprocal(rden[:], den[:]).then_inc(e_rden, 1)
                    if runs(i, 4, C):
                        c, q = i - 4, (b - 4) % 2
                        dve.wait_ge(e_rden, c + 1)
                        dve.wait_ge(e_own2, c + 1)
                        nc.vector.tensor_tensor(by_head(nrm[:]), by_head(own2[:]), heads(rden[:], HC), ALU.mult
                                                ).then_inc(e_nrm, 1)
                    if runs(i, 5, C):
                        c, o = i - 5, (b - 5) % U
                        dve.wait_ge(e_yg, c + 1)
                        dve.wait_ge(e_xdb, c + 1)
                        until(dve, e_n1, c - U)
                        if not isinstance(c, int) or c >= U:
                            dve.wait_ge(x1_sent[o], 16 * b_count(i, b, 5))
                        nc.vector.scalar_tensor_tensor(x1e[o][:], yg[:], r[:, 2:3], xdb[o][:], ALU.mult, ALU.add
                                                       ).then_inc(e_x1, 1)
                    if runs(i, 4, C):
                        c, o = i - 4, (b - 4) % U
                        dve.wait_ge(e_nrm, c + 1)
                        nc.vector.tensor_tensor(ye[o][:], nrm[:], hd[o][:, D:2 * D], ALU.add).then_inc(e_y, 1)

                stages(dve, C, LAGE, step, first=3)

            @block.scalar
            def _(act):
                def step(i, b):
                    r = rr[(b - 1) % 2]
                    if runs(i, 2, C):
                        c, q = i - 2, (b - 2) % 2
                        act.wait_ge(e_trans, c + 1)
                        until(act, e_hd, c - 2)
                        nc.scalar.activation(het[q][:].rearrange("p k n -> p (k n)"), ps_t[:], ACT.Copy).then_inc(e_het, 1)
                    if runs(i, 3, C):
                        c, q = i - 3, (b - 3) % 2
                        act.wait_ge(e_diff, 2 * (c + 1))
                        until(act, e_exp_t, c - 2)
                        nc.scalar.activation(ex[q][:], dm[:], ACT.Exp, scale=-1.0).then_inc(e_exp, 1)
                    if runs(i, 2, C):
                        c, o = i - 2, (b - 2) % U
                        act.wait_ge(e_hs, c + 1)
                        until(act, e_msg, c - U, 2)
                        nc.scalar.activation(hs[o][:], ps_hs[:, 0:D + 2 * H], ACT.Copy).then_inc(e_hs_sb, 1)
                    if runs(i, 1, C):
                        c, q, o = i - 1, (b - 1) % 2, (b - 1) % U
                        act.wait_ge(e_nb, i)
                        until(act, e_trans, c - 2)
                        for n in range(2):
                            last = nc.scalar.activation(he[q][:, n, :], xe[o][:, n, :], ACT.Relu, bias=nbe[b % 2][:, n:n + 1],
                                                        scale=rr[b % 2][:, n:n + 1])
                        last.then_inc(e_h, 1)
                    if runs(i, 2, C):
                        c, q = i - 2, (b - 2) % 2
                        act.wait_ge(e_logits, c + 1)
                        until(act, e_diff, c - 2, 2)
                        nc.scalar.activation(lk[q][:], ps_l[0:H, 0:2 * P], ACT.Copy).then_inc(e_lk, 1)
                    if runs(i, 2, C):
                        c, o = i - 2, (b - 2) % U
                        act.wait_ge(e_hd, c + 1)
                        until(act, e_y, c - U)
                        nc.scalar.activation(hd[o][:], ps_hd[o % 2][:], ACT.Copy).then_inc(e_hd_sb, 1)
                    if runs(i, 7, C):
                        c, q, o = i - 7, (b - 7) % 2, (b - 7) % U
                        act.wait_ge(e_nb, i - 1)
                        if not isinstance(c, int) or c >= 2:
                            act.wait_ge(n1_sent[q], 16 * half_count(i, b, 7))
                        nc.scalar.activation(n1e[q][:], x1e[o][:], ACT.Relu, bias=nbe[(b - 1) % 2][:, 3:4], scale=r[:, 3:4]
                                             ).then_inc(e_n1, 1)

                stages(act, C, LAGE, step, first=3)

            @block.tensor
            def _(pe):
                pe.wait_ge(init_done, 8)

                def step(i, b):
                    if runs(i, 2, C):
                        c, q = i - 2, (b - 2) % 2
                        pe.wait_ge(e_h, c + 1)
                        until(pe, e_het, c - 1)
                        for n in range(2):
                            for k in range(K):
                                last = nc.tensor.transpose(ps_t[:, (n * K + k) * P:(n * K + k + 1) * P],
                                                           he[q][:, n, k * P:(k + 1) * P], ident[:])
                        last.then_inc(e_trans, 1)
                    if runs(i, 4, C):
                        c, q, o = i - 4, (b - 4) % 2, (b - 4) % U
                        pe.wait_ge(e_msg, 2 * (c + 1))
                        until(pe, e_acc, c - 1)
                        nc.tensor.matmul(ps_a[:, 0:NH + 1], same[o][:], msg[q][:], start=True, stop=False)
                        nc.tensor.matmul(ps_a[:, NH:NH + 1], cont[o][:], acc[1 - q][:, NH:NH + 1], start=False, stop=True)
                        nc.tensor.matmul(ps_c[:, 0:NH], cont[o][:], acc[1 - q][:, 0:NH], start=True, stop=True
                                         ).then_inc(e_sums, 1)
                    if runs(i, 2, C):
                        c, q = i - 2, (b - 2) % 2
                        pe.wait_ge(e_het, c + 1)
                        until(pe, e_hs_sb, c - 1)
                        for k in range(K):
                            nc.tensor.matmul(ps_hs[:, 0:D + 2 * H], het[q][:, k, :], w_src[:, k, :], start=k == 0, stop=False)
                        for k in range(K):
                            last = nc.tensor.matmul(ps_hs[:, D:D + 2 * H], het[q][:, K + k, :], w_att[:, k, :, :],
                                                    start=False, stop=k == K - 1)
                        last.then_inc(e_hs, 1)
                    if runs(i, 2, C):
                        c, q = i - 2, (b - 2) % 2
                        until(pe, e_hd_sb, c - 2)
                        nc.tensor.matmul(ps_hd[q][:], het[q][:, K, :], w_all[:, 0, :], start=True, stop=False)
                    if runs(i, 3, C):
                        c, q = i - 3, (b - 3) % 2
                        pe.wait_ge(e_exp, c + 1)
                        until(pe, e_xw, c - 1)
                        for n in range(3):
                            last = nc.tensor.matmul(ps_x[:, n * H:(n + 1) * H], ex[q][:, n, :], ident[0:H, 0:H],
                                                    start=True, stop=True)
                        last.then_inc(e_exp_t, 1)
                    if runs(i, 2, C):
                        c, q = i - 2, (b - 2) % 2
                        for k in range(1, K):
                            nc.tensor.matmul(ps_hd[q][:], het[q][:, K + k, :], w_all[:, k, :], start=False, stop=False)
                        nc.tensor.matmul(ps_hd[q][:, D:2 * D], ones3[:], bias_y[:], start=False, stop=True
                                         ).then_inc(e_hd, 1)
                    if runs(i, 2, C):
                        c, q = i - 2, (b - 2) % 2
                        pe.wait_ge(e_leaky, c + 1)
                        until(pe, e_lk, c - 1)
                        for n in range(2):
                            last = nc.tensor.matmul(ps_l[0:H, n * P:(n + 1) * P], lkt[q][:, n * H:(n + 1) * H], ident[:],
                                                    start=True, stop=True)
                        last.then_inc(e_logits, 1)

                stages(pe, C, LAGE, step, first=3)


        end_phase()

        with ExitStack() as st, nc.Block() as block:
            sidx = [sb(st, f"sidx{b}", [P, 4], i32) for b in range(U)]
            got = [sb(st, f"got{b}", [P, 2]) for b in range(U)]
            is_slot = sb(st, "is_slot", [P, C])
            l_staged, l_copied, l_flag, l_index = sem("l_staged"), sem("l_copied"), sem("l_flag"), sem("l_index")
            l_got = [sem(f"l_got{b}") for b in range(U)]

            @block.gpsimd
            def _(pool):
                def step(i, b):
                    if runs(i, 3, C):
                        c, o = i - 3, (b - 3) % U
                        pool.wait_ge(l_got[o], 16 * (b_count(i, b, 3) + 1))
                        passed(pool)
                        nc.gpsimd.tensor_copy(col(place_src, c), got[o][:, 0:1]).then_inc(l_copied, 1)
                        nc.gpsimd.tensor_copy(col(dis_src, c), got[o][:, 1:2]).then_inc(l_copied, 1)
                    if runs(i, 0, C):
                        after(pool, l_copied, 2 * (i - U + 1))
                        passed(pool)
                        nc.gpsimd.tensor_copy(sidx[b][:], cols(index, i)).then_inc(l_staged, 1)
                        pool.wait_ge(l_staged, i + 1)
                        passed(pool)
                        pool.indirect_dma_start(got[b][:], None, place, bass.IndirectOffsetOnAxis(sidx[b][:, 0:1], 0)
                                                ).then_inc(l_got[b], 16)

                stages(pool, C, 3, step)

            @block.vector
            def _(dve):
                dve.wait_ge(l_copied, 2 * C)
                nc.vector.tensor_copy(index[:, :, 0], place_src[:])
                nc.vector.tensor_scalar(is_slot[:], place_src[:], float(N), float(EP), ALU.is_ge, ALU.mult
                                        ).then_inc(l_flag, 1)
                dve.wait_ge(l_flag, 1)
                nc.vector.tensor_tensor(index[:, :, 1], place_src[:], is_slot[:], ALU.add)
                nc.vector.tensor_tensor(dis2_own[:], dis_own[:], dis_own[:], ALU.mult)

        end_phase()

        for hop in (1, 2):
            if hop == 2:
                end_phase()
            with ExitStack() as st, nc.Block() as block:
                kr = [sb(st, f"hkr{hop}{b}", [P, P + 2]) for b in range(U)]
                sidx = [sb(st, f"hidx{hop}{b}", [P, 4], i32) for b in range(U)]
                far_row = [sb(st, f"far_row{hop}{b}", [P, D]) for b in range(U)]
                own_row = [sb(st, f"own_row{hop}{b}", [P, D]) for b in range(U)]
                same = [sb(st, f"hsame{hop}{b}", [P, P]) for b in range(2)]
                cont = [sb(st, f"hcont{hop}{b}", [P, P]) for b in range(2)]
                msg = [sb(st, f"hmsg{hop}{b}", [P, D + 1]) for b in range(2)]
                own = [sb(st, f"hown{hop}{b}", [P, D]) for b in range(2)]
                acc = [sb(st, f"hacc{hop}{b}", [P, D + 1]) for b in range(2)]
                uu = [sb(st, f"uu{hop}{b}", [P, D]) for b in range(U)]
                ps_a = [pb(st, f"hps_a{hop}{b}") for b in range(2)]
                kr_loaded = [sem(f"h{hop}_kr_loaded{b}") for b in range(U)]
                own_loaded = [sem(f"h{hop}_own_loaded{b}") for b in range(U)]
                far_gathered = [sem(f"h{hop}_far_gathered{b}") for b in range(U)]
                sent = [sem(f"h{hop}_sent{b}") for b in range(U)]
                (h_staged, h_sel, h_msg, h_own, h_sums, h_acc, h_u, h_init) = [
                    sem(f"h{hop}_{n}") for n in "staged sel msg own sums acc u init".split()]
                if hop == 2:
                    x1o = [sb(st, f"x1o{b}", [P, D]) for b in range(U)]
                    ut = [sb(st, f"ut{b}", [P, K, P]) for b in range(2)]
                    a1 = [sb(st, f"a1{b}", [P, 2]) for b in range(U)]
                    z = [sb(st, f"z{b}", [P, D]) for b in range(2)]
                    zn = [sb(st, f"zn{b}", [P, D]) for b in range(2)]
                    zx = [sb(st, f"hzx{b}", [P, D]) for b in range(2)]
                    oidx = [sb(st, f"oidx{b}", [P, 4], i32) for b in range(U)]
                    h_oidx = sem("h2_oidx")
                    oe = [sb(st, f"oe{b}", [P, D]) for b in range(U)]
                    ps_t = pb(st, "hps_t")
                    ps_z = pb(st, "hps_z")
                    x1_loaded = [sem(f"h2_x1_loaded{b}") for b in range(U)]
                    (h_a0, h_a1, h_trans, h_ut, h_prod, h_z, h_zn, h_zx, h_o) = [
                        sem(f"h2_{n}") for n in "a0 a1 trans ut prod z zn zx o".split()]
                first_own = N + (hop - 1) * EP
                LAGH = 8

                @block.sync
                def _(sp):
                    def step(i, b):
                        if runs(i, 0, C):
                            after(sp, h_sel, 2 * (i - U + 1))
                            at = keys[i * P:i * P + P + 2] if isinstance(i, int) else keys[bass.ds(i * P, P + 2)]
                            sp.dma_start(kr[b][:], at.partition_broadcast(P)).then_inc(kr_loaded[b], 16)
                            after(sp, h_own, i - U + 1)
                            sp.dma_start(own_row[b][:], slot_rows(rows, i, first_own)).then_inc(own_loaded[b], 16)
                        if hop == 1 and runs(i, 4, C):
                            c, o = i - 4, (b - 4) % U
                            sp.wait_ge(h_u, c + 1)
                            sp.dma_start(slot_rows(rows, c, N + EP), uu[o][:]).then_inc(sent[o], 16)
                        if hop == 2 and runs(i, 2, C):
                            c, o = i - 2, (b - 2) % U
                            after(sp, h_zx, c - U + 1)
                            sp.dma_start(x1o[o][:], slot_rows(x1_slots, c, 0)).then_inc(x1_loaded[o], 16)

                    stages(sp, C, LAGH, step)
                    for b in range(U):
                        sp.wait_ge(sent[b], 16 * (C // U))

                @block.gpsimd
                def _(pool):
                    def step(i, b):
                        if runs(i, 0, C):
                            after(pool, h_msg, i - U + 1)
                            passed(pool)
                            nc.gpsimd.tensor_copy(sidx[b][:], cols(index, i)).then_inc(h_staged, 1)
                            pool.wait_ge(h_staged, i + 1)
                            passed(pool)
                            pool.indirect_dma_start(far_row[b][:], None, rows[0:N + hop * EP, :],
                                                    bass.IndirectOffsetOnAxis(sidx[b][:, hop - 1:hop], 0)
                                                    ).then_inc(far_gathered[b], 16)
                        if hop == 2 and runs(i, 5, C):
                            c, o = i - 5, (b - 5) % U
                            pool.wait_ge(h_z, c + 1)
                            pool.wait_ge(x1_loaded[o], 16 * (b_count(i, b, 5) + 1))
                            after(pool, h_o, c - 1)
                            nc.gpsimd.tensor_tensor(zx[o % 2][:], z[o % 2][:], x1o[o][:], ALU.add).then_inc(h_zx, 1)
                            pool.wait_ge(h_zn, c + 1)
                            if not isinstance(c, int) or c >= U:
                                pool.wait_ge(sent[o], 16 * b_count(i, b, 5))
                            pool.wait_ge(h_zx, c + 1)
                            nc.gpsimd.tensor_tensor(oe[o][:], zx[o % 2][:], zn[o % 2][:], ALU.add).then_inc(h_o, 1)
                            nc.gpsimd.tensor_copy(oidx[o][:], cols(index, c)).then_inc(h_oidx, 1)
                            pool.wait_ge(h_o, c + 1)
                            pool.wait_ge(h_oidx, c + 1)
                            passed(pool)
                            pool.indirect_dma_start(out, bass.IndirectOffsetOnAxis(oidx[o][:, 2:3], 0), oe[o][:], None,
                                                    bounds_check=N - 1, oob_is_err=False).then_inc(sent[o], 16)

                    stages(pool, C, LAGH, step)

                @block.vector
                def _(dve):
                    nc.vector.memset(acc[1][:], 0.0).then_inc(h_init, 1)

                    def step(i, b):
                        if runs(i, 1, C):
                            c, o = i - 1, (b - 1) % U
                            q = o % 2
                            dve.wait_ge(kr_loaded[o], 16 * (b_count(i, b, 1) + 1))
                            after(dve, h_sums, c - 1)
                            nc.vector.scalar_tensor_tensor(same[q][:], kr[o][:, 1:P + 1], col(key_col, c), tri[:],
                                                           ALU.is_equal, ALU.mult).then_inc(h_sel, 1)
                            nc.vector.tensor_scalar(cont[q][:], kr[o][:, 1:P + 1], kr[o][:, 0:1], last_row[:],
                                                    ALU.is_equal, ALU.mult).then_inc(h_sel, 1)
                            dve.wait_ge(far_gathered[o], 16 * (b_count(i, b, 1) + 1))
                            nc.vector.tensor_scalar(msg[q][:, 0:D], far_row[o][:], 0.0, col(dis_src, c), ALU.max, ALU.mult)
                            nc.vector.tensor_copy(msg[q][:, D:D + 1], col(dis_src, c)).then_inc(h_msg, 1)
                            dve.wait_ge(own_loaded[o], 16 * (b_count(i, b, 1) + 1))
                            after(dve, h_u, c - 1)
                            nc.vector.tensor_scalar(own[q][:], own_row[o][:], 0.0, col(dis2_own, c), ALU.max, ALU.mult
                                                    ).then_inc(h_own, 1)
                        if runs(i, 2, C):
                            c, o = i - 2, (b - 2) % U
                            q = o % 2
                            dve.wait_ge(h_acc, c + 1)
                            dve.wait_ge(h_own, c + 1)
                            if hop == 1:
                                if not isinstance(c, int) or c >= U:
                                    dve.wait_ge(sent[o], 16 * b_count(i, b, 2))
                            else:
                                after(dve, h_trans, c - U + 1)
                            nc.vector.scalar_tensor_tensor(uu[o][:], acc[q][:, 0:D], col(dis_own, c), own[q][:],
                                                           ALU.mult, ALU.add).then_inc(h_u, 1)
                            if hop == 2:
                                after(dve, h_z, c - U + 1)
                                nc.vector.tensor_tensor(a1[o][:, 0:1], acc[q][:, D:D + 1], col(dis_own, c), ALU.add
                                                        ).then_inc(h_a0, 1)
                                dve.wait_ge(h_a0, c + 1)
                                nc.vector.tensor_tensor(a1[o][:, 1:2], a1[o][:, 0:1], col(dis_own, c), ALU.mult
                                                        ).then_inc(h_a1, 1)
                        if hop == 2 and runs(i, 4, C):
                            c, q, o = i - 4, (b - 4) % 2, (b - 4) % U
                            dve.wait_ge(h_prod, c + 1)
                            dve.wait_ge(h_a1, c + 1)
                            after(dve, h_zx, c - 1)
                            nc.vector.scalar_tensor_tensor(z[q][:], b1w2_b[:], a1[o][:, 1:2], ps_z[:, 0:D], ALU.mult,
                                                           ALU.add).then_inc(h_z, 1)
                            dve.wait_ge(h_z, c + 1)
                            after(dve, h_o, c - 1)
                            nc.vector.scalar_tensor_tensor(zn[q][:], z[q][:], 0.0, am1_b[:], ALU.min, ALU.mult
                                                           ).then_inc(h_zn, 1)

                    stages(dve, C, LAGH, step)

                @block.scalar
                def _(act):
                    def step(i, b):
                        if runs(i, 1, C):
                            c, q = i - 1, (b - 1) % 2
                            act.wait_ge(h_sums, c + 1)
                            after(act, h_u, c - 1)
                            if hop == 2:
                                after(act, h_a1, c - 1)
                            nc.scalar.activation(acc[q][:], ps_a[q][:, 0:D + 1], ACT.Copy).then_inc(h_acc, 1)
                        if hop == 2 and runs(i, 3, C):
                            c, q = i - 3, (b - 3) % 2
                            act.wait_ge(h_trans, c + 1)
                            after(act, h_prod, c - 1)
                            nc.scalar.activation(ut[q][:].rearrange("p k n -> p (k n)"), ps_t[:, 0:D], ACT.Copy
                                                 ).then_inc(h_ut, 1)

                    stages(act, C, LAGH, step)

                @block.tensor
                def _(pe):
                    pe.wait_ge(h_init, 1)

                    def step(i, b):
                        if runs(i, 1, C):
                            c, q = i - 1, (b - 1) % 2
                            pe.wait_ge(h_msg, c + 1)
                            after(pe, h_acc, c - 1)
                            nc.tensor.matmul(ps_a[q][:, 0:D + 1], same[q][:], msg[q][:], start=True, stop=False)
                            after(pe, h_acc, c)
                            nc.tensor.matmul(ps_a[q][:, 0:D + 1], cont[q][:], acc[1 - q][:], start=False, stop=True
                                             ).then_inc(h_sums, 1)
                        if hop == 2 and runs(i, 3, C):
                            c, o = i - 3, (b - 3) % U
                            pe.wait_ge(h_u, c + 1)
                            after(pe, h_ut, c)
                            for k in range(K):
                                last = nc.tensor.transpose(ps_t[:, k * P:(k + 1) * P], uu[o][:, k * P:(k + 1) * P],
                                                           ident[:])
                            last.then_inc(h_trans, 1)
                            pe.wait_ge(h_ut, c + 1)
                            after(pe, h_z, c)
                            for k in range(K):
                                nc.tensor.matmul(ps_z[:, 0:D], ut[o % 2][:, k, :], w_12[:, k, :], start=k == 0, stop=False)
                            nc.tensor.matmul(ps_z[:, 0:D], ones3[:], bias_2[:], start=False, stop=True
                                             ).then_inc(h_prod, 1)

                    stages(pe, C, LAGH, step)


_INS = ["x", "src", "dst", "L0_gnn_W", "L0_gnn_a_src", "L0_gnn_a_dst", "L0_gnn_bias_gat", "L0_gnn_W_res", "L0_gnn_b_res",
        "L0_gnn_gamma", "L0_gnn_beta", "L1_gnn_W1", "L1_gnn_b1", "L1_gnn_W2", "L1_gnn_b2", "L1_gnn_prelu_a"]


def kernel(**inputs):
    import numpy as np
    import concourse.bacc as bacc
    from concourse import mybir as _mybir
    from concourse.bass_utils import run_bass_kernel_spmd

    nc = bacc.Bacc("TRN2", target_bir_lowering=False, num_devices=1)
    arrays, args = {}, []
    for name in _INS:
        a = np.ascontiguousarray(inputs[name])
        arrays[f"in_{name}"] = a
        args.append(nc.dram_tensor(f"in_{name}", a.shape, _mybir.dt.from_np(a.dtype), kind="ExternalInput").ap())
    args.append(nc.dram_tensor("out_x", inputs["x"].shape, _mybir.dt.float32, kind="ExternalOutput").ap())
    gat_then_gcn_kernel(nc, *args)
    r = run_bass_kernel_spmd(nc, [arrays], core_ids=[0])
    return r.results[0]["out_x"]
```

```python
import math
from contextlib import ExitStack

import concourse.bass as bass
from concourse import mybir


def gat_then_gcn_kernel(
    nc, x, src, dst, w_gat, a_src, a_dst, bias_gat, w_res, b_res, gamma, beta, w1, b1, w2, b2, prelu_a, out
):
    fp32, bf16, i32 = mybir.dt.float32, mybir.dt.bfloat16, mybir.dt.int32
    ALU, ACT, AX = mybir.AluOpType, mybir.ActivationFunctionType, mybir.AxisListType

    P = 128
    N, D = x.shape
    E = src.shape[0]
    H, HC = a_src.shape
    K = D // P
    EPS, TINY, SLOPE = 1e-5, 1e-16, 0.2
    T = 4
    GROUP = T * P
    G = math.ceil(N / GROUP)
    U = 4
    C = U * math.ceil(E / (U * P))
    EP = C * P
    FAR = float(1 << 23)
    LOW = -1e37
    NH = H * (HC + 1)
    assert D == H * HC and G % U == 0 and G >= 3 * U and C > 3 * U

    rows = nc.dram_tensor("rows", [N + EP, D + 2], fp32, kind="Internal").ap()
    n1_slots = nc.dram_tensor("n1_slots", [EP, D + 2], fp32, kind="Internal").ap()
    x1_slots = nc.dram_tensor("x1_slots", [EP, D], fp32, kind="Internal").ap()
    keys = nc.dram_tensor("keys", [EP + 2], fp32, kind="Internal").ap()
    srcs = nc.dram_tensor("srcs", [EP], fp32, kind="Internal").ap()

    top = ExitStack()

    def sb(stack, name, shape, dt=fp32):
        return stack.enter_context(nc.sbuf_tensor(name, shape, dt))

    def pb(stack, name, shape=(P, 512), dt=fp32):
        return stack.enter_context(nc.psum_tensor(name, list(shape), dt))

    in_use = []

    def sem(name):
        in_use.append(nc.alloc_semaphore(name=name))
        return in_use[-1]

    def end_phase():
        nc.clear_and_free_semaphores(list(in_use))
        in_use.clear()
        nc.all_engine_barrier()

    with top:
        ident = sb(top, "ident", [P, P])
        tri = sb(top, "tri", [P, P])
        last_row = sb(top, "last_row", [P, 1])
        low = sb(top, "low", [H, 1])
        neg_half = sb(top, "neg_half", [P, 2 * T])
        eps = sb(top, "eps", [P, T])
        eps_d = sb(top, "eps_d", [P, T])
        gamma_d = sb(top, "gamma_d", [P, D])
        ones3 = sb(top, "ones3", [3, P], bf16)
        w_all = sb(top, "w_all", [P, K, 2 * D])
        w_sum = sb(top, "w_sum", [P, K, D])
        w_12 = sb(top, "w_12", [P, K, D])
        w_src = sb(top, "w_src", [P, K, D + 2 * H])
        w_att = sb(top, "w_att", [P, K, 2, H])
        gamma_b = sb(top, "gamma_b", [P, D])
        beta_b = sb(top, "beta_b", [P, D])
        am1_b = sb(top, "am1_b", [P, D])
        b1w2_b = sb(top, "b1w2_b", [P, D])
        bias_y = sb(top, "bias_y", [3, D], bf16)
        bias_yc = sb(top, "bias_yc", [3, D], bf16)
        bias_z = sb(top, "bias_z", [3, D], bf16)
        bias_2 = sb(top, "bias_2", [3, D], bf16)
        key_col = sb(top, "key_col", [P, C])
        index = sb(top, "index", [P, C, 4], i32)
        neg_last = sb(top, "neg_last", [P, 1])
        cont_bias = sb(top, "cont_bias", [P, C])
        src_col = sb(top, "src_col", [P, C])
        edges = sb(top, "edges", [P, C, 2])
        tag = sb(top, "tag", [P, C, 2])
        dis2_own = sb(top, "dis2_own", [P, C])
        src_behind = sb(top, "src_behind", [P, C])

        with ExitStack() as st, nc.Block() as block:
            w1_in = sb(st, "w1_in", [P, K, D])
            w2_in = sb(st, "w2_in", [P, K, D])
            w1_t = sb(st, "w1_t", [P, K, D])
            as_b = sb(st, "as_b", [P, D])
            ad_b = sb(st, "ad_b", [P, D])
            bg_b = sb(st, "bg_b", [P, D])
            br_b = sb(st, "br_b", [P, D])
            a_b = sb(st, "a_b", [P, D])
            b2_b = sb(st, "b2_b", [P, D])
            b1_col = sb(st, "b1_col", [P, K])
            b1_rep = sb(st, "b1_rep", [P, K, P])
            mean_w = sb(st, "mean_w", [P, K + 1])
            prod = sb(st, "prod", [P, D])
            part = sb(st, "part", [P, 3, D], bf16)
            rest = sb(st, "rest", [P, D])
            pick = sb(st, "pick", [P, D])
            cz_b = sb(st, "cz_b", [P, D])
            by_b = sb(st, "by_b", [P, D])
            byc_b = sb(st, "byc_b", [P, D])
            EPART = max(q for q in range(1, P + 1) if E % q == 0)
            key_i = sb(st, "key_i", [EPART, E // EPART], i32)
            src_i = sb(st, "src_i", [EPART, E // EPART], i32)
            key_f = sb(st, "key_f", [EPART, E // EPART])
            src_f = sb(st, "src_f", [EPART, E // EPART])
            edge_val = sb(st, "edge_val", [1, 2 + EP - E + 1])
            far_zero = sb(st, "far_zero", [1, max(1, EP - E)])
            slot_i = sb(st, "slot_i", [P, C], i32)
            slot_row = sb(st, "slot_row", [P, C])
            CR = math.ceil(C / P)
            by_chunk = sb(st, "by_chunk", [P, 4, CR, P])
            next_col = sb(st, "next_col", [P, C])
            prev_col = sb(st, "prev_col", [P, C])
            first = sb(st, "first", [P, C])
            far = sb(st, "far", [P, C])
            ps_w = pb(st, "ps_w")
            ps_b = pb(st, "ps_b")
            ps_t = pb(st, "ps_t", (P, 512))

            weights_in = sem("weights_in")
            vectors_in = sem("vectors_in")
            edges_in = sem("edges_in")
            edges_f = sem("edges_f")
            edge_consts = sem("edge_consts")
            keys_out = sem("keys_out")
            chunks_in = sem("chunks_in")
            slots_ready = sem("slots_ready")
            consts_ready = sem("consts_ready")
            pool_step = sem("pool_step")
            dve_step = sem("dve_step")
            w1t_ready = sem("w1t_ready")
            w1t_copied = sem("w1t_copied")
            w12_ready = sem("w12_ready")
            b1rep_ready = sem("b1rep_ready")
            b1w2_ready = sem("b1w2_ready")
            trans_ready = sem("trans_ready")
            trans_copied = sem("trans_copied")

            def row_of(v):
                return v.partition_broadcast(P)

            @block.sync
            def _(sp):
                sp.dma_start(src_i[:], src.rearrange("(p n) -> p n", p=EPART)).then_inc(edges_in, 16)
                sp.dma_start(key_i[:], dst.rearrange("(p n) -> p n", p=EPART)).then_inc(edges_in, 16)
                for to, of in ((w_all[:, :, 0:D], w_gat), (w_all[:, :, D:2 * D], w_res), (w1_in[:], w1), (w2_in[:], w2)):
                    sp.dma_start(to, of.rearrange("(k p) d -> p k d", p=P)).then_inc(weights_in, 16)
                for to, of in ((as_b, a_src.rearrange("h c -> (h c)")), (ad_b, a_dst.rearrange("h c -> (h c)")),
                               (bg_b, bias_gat), (br_b, b_res), (gamma_b, gamma), (beta_b, beta), (a_b, prelu_a),
                               (b2_b, b2)):
                    sp.dma_start(to[:], row_of(of)).then_inc(vectors_in, 16)
                for k in range(K):
                    sp.dma_start(b1_col[:, k:k + 1], b1[k * P:(k + 1) * P].rearrange("(p o) -> p o", o=1)).then_inc(vectors_in, 16)
                sp.wait_ge(edge_consts, 1)
                sp.wait_ge(edges_f, 2)
                sp.dma_start(keys[0:1].rearrange("(o n) -> o n", o=1), edge_val[:, 0:1]).then_inc(keys_out, 16)
                sp.dma_start(keys[1 + E:EP + 2].rearrange("(o n) -> o n", o=1), edge_val[:, 2:3 + EP - E]).then_inc(keys_out, 16)
                sp.dma_start(keys[1:1 + E].rearrange("(p n) -> p n", p=EPART), key_f[:]).then_inc(keys_out, 16)
                sp.dma_start(srcs[0:E].rearrange("(p n) -> p n", p=EPART), src_f[:]).then_inc(keys_out, 16)
                sp.dma_start(srcs[E:EP].rearrange("(o n) -> o n", o=1), far_zero[:, 0:EP - E]).then_inc(keys_out, 16)
                sp.wait_ge(keys_out, 5 * 16)
                for n, row in enumerate((keys[1:1 + EP], keys[2:2 + EP], srcs, keys[0:EP])):
                    for r in range(CR):
                        m = min(P, C - r * P)
                        sp.dma_start(by_chunk[0:m, n, r, :],
                                     row[r * P * P:(r * P + m) * P].rearrange("(c p) -> c p", p=P)).then_inc(chunks_in, 16)

            @block.gpsimd
            def _(pool):
                steps = [0]

                def done(ins):
                    steps[0] += 1
                    ins.then_inc(pool_step, 1)
                    pool.wait_ge(pool_step, steps[0])

                nc.gpsimd.memset(edge_val[:], FAR)
                done(nc.gpsimd.memset(far_zero[:], 0.0))
                nc.gpsimd.memset(edge_val[:, 0:1], -1.0).then_inc(edge_consts, 1)
                nc.gpsimd.memset(ident[:], 0.0)
                nc.gpsimd.memset(tri[:], 1.0)
                nc.gpsimd.memset(low[:], LOW)
                nc.gpsimd.memset(neg_half[:], -0.5)
                nc.gpsimd.memset(eps[:], EPS)
                nc.gpsimd.memset(eps_d[:], EPS * D)
                nc.gpsimd.memset(ones3[:], 1.0)
                nc.gpsimd.memset(index[:, :, 3], 0)
                done(nc.gpsimd.memset(last_row[:], 1.0))
                nc.gpsimd.affine_select(out=ident[:], in_=ident[:], compare_op=ALU.not_equal, fill=1.0,
                                        base=0, pattern=[[-1, P]], channel_multiplier=1)
                nc.gpsimd.affine_select(out=tri[:], in_=tri[:], compare_op=ALU.is_ge, fill=0.0,
                                        base=0, pattern=[[1, P]], channel_multiplier=-1)
                nc.gpsimd.affine_select(out=last_row[:], in_=last_row[:], compare_op=ALU.is_ge, fill=0.0,
                                        base=1 - P, pattern=[[1, 1]], channel_multiplier=1).then_inc(consts_ready, 1)
                done(nc.gpsimd.iota(slot_i[:], pattern=[[P, C]], base=N, channel_multiplier=1))
                nc.gpsimd.tensor_copy(slot_row[:], slot_i[:]).then_inc(slots_ready, 1)

            @block.vector
            def _(dve):
                steps = [0]

                def done(ins):
                    steps[0] += 1
                    ins.then_inc(dve_step, 1)
                    dve.wait_ge(dve_step, steps[0])

                dve.wait_ge(edges_in, 32)
                nc.vector.tensor_copy(key_f[:], key_i[:]).then_inc(edges_f, 1)
                nc.vector.tensor_copy(src_f[:], src_i[:]).then_inc(edges_f, 1)
                dve.wait_ge(weights_in, 4 * 16)
                dve.wait_ge(vectors_in, (8 + K) * 16)
                dve.wait_ge(consts_ready, 1)
                for k in range(K):
                    done(nc.vector.tensor_tensor(w_sum[:, k, :], w_all[:, k, 0:D], w_all[:, k, D:2 * D], ALU.add))
                    done(nc.vector.reduce_sum(mean_w[:, k:k + 1], w_sum[:, k, :], axis=AX.X))
                    done(nc.vector.tensor_scalar(mean_w[:, k:k + 1], mean_w[:, k:k + 1], 1.0 / D, None, ALU.mult))
                    done(nc.vector.tensor_scalar(w_sum[:, k, :], w_sum[:, k, :], mean_w[:, k:k + 1], None, ALU.subtract))
                for k in range(K):
                    nc.vector.tensor_copy(w_src[:, k, 0:D], w_all[:, k, 0:D])
                    nc.vector.memset(w_src[:, k, D + H:], 0.0)
                    for a, to in ((as_b, w_src[:, k, D:D + H]), (ad_b, w_att[:, k, 0, :])):
                        done(nc.vector.tensor_tensor(prod[:], w_all[:, k, 0:D], a[:], ALU.mult))
                        done(nc.vector.reduce_sum(to, prod[:].rearrange("p (h c) -> p h c", h=H), axis=AX.X))
                    done(nc.vector.tensor_tensor(w_att[:, k, 1, :], w_src[:, k, D:D + H], w_att[:, k, 0, :], ALU.add))
                nc.vector.tensor_scalar(gamma_d[:], gamma_b[:], math.sqrt(D), None, ALU.mult)
                nc.vector.tensor_scalar(am1_b[:], a_b[:], -1.0, None, ALU.add)
                for k in range(K):
                    last = nc.vector.tensor_scalar(b1_rep[:, k, :], tri[:], 0.0, b1_col[:, k:k + 1], ALU.mult, ALU.add)
                last.then_inc(b1rep_ready, 1)
                dve.wait_ge(w1t_ready, 1)
                nc.vector.tensor_copy(w1_t[:].rearrange("p k d -> p (k d)"), ps_w[:]).then_inc(w1t_copied, 1)
                done(nc.vector.tensor_tensor(by_b[:], bg_b[:], br_b[:], ALU.add))
                done(nc.vector.reduce_sum(mean_w[:, K:K + 1], by_b[:], axis=AX.X))
                done(nc.vector.tensor_scalar(mean_w[:, K:K + 1], mean_w[:, K:K + 1], 1.0 / D, None, ALU.mult))
                done(nc.vector.tensor_scalar(byc_b[:], by_b[:], mean_w[:, K:K + 1], None, ALU.subtract))
                for to, of in ((bias_y, by_b), (bias_yc, byc_b), (bias_2, b2_b), (bias_z, cz_b)):
                    if to is bias_z:
                        dve.wait_ge(w12_ready, 1)
                        nc.vector.tensor_copy(w_12[:].rearrange("p k d -> p (k d)"), ps_w[:])
                        dve.wait_ge(b1w2_ready, 1)
                        done(nc.vector.tensor_copy(b1w2_b[:], ps_b[:, 0:D]))
                        done(nc.vector.tensor_tensor(cz_b[:], b1w2_b[:], b2_b[:], ALU.add))
                    done(nc.vector.tensor_copy(part[:, 0, :], of[:]))
                    done(nc.vector.tensor_tensor(rest[:], of[:], part[:, 0, :], ALU.subtract))
                    done(nc.vector.tensor_copy(part[:, 1, :], rest[:]))
                    done(nc.vector.tensor_tensor(rest[:], rest[:], part[:, 1, :], ALU.subtract))
                    done(nc.vector.tensor_copy(part[:, 2, :], rest[:]))
                    done(nc.vector.tensor_scalar(pick[:], part[:, 0, :], ident[:, 0:1], None, ALU.mult))
                    done(nc.vector.scalar_tensor_tensor(pick[:], part[:, 1, :], ident[:, 1:2], pick[:], ALU.mult, ALU.add))
                    done(nc.vector.scalar_tensor_tensor(to[:], part[0:3, 2, :], ident[0:3, 2:3], pick[0:3, :], ALU.mult, ALU.add))
                n = 0
                for cols in (key_col, next_col, src_col, prev_col):
                    for r in range(CR):
                        m = min(P, C - r * P)
                        n += 1
                        dve.wait_ge(trans_ready, n)
                        nc.vector.tensor_copy(cols[:, r * P:r * P + m], ps_t[:, 0:m]).then_inc(trans_copied, 1)
                dve.wait_ge(trans_copied, n)
                nc.vector.tensor_scalar(neg_last[:], last_row[:], -1.0, None, ALU.mult)
                nc.vector.memset(cont_bias[:, 0:1], 0.0)
                nc.vector.tensor_scalar(cont_bias[:, 1:C], key_col[:, 0:C - 1], 1.0, last_row[:], ALU.add, ALU.mult)
                nc.vector.tensor_copy(index[:, :, 0], src_col[:])
                dve.wait_ge(slots_ready, 1)
                nc.vector.tensor_tensor(tag[:, :, 1], slot_row[:], key_col[:], ALU.subtract)
                nc.vector.tensor_scalar(index[:, :, 1], key_col[:], float(N - 1), None, ALU.min)
                nc.vector.tensor_tensor(first[:], key_col[:], prev_col[:], ALU.is_equal)
                done(nc.vector.tensor_tensor(far[:], key_col[:], next_col[:], ALU.is_equal))
                nc.vector.tensor_scalar(edges[:, :, 0], first[:], -1.0, -LOW, ALU.add, ALU.mult)
                nc.vector.tensor_scalar(edges[:, :, 1], far[:], -1.0, -LOW, ALU.add, ALU.mult)
                done(nc.vector.scalar_tensor_tensor(index[:, :, 2], far[:], FAR, key_col[:], ALU.mult, ALU.add))

            @block.tensor
            def _(pe):
                pe.wait_ge(weights_in, 4 * 16)
                pe.wait_ge(consts_ready, 1)
                for k in range(K):
                    for i in range(K):
                        last = nc.tensor.transpose(ps_w[:, k * D + i * P:k * D + (i + 1) * P],
                                                   w1_in[:, i, k * P:(k + 1) * P], ident[:])
                last.then_inc(w1t_ready, 1)
                pe.wait_ge(b1rep_ready, 1)
                for k in range(K):
                    last = nc.tensor.matmul(ps_b[:, 0:D], b1_rep[:, k, :], w2_in[:, k, :], start=k == 0, stop=k == K - 1)
                last.then_inc(b1w2_ready, 1)
                pe.wait_ge(w1t_copied, 1)
                for i in range(K):
                    for k in range(K):
                        last = nc.tensor.matmul(ps_w[:, i * D:(i + 1) * D], w1_t[:, k, i * P:(i + 1) * P], w2_in[:, k, :],
                                                start=k == 0, stop=k == K - 1)
                last.then_inc(w12_ready, 1)
                pe.wait_ge(chunks_in, 4 * CR * 16)
                n = 0
                for v in range(4):
                    for r in range(CR):
                        m = min(P, C - r * P)
                        if n:
                            pe.wait_ge(trans_copied, n)
                        n += 1
                        nc.tensor.transpose(ps_t[:, 0:m], by_chunk[0:m, v, r, :], ident[0:m, 0:m]).then_inc(trans_ready, 1)


        end_phase()

        turn = [None]

        def stages(eng, count, lag, body, tail=0, first=2):
            for i in range(first * U):
                body(i, i % U)
            if count // U - tail > first:
                with eng.Fori(first, count // U - tail) as j:
                    turn[0] = j
                    for b in range(U):
                        body(j * U + b, b)
            for i in range(max(first, count // U - tail) * U, count + lag):
                body(i, i % U)

        def b_count(i, b, lag):
            if isinstance(i, int):
                return (i - lag) // U
            return turn[0] + (b - lag) // U

        def half_count(i, b, lag):
            if isinstance(i, int):
                return (i - lag) // 2
            return turn[0] * (U // 2) + (b - lag) // 2

        pool_passed, act_passed = nc.alloc_semaphore(name="pool_passed"), nc.alloc_semaphore(name="act_passed")

        def passed(eng):
            eng.sem_inc(act_passed if eng is nc.scalar else pool_passed, 1)

        def slot_rows(table, c, first):
            return table[bass.ds(c * P + first, P), :] if not isinstance(c, int) else \
                table[first + c * P:first + (c + 1) * P, :]

        def col(table, c):
            return table[:, c:c + 1] if isinstance(c, int) else table[:, bass.ds(c, 1)]

        def tag_col(c, n):
            flat = tag[:].rearrange("p c n -> p (c n)")
            at, wide = (2 * c, 2) if n is None else (2 * c + n, 1)
            return flat[:, at:at + wide] if isinstance(c, int) else flat[:, bass.ds(at, wide)]

        def cols(table, c):
            flat = table[:].rearrange("p c n -> p (c n)")
            return flat[:, 4 * c:4 * c + 4] if isinstance(c, int) else flat[:, bass.ds(c * 4, 4)]

        def runs(i, lag, count):
            return not isinstance(i, int) or 0 <= i - lag < count

        def after(eng, semaphore, value):
            if not isinstance(value, int) or value > 0:
                eng.wait_ge(semaphore, value)

        with ExitStack() as st, nc.Block() as block:
            HT = T // 2
            xg = [sb(st, f"xg{b}", [P, T, D]) for b in range(U)]
            xb = [sb(st, f"xb{b}", [P, T, D]) for b in range(U)]
            x1 = [sb(st, f"x1{b}", [P, T, D]) for b in range(U)]
            n1 = [sb(st, f"n1{b}", [P, T, D + 2]) for b in range(U)]
            n0 = [sb(st, f"n0{b}", [P, T, D]) for b in range(2)]
            h0t = [sb(st, f"h0t{b}", [P, T, K, P]) for b in range(2)]
            h1t = [sb(st, f"h1t{b}", [P, T, K, P]) for b in range(2)]
            yn = sb(st, "yn", [P, T, D])
            zg = [sb(st, f"zg{b}", [P, T, D]) for b in range(2)]
            zx = [sb(st, f"zx{b}", [P, T, D]) for b in range(2)]
            zm = [sb(st, f"zm{b}", [P, T, D]) for b in range(2)]
            og = [sb(st, f"og{b}", [P, T, D]) for b in range(2)]
            junk = sb(st, "junk", [P, T, D])
            bs0 = sb(st, "bs0", [P, T, 6])
            bs1 = sb(st, "bs1", [P, T, 6])
            mv0 = [sb(st, f"mv0{b}", [P, T, 2]) for b in range(2)]
            mv1 = [sb(st, f"mv1{b}", [P, T, 2]) for b in range(2)]
            ssq = [sb(st, f"ssq{b}", [P, T]) for b in range(2)]
            ve = sb(st, "ve", [P, 3, T])
            held = sb(st, "held", [P, 2])
            r0 = [sb(st, f"r0{b}", [P, T]) for b in range(2)]
            ry = [sb(st, f"ry{b}", [P, T]) for b in range(2)]
            r1 = [sb(st, f"r1{b}", [P, T]) for b in range(2)]
            nb0 = [sb(st, f"nb0{b}", [P, T]) for b in range(2)]
            nb1 = [sb(st, f"nb1{b}", [P, T]) for b in range(2)]
            ps_t0 = [pb(st, f"ps_t0{h}") for h in range(2)]
            ps_y = [pb(st, f"ps_y{h}") for h in range(2)]
            ps_t1 = [pb(st, f"ps_t1{h}") for h in range(2)]
            ps_z = [pb(st, f"ps_z{h}") for h in range(2)]

            x_loaded = [sem(f"x_loaded{b}") for b in range(U)]
            rows_stored = [sem(f"rows_stored{b}") for b in range(U)]
            out_stored = [sem(f"out_stored{b}") for b in range(2)]
            x_stats, x1_stats = sem("x_stats"), sem("x1_stats")
            x_moments, x1_moments = sem("x_moments"), sem("x1_moments")
            ve_ready = sem("ve_ready")
            r0_ready, ry_ready, r1_ready = sem("r0_ready"), sem("ry_ready"), sem("r1_ready")
            nb0_ready, nb1_ready = sem("nb0_ready"), sem("nb1_ready")
            xb_pool, xb_dve = sem("xb_pool"), sem("xb_dve")
            n0_ready = sem("n0_ready")
            n1_dve, n1_act = sem("n1_dve"), sem("n1_act")
            t0_ready, t1_ready = sem("t0_ready"), sem("t1_ready")
            h0t_ready, h1t_ready = sem("h0t_ready"), sem("h1t_ready")
            y_ready, z_ready = sem("y_ready"), sem("z_ready")
            ssq_ready, yn_ready, zg_ready = sem("ssq_ready"), sem("yn_ready"), sem("zg_ready")
            x1_ready, zm_ready, zx_ready, og_ready = sem("x1_ready"), sem("zm_ready"), sem("zx_ready"), sem("og_ready")
            LAG = 8

            def group_rows(table, g):
                if isinstance(g, int):
                    at = min(g * GROUP, N - GROUP)
                    part = table[at:at + GROUP, :]
                else:
                    part = table[bass.ds(g * GROUP, GROUP), :]
                return part.rearrange("(p t) d -> p t d", t=T)

            @block.sync
            def _(sp):
                def step(i, b):
                    if runs(i, 0, G):
                        after(sp, n0_ready, i - U + 1)
                        after(sp, xb_pool, i - U + 1)
                        after(sp, xb_dve, i - U + 1)
                        sp.dma_start(xg[b][:], group_rows(x, i)).then_inc(x_loaded[b], 16)
                    if runs(i, 5, G):
                        g, c = i - 5, (b - 5) % U
                        if isinstance(g, int) and g == G - 1:
                            sp.wait_ge(rows_stored[(g - 1) % U], 16 * ((g - 1) // U + 1))
                        sp.wait_ge(n1_dve, g + 1)
                        sp.wait_ge(n1_act, g + 1)
                        sp.dma_start(group_rows(rows[0:N, :], g), n1[c][:]).then_inc(rows_stored[c], 16)
                    if runs(i, 8, G):
                        g = i - 8
                        if isinstance(g, int) and g == G - 1:
                            sp.wait_ge(out_stored[(g - 1) % 2], 16 * ((g - 1) // 2 + 1))
                        sp.wait_ge(og_ready, g + 1)
                        sp.dma_start(group_rows(out, g), og[b % 2][:]).then_inc(out_stored[b % 2], 16)

                stages(sp, G, LAG, step, tail=1, first=3)
                for b in range(U):
                    sp.wait_ge(rows_stored[b], 16 * (G // U))
                for b in range(2):
                    sp.wait_ge(out_stored[b], 16 * (G // 2))

            @block.vector
            def _(dve):
                for b in range(U):
                    nc.vector.memset(n1[b][:, :, D:D + 1], 1.0)
                    nc.vector.memset(n1[b][:, :, D + 1:D + 2], 0.0)

                def step(i, b):
                    if runs(i, 4, G):
                        g, c = i - 4, (b - 4) % U
                        dve.wait_ge(r1_ready, g + 1)
                        after(dve, n1_act, g - 1)
                        nc.vector.scalar_tensor_tensor(nb1[c % 2][:], mv1[c % 2][:, :, 0], -1.0, r1[c % 2][:],
                                                       ALU.mult, ALU.mult).then_inc(nb1_ready, 1)
                        if not isinstance(g, int) or g >= U:
                            dve.wait_ge(rows_stored[c], b_count(i, b, 4) * 16)
                        after(dve, t1_ready, 2 * (g - U + 1))
                        for t in range(HT):
                            last = nc.vector.tensor_scalar(n1[c][:, t, 0:D], x1[c][:, t, :], mv1[c % 2][:, t, 0:1],
                                                           r1[c % 2][:, t:t + 1], ALU.subtract, ALU.mult)
                        last.then_inc(n1_dve, 1)
                    if runs(i, 6, G):
                        g, c = i - 6, (b - 6) % U
                        dve.wait_ge(zg_ready, 2 * g + 2)
                        after(dve, og_ready, g - 1)
                        nc.vector.scalar_tensor_tensor(zm[c % 2][:], zg[c % 2][:], 0.0,
                                                       am1_b[:].unsqueeze(1).broadcast_to([P, T, D]),
                                                       ALU.min, ALU.mult).then_inc(zm_ready, 1)
                    if runs(i, 3, G):
                        g, c = i - 3, (b - 3) % U
                        dve.wait_ge(ry_ready, g + 1)
                        dve.wait_ge(y_ready, 2 * g + 2)
                        after(dve, x1_ready, g)
                        for h in range(2):
                            for t in range(HT):
                                last = nc.vector.scalar_tensor_tensor(
                                    yn[:, h * HT + t, :], ps_y[h][:, t * D:(t + 1) * D],
                                    ry[c % 2][:, h * HT + t:h * HT + t + 1], gamma_d[:], ALU.mult, ALU.mult)
                            last.then_inc(yn_ready, 1)
                        dve.wait_ge(yn_ready, 2 * g + 2)
                        dve.wait_ge(xb_pool, g + 1)
                        dve.wait_ge(xb_dve, g + 1)
                        after(dve, zx_ready, g - U + 1)
                        after(dve, n1_dve, g - U + 1)
                        after(dve, n1_act, g - U + 1)
                        nc.vector.tensor_tensor(x1[c][:], yn[:], xb[c][:], ALU.add).then_inc(x1_ready, 1)
                    if runs(i, 1, G):
                        g, c = i - 1, (b - 1) % U
                        dve.wait_ge(r0_ready, g + 1)
                        after(dve, n0_ready, g - 1)
                        nc.vector.scalar_tensor_tensor(nb0[c % 2][:], mv0[c % 2][:, :, 0], -1.0, r0[c % 2][:],
                                                       ALU.mult, ALU.mult).then_inc(nb0_ready, 1)
                    if runs(i, 3, G):
                        g, c = i - 3, (b - 3) % U
                        dve.wait_ge(x1_ready, g + 1)
                        after(dve, x1_moments, g)
                        for t in range(T):
                            nc.vector.bn_stats(bs1[:, t, :], x1[c][:, t, :]).then_inc(x1_stats, 1)
                        dve.wait_ge(x1_stats, (g + 1) * T)
                        after(dve, nb1_ready, g - 1)
                        after(dve, n1_dve, g - 1)
                        nc.vector.memset(held[:, 0:1], 0.0)
                        for t in range(T):
                            last = nc.vector.bn_aggr(mv1[c % 2][:, t, :], bs1[:, t, :])
                        last.then_inc(x1_moments, 1)
                    if runs(i, 0, G):
                        dve.wait_ge(x_loaded[b], (b_count(i, b, 0) + 1) * 16)
                        after(dve, x1_ready, i - U + 1)
                        nc.vector.tensor_tensor(xb[b][:, HT:T, :], xg[b][:, HT:T, :],
                                                beta_b[:].unsqueeze(1).broadcast_to([P, HT, D]), ALU.add
                                                ).then_inc(xb_dve, 1)
                    if runs(i, 0, G):
                        after(dve, x_moments, i)
                        for t in range(T):
                            nc.vector.bn_stats(bs0[:, t, :], xg[b][:, t, :]).then_inc(x_stats, 1)
                        dve.wait_ge(x_stats, (i + 1) * T)
                        after(dve, nb0_ready, i - 1)
                        nc.vector.memset(held[:, 1:2], 0.0)
                        for t in range(T):
                            last = nc.vector.bn_aggr(mv0[b % 2][:, t, :], bs0[:, t, :])
                        last.then_inc(x_moments, 1)

                stages(dve, G, LAG, step, first=3)

            @block.gpsimd
            def _(pool):
                def ve_count(i, n):
                    if isinstance(i, int):
                        before = sum(min(max(i - lag, 0), G) for lag in (3, 1, 3))
                        return before + sum(0 <= i - lag < G for lag in (3, 1, 3)[:n + 1])
                    return (i - 3) + (i - 1) + (i - 3) + n + 1

                def inv_sd(to, var, i, n, s, add):
                    nc.gpsimd.tensor_tensor(ve[:, n, :], var, add[:, 0:T], ALU.add).then_inc(ve_ready, 1)
                    pool.wait_ge(ve_ready, ve_count(i, n))
                    nc.gpsimd.tensor_tensor(to, ve[:, n, :], neg_half[:, 0:T], ALU.pow).then_inc(s, 1)

                def step(i, b):
                    if runs(i, 3, G):
                        g, c = i - 3, (b - 3) % U
                        pool.wait_ge(ssq_ready, 2 * g + 2)
                        after(pool, yn_ready, 2 * (g - 1))
                        after(pool, ry_ready, g)
                        inv_sd(ry[c % 2][:], ssq[c % 2][:], i, 0, ry_ready, eps_d)
                    if runs(i, 6, G):
                        g, c = i - 6, (b - 6) % U
                        pool.wait_ge(zg_ready, 2 * g + 2)
                        after(pool, og_ready, g - 1)
                        nc.gpsimd.tensor_tensor(zx[c % 2][:], zg[c % 2][:], x1[c][:], ALU.add).then_inc(zx_ready, 1)
                    if runs(i, 1, G):
                        g, c = i - 1, (b - 1) % U
                        pool.wait_ge(x_moments, g + 1)
                        after(pool, n0_ready, g - 1)
                        after(pool, r0_ready, g)
                        inv_sd(r0[c % 2][:], mv0[c % 2][:, :, 1], i, 1, r0_ready, eps)
                    if runs(i, 7, G):
                        g, c = i - 7, (b - 7) % U
                        pool.wait_ge(zm_ready, g + 1)
                        if not isinstance(g, int) or g >= 2:
                            pool.wait_ge(out_stored[c % 2], half_count(i, b, 7) * 16)
                        pool.wait_ge(zx_ready, g + 1)
                        nc.gpsimd.tensor_tensor(og[c % 2][:], zx[c % 2][:], zm[c % 2][:], ALU.add).then_inc(og_ready, 1)
                    if runs(i, 0, G):
                        pool.wait_ge(x_loaded[b], (b_count(i, b, 0) + 1) * 16)
                        after(pool, x1_ready, i - U + 1)
                        nc.gpsimd.tensor_tensor(xb[b][:, 0:HT, :], xg[b][:, 0:HT, :],
                                                beta_b[:].unsqueeze(1).broadcast_to([P, HT, D]), ALU.add
                                                ).then_inc(xb_pool, 1)
                    if runs(i, 3, G):
                        g, c = i - 3, (b - 3) % U
                        pool.wait_ge(x1_moments, g + 1)
                        after(pool, n1_dve, g - 1)
                        after(pool, n1_act, g - 1)
                        after(pool, r1_ready, g)
                        inv_sd(r1[c % 2][:], mv1[c % 2][:, :, 1], i, 2, r1_ready, eps)

                stages(pool, G, LAG, step, first=3)

            @block.scalar
            def _(act):
                def step(i, b):
                    if runs(i, 4, G):
                        g, c = i - 4, (b - 4) % U
                        act.wait_ge(nb1_ready, g + 1)
                        if not isinstance(g, int) or g >= U:
                            act.wait_ge(rows_stored[c], b_count(i, b, 4) * 16)
                        after(act, t1_ready, 2 * (g - U + 1))
                        for t in range(HT, T):
                            last = nc.scalar.activation(n1[c][:, t, 0:D], x1[c][:, t, :], ACT.Relu,
                                                        bias=nb1[c % 2][:, t:t + 1], scale=r1[c % 2][:, t:t + 1])
                        last.then_inc(n1_act, 1)
                    if runs(i, 2, G):
                        g, c = i - 2, (b - 2) % U
                        for h in range(2):
                            act.wait_ge(t0_ready, 2 * g + h + 1)
                            after(act, y_ready, 2 * (g - 2) + h + 1)
                            nc.scalar.activation(h0t[c % 2][:, h * HT:(h + 1) * HT, :, :].rearrange("p t k n -> p (t k n)"),
                                                 ps_t0[h][:], ACT.Copy).then_inc(h0t_ready, 1)
                    for h in range(2):
                        if runs(i, 5, G):
                            g, c = i - 5, (b - 5) % U
                            act.wait_ge(z_ready, 2 * g + h + 1)
                            after(act, zm_ready, g - 1)
                            after(act, zx_ready, g - 1)
                            nc.scalar.activation(zg[c % 2][:, h * HT:(h + 1) * HT, :].rearrange("p t d -> p (t d)"),
                                                 ps_z[h][:], ACT.Copy).then_inc(zg_ready, 1)
                    if runs(i, 4, G):
                        g, c = i - 4, (b - 4) % U
                        for h in range(2):
                            act.wait_ge(t1_ready, 2 * g + h + 1)
                            after(act, z_ready, 2 * (g - 2) + h + 1)
                            nc.scalar.activation(h1t[c % 2][:, h * HT:(h + 1) * HT, :, :].rearrange("p t k n -> p (t k n)"),
                                                 ps_t1[h][:], ACT.Relu).then_inc(h1t_ready, 1)
                    if runs(i, 1, G):
                        g, c = i - 1, (b - 1) % U
                        act.wait_ge(nb0_ready, g + 1)
                        after(act, t0_ready, 2 * (g - 1))
                        for t in range(T):
                            last = nc.scalar.activation(n0[c % 2][:, t, :], xg[c][:, t, :], ACT.Relu,
                                                        bias=nb0[c % 2][:, t:t + 1], scale=r0[c % 2][:, t:t + 1])
                        last.then_inc(n0_ready, 1)
                    if runs(i, 2, G):
                        g, c = i - 2, (b - 2) % U
                        for h in range(2):
                            act.wait_ge(y_ready, 2 * g + h + 1)
                            after(act, ry_ready, g - 1)
                            after(act, ssq_ready, 2 * g)
                            for t in range(h * HT, (h + 1) * HT):
                                last = nc.scalar.activation(junk[:, t, :], ps_y[h][:, (t - h * HT) * D:(t - h * HT + 1) * D],
                                                            ACT.Square, accum_out=ssq[c % 2][:, t:t + 1])
                            last.then_inc(ssq_ready, 1)

                stages(act, G, LAG, step, first=3)

            @block.tensor
            def _(pe):
                def products(i, g, c, of, ready, to, used, w, bias, done):
                    for h in range(2):
                        pe.wait_ge(ready, 2 * g + h + 1)
                        after(pe, used, 2 * (g - 1) + h + 1)
                        for t in range(HT):
                            o = to[h][:, t * D:(t + 1) * D]
                            for k in range(K):
                                nc.tensor.matmul(o, of[c % 2][:, h * HT + t, k, :], w[:, k, :], start=k == 0, stop=False)
                            last = nc.tensor.matmul(o, ones3[:], bias[:], start=False, stop=True)
                        last.then_inc(done, 1)

                def transposes(g, h, of, to, copied, done):
                    after(pe, copied, 2 * (g - 1) + h + 1)
                    for t in range(HT):
                        for k in range(K):
                            last = nc.tensor.transpose(to[h][:, (t * K + k) * P:(t * K + k + 1) * P],
                                                       of[:, h * HT + t, k * P:(k + 1) * P], ident[:])
                    last.then_inc(done, 1)

                def step(i, b):
                    if runs(i, 5, G):
                        products(i, i - 5, b - 5, h1t, h1t_ready, ps_z, zg_ready, w_12, bias_z, z_ready)
                    if runs(i, 4, G):
                        g, c = i - 4, (b - 4) % U
                        pe.wait_ge(n1_dve, g + 1)
                        transposes(g, 0, n1[c], ps_t1, h1t_ready, t1_ready)
                        pe.wait_ge(n1_act, g + 1)
                        transposes(g, 1, n1[c], ps_t1, h1t_ready, t1_ready)
                    if runs(i, 2, G):
                        products(i, i - 2, b - 2, h0t, h0t_ready, ps_y, yn_ready, w_sum, bias_yc, y_ready)
                    if runs(i, 1, G):
                        g, c = i - 1, (b - 1) % U
                        pe.wait_ge(n0_ready, g + 1)
                        for h in range(2):
                            transposes(g, h, n0[c % 2], ps_t0, h0t_ready, t0_ready)

                stages(pe, G, LAG, step, first=3)


        end_phase()

        with ExitStack() as st, nc.Block() as block:
            kr = [sb(st, f"kr{b}", [P, P + 2]) for b in range(U)]
            stage = [sb(st, f"stage{b}", [P, 4], i32) for b in range(U)]
            xe = [sb(st, f"xe{b}", [P, 2, D]) for b in range(U)]
            xdb = [sb(st, f"xdb{b}", [P, D]) for b in range(U)]
            bse = sb(st, "bse", [P, 4, 6])
            mve = [sb(st, f"mve{b}", [P, 4, 2]) for b in range(2)]
            vv = [sb(st, f"vv{b}", [P, 5]) for b in range(2)]
            rr = [sb(st, f"rr{b}", [P, 5]) for b in range(2)]
            nbe = [sb(st, f"nbe{b}", [P, 4]) for b in range(2)]
            he = [sb(st, f"he{b}", [P, 2, D]) for b in range(2)]
            het = [sb(st, f"het{b}", [P, 2 * K, P]) for b in range(2)]
            hs = [sb(st, f"hs{b}", [P, D + 2 * H]) for b in range(U)]
            hd = [sb(st, f"hd{b}", [P, 2 * D]) for b in range(U)]
            edge = [sb(st, f"edge{b}", [P, 2, H]) for b in range(2)]
            same = [sb(st, f"same{b}", [P, P]) for b in range(U)]
            cont = [sb(st, f"cont{b}", [P, P]) for b in range(U)]
            lkt = [sb(st, f"lkt{b}", [P, 2 * H]) for b in range(2)]
            lk = [sb(st, f"lk{b}", [H, 2 * P]) for b in range(2)]
            mx = sb(st, "mx", [H, P])
            fw = sb(st, "fw", [H, P])
            mm = [sb(st, f"mm{b}", [H, P]) for b in range(2)]
            dm = sb(st, "dm", [H, 2 * P + 1])
            ex = [sb(st, f"ex{b}", [H, 2 * P + 1]) for b in range(2)]
            xw = [sb(st, f"xw{b}", [P, 3 * H]) for b in range(2)]
            msg = [sb(st, f"msg{b}", [P, NH + 1]) for b in range(2)]
            car = sb(st, "car", [P, NH])
            acc = [sb(st, f"acc{b}", [P, NH + 1]) for b in range(2)]
            own = [sb(st, f"own{b}", [P, D]) for b in range(2)]
            own2 = sb(st, "own2", [P, D])
            den = sb(st, "den", [P, H])
            rden = sb(st, "rden", [P, H])
            nrm = sb(st, "nrm", [P, D])
            ye = [sb(st, f"ye{b}", [P, D]) for b in range(U)]
            yg = sb(st, "yg", [P, D])
            x1e = [sb(st, f"x1e{b}", [P, D]) for b in range(U)]
            n1e = [sb(st, f"n1e{b}", [P, D + 2]) for b in range(U)]
            pidx = [sb(st, f"pidx{b}", [P, 4], i32) for b in range(U)]
            hold = sb(st, "hold", [P, U])
            ps_t = pb(st, "ps_te")
            ps_hs = pb(st, "ps_hs")
            ps_hd = [pb(st, f"ps_hd{b}") for b in range(2)]
            ps_l = pb(st, "ps_le")
            ps_x = pb(st, "ps_xe")
            ps_a = pb(st, "ps_ae")
            ps_e = pb(st, "ps_ee")

            kr_loaded = [sem(f"kr_loaded{b}") for b in range(U)]
            src_gathered = [sem(f"src_gathered{b}") for b in range(U)]
            dst_gathered = [sem(f"dst_gathered{b}") for b in range(U)]
            row_sent = [sem(f"row_sent{b}") for b in range(U)]
            x1_sent = [sem(f"x1_sent{b}") for b in range(U)]
            n1_sent = [sem(f"n1_sent{b}") for b in range(U)]
            (e_staged, e_xdb, e_stats, e_moments, e_var, e_nb, e_h, e_trans, e_het, e_hs, e_hd, e_hs_sb, e_hd_sb,
             e_same, e_cont, e_edge, e_edge_t, e_leaky, e_logits, e_lk, e_pair, e_fwd, e_max, e_diff, e_exp, e_exp_t, e_xw, e_msg,
             e_sums, e_car, e_acc, e_deg, e_own, e_own2, e_den, e_rden, e_nrm, e_y, y_stats,
             e_yg, e_x1, x1_stats, e_n1, e_pidx, e_dis_own, rr_ready, init_done) = [
                sem("e_" + n) for n in (
                    "staged xdb stats moments var nb h trans het hs hd hs_sb hd_sb same cont edge edget leaky logits lk pair "
                    "fwd max diff exp exp_t xw msg sums car acc deg own own2 den rden nrm y ystats "
                    "yg x1 x1stats n1 pidx disown rr init").split()]
            LAGE = 9

            def until(eng, semaphore, c, per=1):
                if isinstance(c, int):
                    c = min(c, C - 1)
                after(eng, semaphore, (c + 1) * per)

            def edge_cols(c):
                flat = edges[:].rearrange("p c n -> p (c n)")
                flat = flat[:, 2 * c:2 * c + 2] if isinstance(c, int) else flat[:, bass.ds(2 * c, 2)]
                return flat.unsqueeze(2).broadcast_to([P, 2, H])

            def normed(i):
                return not isinstance(i, int) or 1 <= i < C + 6

            @block.sync
            def _(sp):
                def step(i, b):
                    if runs(i, 0, C):
                        until(sp, e_same, i - U)
                        until(sp, e_cont, i - U)
                        at = keys[i * P:i * P + P + 2] if isinstance(i, int) else keys[bass.ds(i * P, P + 2)]
                        sp.dma_start(kr[b][:], at.partition_broadcast(P)).then_inc(kr_loaded[b], 16)
                    if runs(i, 6, C):
                        c, o = i - 6, (b - 6) % U
                        sp.wait_ge(e_x1, c + 1)
                        sp.dma_start(slot_rows(x1_slots, c, 0), x1e[o][:]).then_inc(x1_sent[o], 16)
                    if runs(i, 8, C):
                        c, o = i - 8, (b - 8) % U
                        sp.wait_ge(e_n1, c + 1)
                        sp.dma_start(slot_rows(n1_slots, c, 0), n1e[o][:]).then_inc(n1_sent[o], 16)

                stages(sp, C, LAGE, step, first=3)
                for b in range(U):
                    sp.wait_ge(x1_sent[b], 16 * (C // U))
                    sp.wait_ge(n1_sent[b], 16 * (C // U))

            @block.gpsimd
            def _(pool):
                for b in range(2):
                    nc.gpsimd.memset(vv[b][:], 1.0).then_inc(init_done, 1)

                def step(i, b):
                    if runs(i, 2, C):
                        c, o = i - 2, (b - 2) % U
                        until(pool, e_x1, c - U)
                        pool.wait_ge(dst_gathered[o], 16 * (b_count(i, b, 2) + 1))
                        nc.gpsimd.tensor_tensor(xdb[o][:], xe[o][:, 1, :], beta_b[:], ALU.add).then_inc(e_xdb, 1)
                    if runs(i, 0, C):
                        until(pool, e_h, i - U)
                        until(pool, e_xdb, i - U)
                        pool.wait_ge(e_staged, i + 1)
                        passed(pool)
                        pool.indirect_dma_start(xe[b][:, 0, :], None, x, bass.IndirectOffsetOnAxis(stage[b][:, 0:1], 0)
                                                ).then_inc(src_gathered[b], 16)
                        pool.indirect_dma_start(xe[b][:, 1, :], None, x, bass.IndirectOffsetOnAxis(stage[b][:, 1:2], 0)
                                                ).then_inc(dst_gathered[b], 16)
                    if runs(i, 4, C):
                        c, q = i - 4, (b - 4) % 2
                        pool.wait_ge(e_acc, c + 1)
                        pool.wait_ge(e_own, c + 1)
                        until(pool, e_nrm, c - 1)
                        nc.gpsimd.tensor_tensor(own2[:].rearrange("p (h c) -> p h c", h=H),
                                                own[q][:].rearrange("p (h c) -> p h c", h=H),
                                                acc[q][:, 0:NH].rearrange("p (h c) -> p h c", h=H)[:, :, 0:HC],
                                                ALU.add).then_inc(e_own2, 1)
                    if isinstance(i, int) and i == 0:
                        pool.wait_ge(init_done, 7)
                    if not isinstance(i, int) or i < C + 6:
                        for s, lag in ((e_var, 1), (e_deg, 5)):
                            if normed(i) if s is e_var else runs(i, lag, C):
                                pool.wait_ge(s, i - lag + 1)
                        for s, lag in ((e_h, 3), (e_x1, 7), (e_n1, 8), (e_dis_own, 7)):
                            until(pool, s, i - lag)
                        after(pool, rr_ready, i - 1)
                        nc.gpsimd.tensor_tensor(rr[b % 2][:], vv[b % 2][:], neg_half[:, 0:5], ALU.pow).then_inc(rr_ready, 1)
                    if runs(i, 3, C):
                        c, o = i - 3, (b - 3) % U
                        pool.wait_ge(e_xw, c + 1)
                        pool.wait_ge(e_hd_sb, c + 1)
                        until(pool, e_own2, c - 2)
                        nc.gpsimd.tensor_tensor(own[o % 2][:].rearrange("p (h c) -> p h c", h=H),
                                                hd[o][:, 0:D].rearrange("p (h c) -> p h c", h=H),
                                                xw[o % 2][:, H:2 * H].unsqueeze(2).broadcast_to([P, H, HC]),
                                                ALU.mult).then_inc(e_own, 1)
                    if runs(i, 8, C):
                        c, o = i - 8, (b - 8) % U
                        pool.wait_ge(e_pidx, c + 1)
                        pool.wait_ge(e_n1, c + 1)
                        passed(pool)
                        pool.indirect_dma_start(rows[0:N, :], bass.IndirectOffsetOnAxis(pidx[o][:, 2:3], 0), n1e[o][:], None,
                                                bounds_check=N - 1, oob_is_err=False).then_inc(row_sent[o], 16)

                stages(pool, C, LAGE, step, first=3)
                for b in range(U):
                    pool.wait_ge(row_sent[b], 16 * (C // U))

            @block.vector
            def _(dve):
                def by_head(ap):
                    return ap.rearrange("p (h c) -> p h c", h=H)

                def heads(ap, n):
                    return ap.unsqueeze(2).broadcast_to([P, H, n])

                nc.vector.memset(acc[1][:], 0.0).then_inc(init_done, 1)
                for b in range(2):
                    nc.vector.memset(msg[b][:, NH:NH + 1], 1.0).then_inc(init_done, 1)
                    nc.vector.memset(mve[b][:], 1.0).then_inc(init_done, 1)
                dve.wait_ge(init_done, 7)

                def step(i, b):
                    if runs(i, 3, C):
                        c, q, o = i - 3, (b - 3) % 2, (b - 3) % U
                        dve.wait_ge(e_lk, c + 1)
                        nc.vector.tensor_tensor(mx[:], lk[q][:, 0:P], lk[q][:, P:2 * P], ALU.max).then_inc(e_pair, 1)
                    if runs(i, 1, C):
                        c, o = i - 1, (b - 1) % U
                        dve.wait_ge(src_gathered[o], 16 * (b_count(i, b, 1) + 1))
                        nc.vector.bn_stats(bse[:, 0, :], xe[o][:, 0, :]).then_inc(e_stats, 1)
                        dve.wait_ge(dst_gathered[o], 16 * (b_count(i, b, 1) + 1))
                        nc.vector.bn_stats(bse[:, 1, :], xe[o][:, 1, :]).then_inc(e_stats, 1)
                    if runs(i, 3, C):
                        c, q, o = i - 3, (b - 3) % 2, (b - 3) % U
                        dve.wait_ge(e_pair, c + 1)
                        dve.wait_ge(e_edge_t, c + 1)
                        before = low[:] if isinstance(c, int) and c == 0 else mm[1 - q][:, P - 1:P]
                        nc.vector.tensor_tensor_scan(fw[:], ps_e[0:H, 0:P], mx[:], before, ALU.add, ALU.max
                                                     ).then_inc(e_fwd, 1)
                    if runs(i, 5, C):
                        c, o = i - 5, (b - 5) % U
                        dve.wait_ge(e_y, c + 1)
                        nc.vector.bn_stats(bse[:, 2, :], ye[o][:]).then_inc(y_stats, 1)
                    if runs(i, 3, C):
                        c, q, o = i - 3, (b - 3) % 2, (b - 3) % U
                        dve.wait_ge(e_fwd, c + 1)
                        nc.vector.tensor_tensor_scan(mm[q][:, ::-1], ps_e[0:H, P:2 * P][:, ::-1], fw[:, ::-1], low[:],
                                                     ALU.add, ALU.max).then_inc(e_max, 1)
                    if runs(i, 6, C):
                        c, o = i - 6, (b - 6) % U
                        dve.wait_ge(e_x1, c + 1)
                        nc.vector.bn_stats(bse[:, 3, :], x1e[o][:]).then_inc(x1_stats, 1)
                    if runs(i, 3, C):
                        c, q, o = i - 3, (b - 3) % 2, (b - 3) % U
                        dve.wait_ge(e_max, c + 1)
                        until(dve, e_exp, c - 1)
                        nc.vector.tensor_tensor(dm[:, 0:2 * P].rearrange("h (n p) -> h n p", n=2), mm[q][:].unsqueeze(1).broadcast_to([H, 2, P]),
                                                lk[q][:].rearrange("h (n p) -> h n p", n=2), ALU.subtract
                                                ).then_inc(e_diff, 1)
                        nc.vector.tensor_scalar(dm[:, 2 * P:], mm[q][:, 0:1], before, 0.0, ALU.subtract, ALU.max
                                                ).then_inc(e_diff, 1)
                    for s, lag, per in ((e_stats, 1, 2), (y_stats, 5, 1), (x1_stats, 6, 1)):
                        if runs(i, lag, C):
                            dve.wait_ge(s, (i - lag + 1) * per)
                    nc.vector.memset(hold[:, b:b + 1], 0.0)
                    for n, lag in ((0, 1), (1, 1), (2, 5), (3, 6)):
                        if runs(i, lag, C):
                            last = nc.vector.bn_aggr(mve[b % 2][:, n, :], bse[:, n, :])
                    if normed(i):
                        last.then_inc(e_moments, 1)
                    if runs(i, 4, C):
                        c, q = i - 4, (b - 4) % 2
                        a = by_head(acc[q][:, 0:NH])
                        dve.wait_ge(e_acc, c + 1)
                        nc.vector.scalar_tensor_tensor(den[:], a[:, :, HC], TINY, xw[q][:, H:2 * H], ALU.add, ALU.add
                                                       ).then_inc(e_den, 1)
                    if not isinstance(i, int) or 2 <= i < C + 6:
                        dve.wait_ge(rr_ready, i - 1)
                    if normed(i):
                        dve.wait_ge(e_moments, i)
                        nc.vector.tensor_scalar(vv[b % 2][:, 0:4], mve[b % 2][:, :, 1], EPS, None, ALU.add
                                                ).then_inc(e_var, 1)
                    if runs(i, 5, C):
                        q = (b - 5) % 2
                        nc.vector.tensor_scalar(vv[b % 2][:, 4:5], acc[q][:, NH:NH + 1], 1.0, 1.0, ALU.add, ALU.max
                                                ).then_inc(e_deg, 1)
                    if runs(i, 4, C):
                        c, q = i - 4, (b - 4) % 2
                        dve.wait_ge(e_den, c + 1)
                        nc.vector.reciprocal(rden[:], den[:]).then_inc(e_rden, 1)
                    if runs(i, 1, C):
                        c, o = i - 1, (b - 1) % U
                        dve.wait_ge(kr_loaded[o], 16 * (b_count(i, b, 1) + 1))
                        until(dve, e_sums, c - U)
                        nc.vector.scalar_tensor_tensor(same[o][:], kr[o][:, 1:P + 1], col(key_col, c), tri[:],
                                                       ALU.is_equal, ALU.mult).then_inc(e_same, 1)
                    if runs(i, 5, C):
                        c, o = i - 5, (b - 5) % U
                        until(dve, e_x1, c - 1)
                        nc.vector.scalar_tensor_tensor(yg[:], ye[o][:], mve[b % 2][:, 2, 0:1], gamma_b[:], ALU.subtract,
                                                       ALU.mult).then_inc(e_yg, 1)
                    r = rr[b % 2]
                    if runs(i, 3, C):
                        c, q = i - 3, (b - 3) % 2
                        dve.wait_ge(e_exp_t, c + 1)
                        until(dve, e_den, c - 2)
                        until(dve, e_own, c - 2)
                        nc.vector.tensor_copy(xw[q][:], ps_x[:, 0:3 * H]).then_inc(e_xw, 1)
                    if runs(i, 2, C):
                        c, q, o = i - 2, (b - 2) % 2, (b - 2) % U
                        dve.wait_ge(e_hs_sb, c + 1)
                        until(dve, e_logits, c - 2)
                        nc.vector.scalar_tensor_tensor(lkt[q][:], hs[o][:, D:D + 2 * H], SLOPE, hs[o][:, D:D + 2 * H],
                                                       ALU.mult, ALU.max).then_inc(e_leaky, 1)
                    if runs(i, 3, C):
                        c, q = i - 3, (b - 3) % 2
                        dve.wait_ge(e_xw, c + 1)
                        until(dve, e_acc, c - 1)
                        nc.vector.tensor_tensor(by_head(car[:]), by_head(acc[1 - q][:, 0:NH]),
                                                heads(xw[q][:, 2 * H:3 * H], HC + 1), ALU.mult).then_inc(e_car, 1)
                    if runs(i, 3, C):
                        c, q, o = i - 3, (b - 3) % 2, (b - 3) % U
                        dve.wait_ge(e_xw, c + 1)
                        m = by_head(msg[q][:, 0:NH])
                        nc.vector.tensor_copy(m[:, :, HC], xw[q][:, 0:H]).then_inc(e_msg, 1)
                        nc.vector.tensor_tensor(m[:, :, 0:HC], by_head(hs[o][:, 0:D]), heads(xw[q][:, 0:H], HC), ALU.mult
                                                ).then_inc(e_msg, 1)
                    if normed(i):
                        dve.wait_ge(rr_ready, i + 1)
                        until(dve, e_h, i - 3)
                        until(dve, e_n1, i - 8)
                        nc.vector.scalar_tensor_tensor(nbe[b % 2][:], mve[b % 2][:, :, 0], -1.0, r[:, 0:4], ALU.mult, ALU.mult
                                                       ).then_inc(e_nb, 1)
                    if runs(i, 4, C):
                        c, q = i - 4, (b - 4) % 2
                        dve.wait_ge(e_rden, c + 1)
                        dve.wait_ge(e_own2, c + 1)
                        nc.vector.tensor_tensor(by_head(nrm[:]), by_head(own2[:]), heads(rden[:], HC), ALU.mult
                                                ).then_inc(e_nrm, 1)
                    if runs(i, 5, C):
                        c, o = i - 5, (b - 5) % U
                        dve.wait_ge(e_yg, c + 1)
                        dve.wait_ge(e_xdb, c + 1)
                        until(dve, e_n1, c - U)
                        if not isinstance(c, int) or c >= U:
                            dve.wait_ge(x1_sent[o], 16 * b_count(i, b, 5))
                        nc.vector.scalar_tensor_tensor(x1e[o][:], yg[:], r[:, 2:3], xdb[o][:], ALU.mult, ALU.add
                                                       ).then_inc(e_x1, 1)
                    if runs(i, 4, C):
                        c, o = i - 4, (b - 4) % U
                        dve.wait_ge(e_nrm, c + 1)
                        nc.vector.tensor_tensor(ye[o][:], nrm[:], hd[o][:, D:2 * D], ALU.add).then_inc(e_y, 1)

                stages(dve, C, LAGE, step, first=3)

            @block.scalar
            def _(act):
                def step(i, b):
                    r = rr[(b - 1) % 2]
                    if runs(i, 0, C):
                        until(act, e_stats, i - U, 2)
                        passed(act)
                        nc.scalar.activation(stage[b][:], cols(index, i), ACT.Copy).then_inc(e_staged, 1)
                    if runs(i, 2, C):
                        c, q = i - 2, (b - 2) % 2
                        act.wait_ge(e_trans, c + 1)
                        until(act, e_hd, c - 2)
                        nc.scalar.activation(het[q][:].rearrange("p k n -> p (k n)"), ps_t[:], ACT.Copy).then_inc(e_het, 1)
                    if runs(i, 3, C):
                        c, o = i - 3, (b - 3) % U
                        act.wait_ge(e_hd, c + 1)
                        until(act, e_y, c - U)
                        nc.scalar.activation(hd[o][:], ps_hd[o % 2][:], ACT.Copy).then_inc(e_hd_sb, 1)
                    if runs(i, 4, C):
                        c, q = i - 4, (b - 4) % 2
                        act.wait_ge(e_sums, c + 1)
                        until(act, e_den, c - 2)
                        until(act, e_own2, c - 2)
                        until(act, e_deg, c - 2)
                        until(act, e_car, c - 1)
                        nc.scalar.activation(acc[q][:], ps_a[:, 0:NH + 1], ACT.Copy).then_inc(e_acc, 1)
                    if runs(i, 3, C):
                        c, q = i - 3, (b - 3) % 2
                        act.wait_ge(e_diff, 2 * (c + 1))
                        until(act, e_exp_t, c - 2)
                        nc.scalar.activation(ex[q][:], dm[:], ACT.Exp, scale=-1.0).then_inc(e_exp, 1)
                    if runs(i, 2, C):
                        c, o = i - 2, (b - 2) % U
                        act.wait_ge(e_hs, c + 1)
                        until(act, e_msg, c - U, 2)
                        nc.scalar.activation(hs[o][:], ps_hs[:, 0:D + 2 * H], ACT.Copy).then_inc(e_hs_sb, 1)
                    if runs(i, 6, C):
                        c = i - 6
                        act.wait_ge(rr_ready, i)
                        passed(act)
                        nc.scalar.activation(tag_col(c, 0), r[:, 4:5], ACT.Copy).then_inc(e_dis_own, 1)
                    if runs(i, 1, C):
                        c, q = i - 1, (b - 1) % 2
                        until(act, e_edge_t, c - 2)
                        passed(act)
                        nc.scalar.activation(edge[q][:], edge_cols(c), ACT.Copy).then_inc(e_edge, 1)
                    if runs(i, 2, C):
                        c, o = i - 2, (b - 2) % U
                        act.wait_ge(kr_loaded[o], 16 * (b_count(i, b, 2) + 1))
                        until(act, e_sums, c - U)
                        passed(act)
                        nc.scalar.activation(cont[o][:], kr[o][:, 1:P + 1], ACT.Relu, bias=col(cont_bias, c),
                                             scale=neg_last[:]).then_inc(e_cont, 1)
                    if runs(i, 7, C):
                        c, o = i - 7, (b - 7) % U
                        act.wait_ge(e_nb, i - 1)
                        if not isinstance(c, int) or c >= U:
                            act.wait_ge(n1_sent[o], 16 * b_count(i, b, 7))
                            act.wait_ge(row_sent[o], 16 * b_count(i, b, 7))
                        nc.scalar.activation(n1e[o][:, 0:D], x1e[o][:], ACT.Relu, bias=nbe[(b - 1) % 2][:, 3:4],
                                             scale=r[:, 3:4])
                        act.wait_ge(e_dis_own, c + 1)
                        passed(act)
                        nc.scalar.activation(n1e[o][:, D:D + 2], tag_col(c, None), ACT.Copy).then_inc(e_n1, 1)
                        nc.scalar.activation(pidx[o][:], cols(index, c), ACT.Copy).then_inc(e_pidx, 1)
                    if runs(i, 2, C):
                        c, q = i - 2, (b - 2) % 2
                        act.wait_ge(e_logits, c + 1)
                        until(act, e_diff, c - 2, 2)
                        nc.scalar.activation(lk[q][:], ps_l[0:H, 0:2 * P], ACT.Copy).then_inc(e_lk, 1)
                    if runs(i, 1, C):
                        c, q, o = i - 1, (b - 1) % 2, (b - 1) % U
                        act.wait_ge(e_nb, i)
                        until(act, e_trans, c - 2)
                        for n in range(2):
                            last = nc.scalar.activation(he[q][:, n, :], xe[o][:, n, :], ACT.Relu, bias=nbe[b % 2][:, n:n + 1],
                                                        scale=rr[b % 2][:, n:n + 1])
                        last.then_inc(e_h, 1)

                stages(act, C, LAGE, step, first=3)

            @block.tensor
            def _(pe):
                pe.wait_ge(init_done, 7)

                def step(i, b):
                    if runs(i, 2, C):
                        c, q = i - 2, (b - 2) % 2
                        pe.wait_ge(e_h, c + 1)
                        until(pe, e_het, c - 1)
                        for n in range(2):
                            for k in range(K):
                                last = nc.tensor.transpose(ps_t[:, (n * K + k) * P:(n * K + k + 1) * P],
                                                           he[q][:, n, k * P:(k + 1) * P], ident[:])
                        last.then_inc(e_trans, 1)
                    if runs(i, 4, C):
                        c, q, o = i - 4, (b - 4) % 2, (b - 4) % U
                        pe.wait_ge(e_cont, c + 1)
                        pe.wait_ge(e_msg, 2 * (c + 1))
                        until(pe, e_acc, c - 1)
                        nc.tensor.matmul(ps_a[:, 0:NH + 1], same[o][:], msg[q][:], start=True, stop=False)
                        nc.tensor.matmul(ps_a[:, NH:NH + 1], cont[o][:], acc[1 - q][:, NH:NH + 1], start=False, stop=False)
                        pe.wait_ge(e_car, c + 1)
                        nc.tensor.matmul(ps_a[:, 0:NH], cont[o][:], car[:], start=False, stop=True).then_inc(e_sums, 1)
                    if runs(i, 2, C):
                        c, q = i - 2, (b - 2) % 2
                        pe.wait_ge(e_het, c + 1)
                        until(pe, e_hs_sb, c - 1)
                        for k in range(K):
                            nc.tensor.matmul(ps_hs[:, 0:D + 2 * H], het[q][:, k, :], w_src[:, k, :], start=k == 0, stop=False)
                        for k in range(K):
                            last = nc.tensor.matmul(ps_hs[:, D:D + 2 * H], het[q][:, K + k, :], w_att[:, k, :, :],
                                                    start=False, stop=k == K - 1)
                        last.then_inc(e_hs, 1)
                    if runs(i, 3, C):
                        c, q = i - 3, (b - 3) % 2
                        pe.wait_ge(e_exp, c + 1)
                        until(pe, e_xw, c - 1)
                        for n in range(2):
                            nc.tensor.matmul(ps_x[:, n * H:(n + 1) * H], ex[q][:, n * P:(n + 1) * P], ident[0:H, 0:H],
                                             start=True, stop=True)
                        last = nc.tensor.matmul(ps_x[:, 2 * H:3 * H], ex[q][:, 2 * P:].broadcast_to([H, P]),
                                                ident[0:H, 0:H], start=True, stop=True)
                        last.then_inc(e_exp_t, 1)
                    if runs(i, 2, C):
                        c, q = i - 2, (b - 2) % 2
                        pe.wait_ge(e_edge, c + 1)
                        until(pe, e_max, c - 1)
                        for n in range(2):
                            last = nc.tensor.matmul(ps_e[0:H, n * P:(n + 1) * P], edge[q][:, n, :], ident[:],
                                                    start=True, stop=True)
                        last.then_inc(e_edge_t, 1)
                        pe.wait_ge(e_leaky, c + 1)
                        until(pe, e_lk, c - 1)
                        for n in range(2):
                            last = nc.tensor.matmul(ps_l[0:H, n * P:(n + 1) * P], lkt[q][:, n * H:(n + 1) * H], ident[:],
                                                    start=True, stop=True)
                        last.then_inc(e_logits, 1)
                    if runs(i, 2, C):
                        c, q = i - 2, (b - 2) % 2
                        until(pe, e_hd_sb, c - 2)
                        for k in range(K):
                            nc.tensor.matmul(ps_hd[q][:], het[q][:, K + k, :], w_all[:, k, :], start=k == 0, stop=False)
                        nc.tensor.matmul(ps_hd[q][:, D:2 * D], ones3[:], bias_y[:], start=False, stop=True
                                         ).then_inc(e_hd, 1)

                stages(pe, C, LAGE, step, first=3)


        end_phase()

        for hop in (1, 2):
            if hop == 2:
                end_phase()
            with ExitStack() as st, nc.Block() as block:
                kr2 = [sb(st, f"hkr{hop}{b}", [P, 2 * P + 2]) for b in range(U // 2)]
                own_row2 = [sb(st, f"own_row{hop}{b}", [P, 2, D + 2]) for b in range(U // 2)]
                sidx = [sb(st, f"hidx{hop}{b}", [P, 4], i32) for b in range(U)]
                far_row = [sb(st, f"far_row{hop}{b}", [P, D + 2]) for b in range(U)]
                same = [sb(st, f"hsame{hop}{b}", [P, P]) for b in range(2)]
                cont = [sb(st, f"hcont{hop}{b}", [P, P]) for b in range(2)]
                msg = [sb(st, f"hmsg{hop}{b}", [P, D + 1]) for b in range(2)]
                own = [sb(st, f"hown{hop}{b}", [P, D]) for b in range(U)]
                acc = [sb(st, f"hacc{hop}{b}", [P, D + 1]) for b in range(2)]
                uu = [sb(st, f"uu{hop}{b}", [P, D + 2]) for b in range(U)]
                ps_a = [pb(st, f"hps_a{hop}{b}") for b in range(2)]
                kr_loaded = [sem(f"h{hop}_kr_loaded{b}") for b in range(U // 2)]
                own_loaded = [sem(f"h{hop}_own_loaded{b}") for b in range(U // 2)]
                far_gathered = [sem(f"h{hop}_far_gathered{b}") for b in range(U)]
                sent = [sem(f"h{hop}_sent{b}") for b in range(U)]
                (h_staged, h_same, h_cont, h_row, h_dis, h_own, h_sums, h_acc, h_u, h_tag, h_behind, h_init) = [
                    sem(f"h{hop}_{n}") for n in "staged same cont row dis own sums acc u tag behind init".split()]
                if hop == 2:
                    x1o = [sb(st, f"x1o{b}", [P, D]) for b in range(U)]
                    ut = [sb(st, f"ut{b}", [P, K, P]) for b in range(2)]
                    a1 = [sb(st, f"a1{b}", [P, 1]) for b in range(U)]
                    z = [sb(st, f"z{b}", [P, D]) for b in range(2)]
                    zn = [sb(st, f"zn{b}", [P, D]) for b in range(2)]
                    zx = [sb(st, f"hzx{b}", [P, D]) for b in range(2)]
                    oidx = [sb(st, f"oidx{b}", [P, 4], i32) for b in range(U)]
                    oe = [sb(st, f"oe{b}", [P, D]) for b in range(U)]
                    ps_t = pb(st, "hps_t")
                    ps_z = pb(st, "hps_z")
                    x1_loaded = [sem(f"h2_x1_loaded{b}") for b in range(U)]
                    (h_a1, h_trans, h_ut, h_prod, h_z, h_zn, h_zx, h_o, h_oidx) = [
                        sem(f"h2_{n}") for n in "a1 trans ut prod z zn zx o oidx".split()]
                LAGH = 9
                kr = [kr2[b // 2][:, b % 2 * P:(b % 2 + 1) * P + 2] for b in range(U)]
                own_row = [own_row2[b // 2][:, b % 2, :] for b in range(U)]
                L = 1 if hop == 1 else 0

                @block.sync
                def _(sp):
                    def step(i, b):
                        if b % 2 == 0 and runs(i, 0, C):
                            after(sp, h_same, i - U + 2)
                            after(sp, h_cont, i - U + 2)
                            at = keys[i * P:i * P + 2 * P + 2] if isinstance(i, int) else keys[bass.ds(i * P, 2 * P + 2)]
                            sp.dma_start(kr2[b // 2][:], at.partition_broadcast(P)).then_inc(kr_loaded[b // 2], 16)
                            after(sp, h_own, i - U + 2)
                            table, at = (n1_slots, i * P) if hop == 1 else (rows, i * P + N)
                            of = table[at:at + 2 * P, :] if isinstance(i, int) else table[bass.ds(at, 2 * P), :]
                            sp.dma_start(own_row2[b // 2][:], of.rearrange("(n p) d -> p n d", n=2)
                                         ).then_inc(own_loaded[b // 2], 16)
                        if hop == 1 and runs(i, L + 5, C):
                            c, o = i - L - 5, (b - L - 5) % U
                            sp.wait_ge(h_u, c + 1)
                            sp.wait_ge(h_tag, c + 1)
                            sp.dma_start(slot_rows(rows, c, N), uu[o][:]).then_inc(sent[o], 16)
                        if hop == 2 and runs(i, 4, C):
                            c, o = i - 4, (b - 4) % U
                            after(sp, h_zx, c - U + 1)
                            sp.dma_start(x1o[o][:], slot_rows(x1_slots, c, 0)).then_inc(x1_loaded[o], 16)

                    stages(sp, C, LAGH, step, first=3)
                    for b in range(U):
                        sp.wait_ge(sent[b], 16 * (C // U))

                @block.gpsimd
                def _(pool):
                    def step(i, b):
                        if hop == 2 and runs(i, 9, C):
                            c, o = i - 9, (b - 9) % U
                            pool.wait_ge(h_o, c + 1)
                            pool.wait_ge(h_oidx, c + 1)
                            passed(pool)
                            pool.indirect_dma_start(out, bass.IndirectOffsetOnAxis(oidx[o][:, 2:3], 0), oe[o][:], None,
                                                    bounds_check=N - 1, oob_is_err=False).then_inc(sent[o], 16)
                        if runs(i, L, C):
                            c, o = i - L, (b - L) % U
                            after(pool, h_row, c - U + 1)
                            after(pool, h_dis, c - U + 1)
                            if hop == 1:
                                after(pool, h_behind, c - U + 1)
                            pool.wait_ge(h_staged, c + 1)
                            passed(pool)
                            pool.indirect_dma_start(far_row[o][:], None, rows[0:N, :] if hop == 1 else rows,
                                                    bass.IndirectOffsetOnAxis(sidx[o][:, hop - 1:hop], 0)
                                                    ).then_inc(far_gathered[o], 16)

                    stages(pool, C, LAGH, step, first=3)

                @block.vector
                def _(dve):
                    nc.vector.memset(acc[1][:], 0.0).then_inc(h_init, 1)
                    if hop == 1:
                        nc.vector.tensor_tensor(dis2_own[:], tag[:, :, 0], tag[:, :, 0], ALU.mult).then_inc(h_init, 1)

                    def step(i, b):
                        if hop == 1 and runs(i, 0, C):
                            after(dve, h_row, i - U + 1)
                            nc.vector.tensor_copy(sidx[b][:], cols(index, i)).then_inc(h_staged, 1)
                        if hop == 2 and runs(i, 7, C):
                            c, q, o = i - 7, (b - 7) % 2, (b - 7) % U
                            dve.wait_ge(h_prod, c + 1)
                            dve.wait_ge(h_a1, c + 1)
                            after(dve, h_zx, c - 1)
                            after(dve, h_zn, c - 1)
                            nc.vector.scalar_tensor_tensor(z[q][:], b1w2_b[:], a1[o][:], ps_z[:, 0:D], ALU.mult,
                                                           ALU.add).then_inc(h_z, 1)
                        if runs(i, L + 2, C):
                            c, q, o = i - L - 2, (b - L - 2) % 2, (b - L - 2) % U
                            dve.wait_ge(kr_loaded[o // 2], 16 * (b_count(i, b, L + 2) + 1))
                            after(dve, h_sums, c - 1)
                            nc.vector.scalar_tensor_tensor(same[q][:], kr[o][:, 1:P + 1], col(key_col, c), tri[:],
                                                           ALU.is_equal, ALU.mult).then_inc(h_same, 1)
                        if hop == 2 and runs(i, 7, C):
                            c, q = i - 7, (b - 7) % 2
                            dve.wait_ge(h_z, c + 1)
                            after(dve, h_o, c - 1)
                            nc.vector.scalar_tensor_tensor(zn[q][:], z[q][:], 0.0, am1_b[:], ALU.min, ALU.mult
                                                           ).then_inc(h_zn, 1)
                        if hop == 1 and runs(i, L + 2, C):
                            c, q, o = i - L - 2, (b - L - 2) % 2, (b - L - 2) % U
                            nc.vector.tensor_scalar(cont[q][:], kr[o][:, 1:P + 1], kr[o][:, 0:1], last_row[:],
                                                    ALU.is_equal, ALU.mult).then_inc(h_cont, 1)
                        if runs(i, L + 4, C):
                            c, q, o = i - L - 4, (b - L - 4) % 2, (b - L - 4) % U
                            dve.wait_ge(h_acc, c + 1)
                            dve.wait_ge(h_own, c + 1)
                            if hop == 1:
                                if not isinstance(c, int) or c >= U:
                                    dve.wait_ge(sent[o], 16 * b_count(i, b, L + 4))
                            else:
                                after(dve, h_trans, c - U + 1)
                            nc.vector.scalar_tensor_tensor(uu[o][:, 0:D], acc[q][:, 0:D], tag_col(c, 0), own[o][:],
                                                           ALU.mult, ALU.add).then_inc(h_u, 1)
                        if runs(i, L + 2, C):
                            c, q, o = i - L - 2, (b - L - 2) % 2, (b - L - 2) % U
                            dve.wait_ge(far_gathered[o], 16 * (b_count(i, b, L + 2) + 1))
                            nc.vector.tensor_copy(msg[q][:, D:D + 1], far_row[o][:, D:D + 1]).then_inc(h_dis, 1)
                            if hop == 1:
                                nc.vector.tensor_copy(col(src_behind, c), far_row[o][:, D + 1:D + 2]).then_inc(h_behind, 1)
                        if hop == 2 and runs(i, 7, C):
                            c, q, o = i - 7, (b - 7) % 2, (b - 7) % U
                            dve.wait_ge(x1_loaded[o], 16 * (b_count(i, b, 7) + 1))
                            nc.vector.tensor_tensor(zx[q][:], z[q][:], x1o[o][:], ALU.add).then_inc(h_zx, 1)
                        if hop == 2 and runs(i, 8, C):
                            c, q, o = i - 8, (b - 8) % 2, (b - 8) % U
                            dve.wait_ge(h_zx, c + 1)
                            dve.wait_ge(h_zn, c + 1)
                            if not isinstance(c, int) or c >= U:
                                dve.wait_ge(sent[o], 16 * b_count(i, b, 8))
                            nc.vector.tensor_tensor(oe[o][:], zx[q][:], zn[q][:], ALU.add).then_inc(h_o, 1)

                    stages(dve, C, LAGH, step, first=3)
                    if hop == 1:
                        dve.wait_ge(h_behind, C)
                        nc.vector.tensor_tensor(index[:, :, 1], src_col[:], src_behind[:], ALU.add)

                @block.scalar
                def _(act):
                    if hop == 1:
                        act.wait_ge(h_init, 2)

                    def step(i, b):
                        if hop == 2 and runs(i, 0, C):
                            after(act, h_row, i - U + 1)
                            passed(act)
                            nc.scalar.activation(sidx[b][:], cols(index, i), ACT.Copy).then_inc(h_staged, 1)
                        if hop == 2 and runs(i, 8, C):
                            c, o = i - 8, (b - 8) % U
                            if not isinstance(c, int) or c >= U:
                                act.wait_ge(sent[o], 16 * b_count(i, b, 8))
                            passed(act)
                            nc.scalar.activation(oidx[o][:], cols(index, c), ACT.Copy).then_inc(h_oidx, 1)
                        if hop == 2 and runs(i, L + 2, C):
                            c, q, o = i - L - 2, (b - L - 2) % 2, (b - L - 2) % U
                            act.wait_ge(kr_loaded[o // 2], 16 * (b_count(i, b, L + 2) + 1))
                            after(act, h_sums, c - 1)
                            passed(act)
                            nc.scalar.activation(cont[q][:], kr[o][:, 1:P + 1], ACT.Relu, bias=col(cont_bias, c),
                                                 scale=neg_last[:]).then_inc(h_cont, 1)
                        if runs(i, L + 2, C):
                            c, q, o = i - L - 2, (b - L - 2) % 2, (b - L - 2) % U
                            act.wait_ge(far_gathered[o], 16 * (b_count(i, b, L + 2) + 1))
                            after(act, h_sums, c - 1)
                            nc.scalar.activation(msg[q][:, 0:D], far_row[o][:, 0:D], ACT.Relu,
                                                 scale=far_row[o][:, D:D + 1]).then_inc(h_row, 1)
                            act.wait_ge(own_loaded[o // 2], 16 * (b_count(i, b, L + 2) + 1))
                            after(act, h_u, c - U + 1)
                            passed(act)
                            nc.scalar.activation(own[o][:], own_row[o][:, 0:D], ACT.Relu, scale=col(dis2_own, c)
                                                 ).then_inc(h_own, 1)
                        if hop == 2 and runs(i, 4, C):
                            c, q, o = i - 4, (b - 4) % 2, (b - 4) % U
                            act.wait_ge(h_acc, c + 1)
                            after(act, h_z, c - U + 1)
                            passed(act)
                            nc.scalar.activation(a1[o][:], acc[q][:, D:D + 1], ACT.Identity, bias=col(dis2_own, c),
                                                 scale=tag_col(c, 0)).then_inc(h_a1, 1)
                        if hop == 1 and runs(i, L + 4, C):
                            c, o = i - L - 4, (b - L - 4) % U
                            if not isinstance(c, int) or c >= U:
                                act.wait_ge(sent[o], 16 * b_count(i, b, L + 4))
                                passed(act)
                            nc.scalar.activation(uu[o][:, D:D + 2], tag_col(c, None), ACT.Copy).then_inc(h_tag, 1)
                        if hop == 2 and runs(i, 5, C):
                            c, q = i - 5, (b - 5) % 2
                            act.wait_ge(h_trans, c + 1)
                            after(act, h_prod, c - 1)
                            nc.scalar.activation(ut[q][:].rearrange("p k n -> p (k n)"), ps_t[:, 0:D], ACT.Copy
                                                 ).then_inc(h_ut, 1)
                        if runs(i, L + 3, C):
                            c, q = i - L - 3, (b - L - 3) % 2
                            act.wait_ge(h_sums, c + 1)
                            after(act, h_u, c - 1)
                            if hop == 2:
                                after(act, h_a1, c - 1)
                            nc.scalar.activation(acc[q][:], ps_a[q][:, 0:D + 1], ACT.Copy).then_inc(h_acc, 1)

                    stages(act, C, LAGH, step, first=3)

                @block.tensor
                def _(pe):
                    pe.wait_ge(h_init, 1)

                    def step(i, b):
                        if runs(i, L + 3, C):
                            c, q = i - L - 3, (b - L - 3) % 2
                            pe.wait_ge(h_same, c + 1)
                            pe.wait_ge(h_row, c + 1)
                            pe.wait_ge(h_dis, c + 1)
                            after(pe, h_acc, c - 1)
                            nc.tensor.matmul(ps_a[q][:, 0:D + 1], same[q][:], msg[q][:], start=True, stop=False)
                        if hop == 2 and runs(i, 6, C):
                            c, q = i - 6, (b - 6) % 2
                            pe.wait_ge(h_ut, c + 1)
                            after(pe, h_z, c)
                            for k in range(K):
                                nc.tensor.matmul(ps_z[:, 0:D], ut[q][:, k, :], w_12[:, k, :], start=k == 0, stop=False)
                            nc.tensor.matmul(ps_z[:, 0:D], ones3[:], bias_2[:], start=False, stop=True
                                             ).then_inc(h_prod, 1)
                        if hop == 2 and runs(i, 5, C):
                            c, o = i - 5, (b - 5) % U
                            pe.wait_ge(h_u, c + 1)
                            after(pe, h_ut, c)
                            for k in range(K):
                                last = nc.tensor.transpose(ps_t[:, k * P:(k + 1) * P], uu[o][:, k * P:(k + 1) * P],
                                                           ident[:])
                            last.then_inc(h_trans, 1)
                        if runs(i, L + 3, C):
                            c, q = i - L - 3, (b - L - 3) % 2
                            pe.wait_ge(h_cont, c + 1)
                            after(pe, h_acc, c)
                            nc.tensor.matmul(ps_a[q][:, 0:D + 1], cont[q][:], acc[1 - q][:], start=False, stop=True
                                             ).then_inc(h_sums, 1)

                    stages(pe, C, LAGH, step, first=3)


_INS = ["x", "src", "dst", "L0_gnn_W", "L0_gnn_a_src", "L0_gnn_a_dst", "L0_gnn_bias_gat", "L0_gnn_W_res", "L0_gnn_b_res",
        "L0_gnn_gamma", "L0_gnn_beta", "L1_gnn_W1", "L1_gnn_b1", "L1_gnn_W2", "L1_gnn_b2", "L1_gnn_prelu_a"]


def kernel(**inputs):
    import numpy as np
    import concourse.bacc as bacc
    from concourse import mybir as _mybir
    from concourse.bass_utils import run_bass_kernel_spmd

    nc = bacc.Bacc("TRN2", target_bir_lowering=False, num_devices=1)
    arrays, args = {}, []
    for name in _INS:
        a = np.ascontiguousarray(inputs[name])
        arrays[f"in_{name}"] = a
        args.append(nc.dram_tensor(f"in_{name}", a.shape, _mybir.dt.from_np(a.dtype), kind="ExternalInput").ap())
    args.append(nc.dram_tensor("out_x", inputs["x"].shape, _mybir.dt.float32, kind="ExternalOutput").ap())
    gat_then_gcn_kernel(nc, *args)
    r = run_bass_kernel_spmd(nc, [arrays], core_ids=[0])
    return r.results[0]["out_x"]
```
